# Optimizing a Trainium2 kernel written in Bass

```python
import numpy as np
import jax
import jax.numpy as jnp

def _softmax(x, axis=-1):
    return jax.nn.softmax(x, axis=axis)

def _gelu(x):
    return jax.nn.gelu(x, approximate=True)

def _silu(x):
    return jax.nn.silu(x)

def _sigmoid(x):
    return jax.nn.sigmoid(x)

def _layernorm(x, axis=-1, eps=1e-05):
    m = jnp.mean(x, axis=axis, keepdims=True)
    v = jnp.var(x, axis=axis, keepdims=True)
    return (x - m) / jnp.sqrt(v + eps)

def _scatter_add(tgt, idx, src, axis=0):
    return tgt.at[idx].add(src)

def _segment_sum(src, seg, n):
    return jax.ops.segment_sum(src, seg, n)
kernel_name = 'mk_flamingo_gated_d2_seqx_r8_74f243'

def setup_inputs(seed: int=0):
    np.random.seed(seed)
    _w = jnp.asarray

    def _rec_inputs():
        import jax
        import jax.numpy as jnp
        _rk = jax.random.key(seed)
        x = -0.0002928 + 1 * jax.random.normal(jax.random.fold_in(_rk, 1), (32, 128, 128), jnp.float32)
        _lenS = 128 - jax.random.randint(jax.random.fold_in(_rk, 7), (32,), 0, max(1, 128 // 4) + 1, jnp.int32)
        _lenS2 = 128 - jax.random.randint(jax.random.fold_in(_rk, 8), (32,), 0, max(1, 128 // 4) + 1, jnp.int32)
        _ctx_1024P = jax.random.normal(jax.random.fold_in(_rk, 11), (32, 16, 128), jnp.float32)
        _ctx_1024c = jax.random.dirichlet(jax.random.fold_in(_rk, 511), 0.3 * jnp.ones((16,), jnp.float32), (32, 128))
        _ctx_1024t = jnp.einsum('bsk,bkd->bsd', _ctx_1024c, _ctx_1024P)
        _ctx_1024t = _ctx_1024t * jax.lax.rsqrt(jnp.mean(jnp.square(_ctx_1024t)) + 1e-12) * 0.953939
        ctx_1024 = -1.39393e-06 + 0.999914 * (_ctx_1024t + 0.3 * jax.random.normal(jax.random.fold_in(_rk, 611), (32, 128, 128), jnp.float32))
        _g = jax.random.normal(jax.random.fold_in(_rk, 9001), (2, 2), jnp.float32)
        _g = jnp.sign(_g) * jnp.maximum(jnp.abs(_g), 1.0) + (_g == 0) * 1.0
        g_xattn = _g[0]
        g_ffn = _g[1]
        return (x, ctx_1024, g_xattn, g_ffn)
    x, ctx_1024, g_xattn, g_ffn = _rec_inputs()

    def _L0_xattn_setup():
        import jax, jax.numpy as jnp
        import numpy as np
        B, T, D_MODEL, N_HEAD = (1, 512, 128, 16)
        HEAD_DIM = D_MODEL // N_HEAD
        IS_CAUSAL = True

        def _mha(querys, keys, values, Wq, bq, Wk, bk, Wv, bv, Wo, bo):
            b, t, c = querys.shape
            q = (querys @ Wq.T + bq).reshape(b, t, N_HEAD, HEAD_DIM).transpose(0, 2, 1, 3)
            k = (keys @ Wk.T + bk).reshape(b, t, N_HEAD, HEAD_DIM).transpose(0, 2, 1, 3)
            v = (values @ Wv.T + bv).reshape(b, t, N_HEAD, HEAD_DIM).transpose(0, 2, 1, 3)
            scores = jnp.einsum('bhqd,bhkd->bhqk', q, k) / jnp.sqrt(jnp.float32(HEAD_DIM))
            if IS_CAUSAL:
                causal = jnp.tril(jnp.ones((t, t), dtype=bool))
                scores = jnp.where(causal, scores, jnp.float32(-jnp.inf))
            weights = jax.nn.softmax(scores, axis=-1)
            attn = jnp.einsum('bhqk,bhkd->bhqd', weights, v)
            out = attn.transpose(0, 2, 1, 3).reshape(b, t, c)
            return out @ Wo.T + bo
        key = jax.random.key(seed)
        ks = jax.random.split(key, 11)
        s_in = 1.0 / np.sqrt(D_MODEL)
        return {'querys': jax.random.normal(ks[0], (B, T, D_MODEL), dtype=jnp.float32), 'keys': jax.random.normal(ks[1], (B, T, D_MODEL), dtype=jnp.float32), 'values': jax.random.normal(ks[2], (B, T, D_MODEL), dtype=jnp.float32), 'Wq': jax.random.normal(ks[3], (D_MODEL, D_MODEL), dtype=jnp.float32) * s_in, 'bq': jnp.zeros((D_MODEL,), dtype=jnp.float32), 'Wk': jax.random.normal(ks[4], (D_MODEL, D_MODEL), dtype=jnp.float32) * s_in, 'bk': jnp.zeros((D_MODEL,), dtype=jnp.float32), 'Wv': jax.random.normal(ks[5], (D_MODEL, D_MODEL), dtype=jnp.float32) * s_in, 'bv': jnpp_zeros() if False else jnp.zeros((D_MODEL,), dtype=jnp.float32), 'Wo': jax.random.normal(ks[6], (D_MODEL, D_MODEL), dtype=jnp.float32) * s_in, 'bo': jnp.zeros((D_MODEL,), dtype=jnp.float32)}
    _L0_xattn_all = _L0_xattn_setup()
    _L0_xattn_in = {k: v for k, v in _L0_xattn_all.items() if k in ('Wq', 'bq', 'Wk', 'bk', 'Wv', 'bv', 'Wo', 'bo')}
    del _L0_xattn_all

    def _L0_ffn_setup():
        import jax, jax.numpy as jnp
        import numpy as np
        B, S, D, DO = (4, 256, 128, 128)
        E, K = (20, 2)
        key = jax.random.key(seed)
        ks = jax.random.split(key, 6)
        sc_d = 1.0 / np.sqrt(D)
        sc_h = 1.0 / np.sqrt(D // 4)
        return {'x': jax.random.normal(ks[0], (B, S, D), jnp.float32), 'wg1': jax.random.normal(ks[1], (D, D // 4), jnp.float32) * sc_d, 'bg1': jnp.zeros((D // 4,), jnp.float32), 'wg2': jax.random.normal(ks[2], (D // 4, 2 * E), jnp.float32) * sc_h, 'bg2': jnp.zeros((2 * E,), jnp.float32), 'We': jax.random.normal(ks[3], (E, D, DO), jnp.float32) * sc_d, 'be': jnp.zeros((E, DO), jnp.float32)}
    _L0_ffn_all = _L0_ffn_setup()
    _L0_ffn_in = {k: v for k, v in _L0_ffn_all.items() if k in ('wg1', 'bg1', 'wg2', 'bg2', 'We', 'be')}
    del _L0_ffn_all

    def _L1_xattn_setup():
        import jax, jax.numpy as jnp
        import numpy as np
        D_MODEL = 128
        N_HEADS = 16
        HEAD_D = D_MODEL // N_HEADS
        B, L = (4, 256)
        EPS_CAUSAL = 1e-06

        def _feat(x):
            return jax.nn.elu(x) + 1.0

        def _causal_linear_attn(qs, ks, vs):

            def step(carry, xs):
                Si, Zi = carry
                q, k, v = xs
                Si = Si + jnp.einsum('bhd,bhk->bhdk', k, v)
                Zi = Zi + k
                num = jnp.einsum('bhd,bhkd->bhk', q, Si)
                Vi = num / (q * Zi + EPS_CAUSAL)
                return ((Si, Zi), Vi)
            Bn, Ln, H, D = qs.shape
            K = vs.shape[-1]
            Si0 = jnp.zeros((Bn, H, D, K), qs.dtype)
            Zi0 = jnp.zeros((Bn, H, D), qs.dtype)
            xs = (jnp.swapaxes(qs, 0, 1), jnp.swapaxes(ks, 0, 1), jnp.swapaxes(vs, 0, 1))
            _, out = jax.lax.scan(step, (Si0, Zi0), xs)
            return jnp.swapaxes(out, 0, 1)
        key = jax.random.key(seed)
        ks = jax.random.split(key, 11)
        s = 1.0 / np.sqrt(D_MODEL)
        inp = {'queries': jax.random.normal(ks[0], (B, L, D_MODEL), jnp.float32), 'keys': jax.random.normal(ks[1], (B, L, D_MODEL), jnp.float32), 'values': jax.random.normal(ks[2], (B, L, D_MODEL), jnp.float32), 'Wq': jax.random.uniform(ks[3], (D_MODEL, N_HEADS * HEAD_D), jnp.float32, -s, s), 'bq': jax.random.uniform(ks[4], (N_HEADS * HEAD_D,), jnp.float32, -s, s), 'Wk': jax.random.uniform(ks[5], (D_MODEL, N_HEADS * HEAD_D), jnp.float32, -s, s), 'bk': jax.random.uniform(ks[6], (N_HEADS * HEAD_D,), jnp.float32, -s, s), 'Wv': jax.random.uniform(ks[7], (D_MODEL, N_HEADS * HEAD_D), jnp.float32, -s, s), 'bv': jax.random.uniform(ks[8], (N_HEADS * HEAD_D,), jnp.float32, -s, s), 'Wo': jax.random.uniform(ks[9], (D_MODEL, D_MODEL), jnp.float32, -s, s), 'bo': jax.random.uniform(ks[10], (D_MODEL,), jnp.float32, -s, s)}
        return inp
    _L1_xattn_all = _L1_xattn_setup()
    _L1_xattn_in = {k: v for k, v in _L1_xattn_all.items() if k in ('Wq', 'bq', 'Wk', 'bk', 'Wv', 'bv', 'Wo', 'bo')}
    del _L1_xattn_all

    def _L1_ffn_setup():
        import jax, jax.numpy as jnp
        import numpy as np
        import math
        D_IN = 128
        FEATURES = (512, 512, 128)
        BATCH, SEQ = (8, 256)

        def _conn_dense(kernel_bool, x):
            w = jnp.where(kernel_bool, jnp.float32(1.0), jnp.float32(-1.0))
            return x @ w
        key = jax.random.key(seed)
        kx, kk0, kk1, kk2 = jax.random.split(key, 4)
        x = jax.random.normal(kx, (BATCH, SEQ, D_IN), dtype=jnp.float32)
        k0 = jax.random.randint(kk0, (2 * D_IN, FEATURES[0]), 0, 2).astype(jnp.bool_)
        k1 = jax.random.randint(kk1, (FEATURES[0], FEATURES[1]), 0, 2).astype(jnp.bool_)
        k2 = jax.random.randint(kk2, (FEATURES[1], FEATURES[2]), 0, 2).astype(jnp.bool_)
        s0 = jnp.asarray(1.0 / math.sqrt(2 * D_IN), dtype=jnp.float32)
        s1 = jnp.asarray(1.0 / math.sqrt(FEATURES[0]), dtype=jnp.float32)
        s2 = jnp.asarray(1.0 / math.sqrt(FEATURES[1]), dtype=jnp.float32)
        return {'x': x, 'k0': k0, 'k1': k1, 'k2': k2, 's0': s0, 's1': s1, 's2': s2}
    _L1_ffn_all = _L1_ffn_setup()
    _L1_ffn_in = {k: v for k, v in _L1_ffn_all.items() if k in ('k0', 'k1', 'k2', 's0', 's1', 's2')}
    del _L1_ffn_all
    return {'x': x, 'ctx_1024': ctx_1024, 'g_xattn': g_xattn, 'g_ffn': g_ffn, 'L0_xattn_Wq': _L0_xattn_in['Wq'], 'L0_xattn_bq': _L0_xattn_in['bq'], 'L0_xattn_Wk': _L0_xattn_in['Wk'], 'L0_xattn_bk': _L0_xattn_in['bk'], 'L0_xattn_Wv': _L0_xattn_in['Wv'], 'L0_xattn_bv': _L0_xattn_in['bv'], 'L0_xattn_Wo': _L0_xattn_in['Wo'], 'L0_xattn_bo': _L0_xattn_in['bo'], 'L0_ffn_wg1': _L0_ffn_in['wg1'], 'L0_ffn_bg1': _L0_ffn_in['bg1'], 'L0_ffn_wg2': _L0_ffn_in['wg2'], 'L0_ffn_bg2': _L0_ffn_in['bg2'], 'L0_ffn_We': _L0_ffn_in['We'], 'L0_ffn_be': _L0_ffn_in['be'], 'L1_xattn_Wq': _L1_xattn_in['Wq'], 'L1_xattn_bq': _L1_xattn_in['bq'], 'L1_xattn_Wk': _L1_xattn_in['Wk'], 'L1_xattn_bk': _L1_xattn_in['bk'], 'L1_xattn_Wv': _L1_xattn_in['Wv'], 'L1_xattn_bv': _L1_xattn_in['bv'], 'L1_xattn_Wo': _L1_xattn_in['Wo'], 'L1_xattn_bo': _L1_xattn_in['bo'], 'L1_ffn_k0': _L1_ffn_in['k0'], 'L1_ffn_k1': _L1_ffn_in['k1'], 'L1_ffn_k2': _L1_ffn_in['k2'], 'L1_ffn_s0': _L1_ffn_in['s0'], 'L1_ffn_s1': _L1_ffn_in['s1'], 'L1_ffn_s2': _L1_ffn_in['s2']}

def reference(x, ctx_1024, g_xattn, g_ffn, L0_xattn_Wq, L0_xattn_bq, L0_xattn_Wk, L0_xattn_bk, L0_xattn_Wv, L0_xattn_bv, L0_xattn_Wo, L0_xattn_bo, L0_ffn_wg1, L0_ffn_bg1, L0_ffn_wg2, L0_ffn_bg2, L0_ffn_We, L0_ffn_be, L1_xattn_Wq, L1_xattn_bq, L1_xattn_Wk, L1_xattn_bk, L1_xattn_Wv, L1_xattn_bv, L1_xattn_Wo, L1_xattn_bo, L1_ffn_k0, L1_ffn_k1, L1_ffn_k2, L1_ffn_s0, L1_ffn_s1, L1_ffn_s2):
    import jax
    import jax.numpy as jnp

    def _L0_xattn_ref(querys, keys, values, Wq, bq, Wk, bk, Wv, bv, Wo, bo):
        import jax, jax.numpy as jnp
        import numpy as np
        B, T, D_MODEL, N_HEAD = (1, 512, 128, 16)
        HEAD_DIM = D_MODEL // N_HEAD
        IS_CAUSAL = True

        def _mha(querys, keys, values, Wq, bq, Wk, bk, Wv, bv, Wo, bo):
            b, t, c = querys.shape
            q = (querys @ Wq.T + bq).reshape(b, t, N_HEAD, HEAD_DIM).transpose(0, 2, 1, 3)
            k = (keys @ Wk.T + bk).reshape(b, t, N_HEAD, HEAD_DIM).transpose(0, 2, 1, 3)
            v = (values @ Wv.T + bv).reshape(b, t, N_HEAD, HEAD_DIM).transpose(0, 2, 1, 3)
            scores = jnp.einsum('bhqd,bhkd->bhqk', q, k) / jnp.sqrt(jnp.float32(HEAD_DIM))
            if IS_CAUSAL:
                causal = jnp.tril(jnp.ones((t, t), dtype=bool))
                scores = jnp.where(causal, scores, jnp.float32(-jnp.inf))
            weights = jax.nn.softmax(scores, axis=-1)
            attn = jnp.einsum('bhqk,bhkd->bhqd', weights, v)
            out = attn.transpose(0, 2, 1, 3).reshape(b, t, c)
            return out @ Wo.T + bo
        return _mha(querys, keys, values, Wq, bq, Wk, bk, Wv, bv, Wo, bo)

    def _L0_ffn_ref(x, wg1, bg1, wg2, bg2, We, be):
        import jax, jax.numpy as jnp
        import numpy as np
        B, S, D, DO = (4, 256, 128, 128)
        E, K = (20, 2)
        Bv, Sv, Dv = x.shape
        xf = x.reshape(-1, Dv)
        h = jax.nn.gelu(xf @ wg1 + bg1, approximate=False)
        logits = (xf @ 0.0 + (h @ wg2 + bg2))[:, :E] if False else (h @ wg2 + bg2)[:, :E]
        probs = jax.nn.softmax(logits, axis=-1)
        top_vals, top_idx = jax.lax.top_k(probs, K)
        N = xf.shape[0]
        gates = jnp.zeros((N, E), xf.dtype).at[jnp.arange(N)[:, None], top_idx].set(top_vals)

        def body(y, eb):
            We_e, be_e, g_e = eb
            return (y + g_e[:, None] * (xf @ We_e + be_e), None)
        y0 = jnp.zeros((N, be.shape[-1]), xf.dtype)
        y, _ = jax.lax.scan(body, y0, (We, be, gates.T))
        return y.reshape(Bv, Sv, -1)

    def _L1_xattn_ref(queries, keys, values, Wq, bq, Wk, bk, Wv, bv, Wo, bo):
        import jax, jax.numpy as jnp
        import numpy as np
        D_MODEL = 128
        N_HEADS = 16
        HEAD_D = D_MODEL // N_HEADS
        B, L = (4, 256)
        EPS_CAUSAL = 1e-06

        def _feat(x):
            return jax.nn.elu(x) + 1.0

        def _causal_linear_attn(qs, ks, vs):

            def step(carry, xs):
                Si, Zi = carry
                q, k, v = xs
                Si = Si + jnp.einsum('bhd,bhk->bhdk', k, v)
                Zi = Zi + k
                num = jnp.einsum('bhd,bhkd->bhk', q, Si)
                Vi = num / (q * Zi + EPS_CAUSAL)
                return ((Si, Zi), Vi)
            Bn, Ln, H, D = qs.shape
            K = vs.shape[-1]
            Si0 = jnp.zeros((Bn, H, D, K), qs.dtype)
            Zi0 = jnp.zeros((Bn, H, D), qs.dtype)
            xs = (jnp.swapaxes(qs, 0, 1), jnp.swapaxes(ks, 0, 1), jnp.swapaxes(vs, 0, 1))
            _, out = jax.lax.scan(step, (Si0, Zi0), xs)
            return jnp.swapaxes(out, 0, 1)
        N, Lq, _ = queries.shape
        H = N_HEADS
        Q = (queries @ Wq + bq).reshape(N, Lq, H, -1)
        Kp = (keys @ Wk + bk).reshape(N, keys.shape[1], H, -1)
        V = (values @ Wv + bv).reshape(N, values.shape[1], H, -1)
        Q_lin = _feat(Q)
        K_lin = _feat(Kp)
        V_lin = _causal_linear_attn(Q_lin, K_lin, V)
        new_values = V_lin.reshape(N, Lq, -1)
        return new_values @ Wo + bo

    def _L1_ffn_ref(x, k0, k1, k2, s0, s1, s2):
        import jax, jax.numpy as jnp
        import numpy as np
        import math
        D_IN = 128
        FEATURES = (512, 512, 128)
        BATCH, SEQ = (8, 256)

        def _conn_dense(kernel_bool, x):
            w = jnp.where(kernel_bool, jnp.float32(1.0), jnp.float32(-1.0))
            return x @ w
        h = jnp.concatenate([x, -x], axis=-1)
        h = s0 * _conn_dense(k0, h)
        h = jax.nn.relu(h) * 2
        h = s1 * _conn_dense(k1, h)
        h = jax.nn.relu(h) * 2
        h = s2 * _conn_dense(k2, h)
        return h
    x = x + jnp.tanh(g_xattn[0]) * _L0_xattn_ref(_layernorm(x, axis=-1), ctx_1024, ctx_1024, L0_xattn_Wq, L0_xattn_bq, L0_xattn_Wk, L0_xattn_bk, L0_xattn_Wv, L0_xattn_bv, L0_xattn_Wo, L0_xattn_bo)
    x = x + jnp.tanh(g_ffn[0]) * _L0_ffn_ref(_layernorm(x, axis=-1), L0_ffn_wg1, L0_ffn_bg1, L0_ffn_wg2, L0_ffn_bg2, L0_ffn_We, L0_ffn_be)
    x = x + jnp.tanh(g_xattn[1]) * _L1_xattn_ref(_layernorm(x, axis=-1), ctx_1024, ctx_1024, L1_xattn_Wq, L1_xattn_bq, L1_xattn_Wk, L1_xattn_bk, L1_xattn_Wv, L1_xattn_bv, L1_xattn_Wo, L1_xattn_bo)
    x = x + jnp.tanh(g_ffn[1]) * _L1_ffn_ref(_layernorm(x, axis=-1), L1_ffn_k0, L1_ffn_k1, L1_ffn_k2, L1_ffn_s0, L1_ffn_s1, L1_ffn_s2)
    return x

_drawn_inputs = setup_inputs


def setup_inputs(seed=0):
    import zlib

    import numpy as np

    out = dict(_drawn_inputs(seed))
    spreads = {'g_ffn': (-1.0, 0.2),
     'L0_xattn_bq': (0.0, 0.358),
     'L0_xattn_bk': (0.0, 2.0),
     'L0_xattn_bv': (0.0, 0.1),
     'L0_xattn_bo': (0.0, 0.1),
     'L0_ffn_bg1': (0.0, 0.1),
     'L0_ffn_bg2': (0.0, 0.1),
     'L0_ffn_be': (0.0, 0.694)}
    factors = {'L1_xattn_bk': 27.555}
    for name, (base, spread) in spreads.items():
        noise = np.random.default_rng([zlib.crc32(name.encode()), seed]).standard_normal(out[name].shape)
        drawn = base * np.exp(spread * noise) if base else spread * noise
        out[name] = jnp.asarray(drawn.astype(out[name].dtype))
    for name, factor in factors.items():
        out[name] = (out[name] * factor).astype(out[name].dtype)
    return out
```

```python
from contextlib import ExitStack

import numpy as np

import concourse.bass as bass
from concourse import mybir

F32 = mybir.dt.float32
F16 = mybir.dt.float16
BF16 = mybir.dt.bfloat16
U8 = mybir.dt.uint8
I32 = mybir.dt.int32
ALU = mybir.AluOpType
ACT = mybir.ActivationFunctionType
AX = mybir.AxisListType

SEQS, T, D = 32, 128, 128
GB = 4
GROUPS = SEQS // GB
W = GB * T
H, HD = 16, 8
QUADS, PLACES = 4, 4
E = 20
HID = 32
FF = 512
FC = FF // 128
PARTS = 3
EPS = 1e-5
NEG = -1e30
EXTRA = 1
NE = 4
VH = 18
SCALE1 = 32.0


class Steps:

    def __init__(self, eng, sem):
        self.eng, self.sem, self.n, self.reg, self.stride = eng, sem, 0, None, 0

    def __call__(self, ins):
        self.n += 1
        ins.then_inc(self.sem, 1)
        self.eng.wait_ge(self.sem, self.n if self.reg is None else self.reg * self.stride + self.n)

    def enter(self, reg, stride):
        self.reg, self.stride, self.start = reg, stride, self.n

    def leave(self, trips):
        assert self.n - self.start == self.stride, (self.n - self.start, self.stride)
        self.n, self.reg = self.start + trips * self.stride, None


def build(nc, a, out):
    ctx = ExitStack()
    with ctx:
        def sb(name, shape, dt=F32):
            return ctx.enter_context(nc.sbuf_tensor(name, shape, dt))

        def bank(name):
            return ctx.enter_context(nc.psum_tensor(name, [128, W], F32))

        def sem(name):
            return ctx.enter_context(nc.semaphore(name))

        X = sb("X", [T, SEQS + GB * EXTRA, D])
        XB = sb("XB", [T, GB, D])
        stats = sb("stats", [T, GB, 6])
        mv = sb("mv", [T, GB, 2])
        veps = sb("veps", [T, GB])
        rstd = sb("rstd", [T, GB])
        xn = sb("xn", [T, GB, D])
        xnT = sb("xnT", [D, W])
        XN2T = sb("XN2T", [D, (GROUPS + EXTRA) * W])
        ctxg = [sb(f"ctxg{u}", [D, W]) for u in range(2)]
        QS = [sb(f"QS{u}", [D, 4, W], F16) for u in range(2)]
        KS = [sb(f"KS{u}", [D, 4, W], F16) for u in range(2)]
        Qst = [sb(f"Qst{u}", [128, QUADS, W], F16) for u in range(2)]
        Kpad = [sb(f"Kpad{u}", [128, QUADS, PLACES, W], F16) for u in range(2)]
        Vpad = [sb(f"Vpad{u}", [T, GB, VH, 32]) for u in range(2)]
        Eq = [sb(f"Eq{k}", [T, PLACES, T]) for k in range(NE)]
        rowmax = sb("rowmax", [T, GB, PLACES, QUADS])
        halfneg = sb("halfneg", [T, GB])
        mparts = sb("mparts", [T, GB, PLACES, 2, QUADS], F16)
        mT = [sb(f"mT{u}", [32, W], F16) for u in range(2)]
        Oraw = sb("Oraw", [128, 2, W])
        Rden = sb("Rden", [128, 2, W])
        On = sb("On", [128, 2, W])
        hT = sb("hT", [HID + 1, W])
        LOG, PRB, TMP, ONE1, ONE2 = (Vpad[u][:, :, :, :].rearrange("t b h c -> t (b h c)")[:, k * SEQS * E:(k + 1) * SEQS * E]
                                     .rearrange("t (s e) -> t s e", e=E) for u, k in ((0, 0), (0, 1), (0, 2), (1, 0), (1, 1)))
        red = sb("red", [T, SEQS])
        G3 = sb("G3", [T, SEQS + GB * EXTRA, 128], BF16)
        GT3 = sb("GT3", [128, W], BF16)
        xs = [Eq[k][:, :, :].rearrange("d i t -> d (i t)") for k in range(4)]
        yT = sb("yT", [D, W])
        scratch = [XN2T[:, k * W:(k + 1) * W] for k in range(6)]
        zmin, zexp, zmax = ({"q": scratch[2 * k], "k": scratch[2 * k + 1]} for k in range(3))
        den = sb("den", [128, W])
        phiQ = [sb(f"phiQ{u}", [128, W]) for u in range(2)]
        phiK = sb("phiK", [T, GB, D])
        ksum = sb("ksum", [T, GB, D])
        Wq0 = sb("Wq0", [D, D]); Wk0 = sb("Wk0", [D, D]); Wv0 = sb("Wv0", [D, D]); Wo0 = sb("Wo0", [D, D])
        Wo0R = sb("Wo0R", [128, 2, D])
        Wq1 = sb("Wq1", [D, D]); Wk1 = sb("Wk1", [D, D]); Wv1 = sb("Wv1", [D, D]); Wo1 = sb("Wo1", [D, D])
        cols = sb("cols", [128, 6])
        bvrep = sb("bvrep", [D, T])
        bo0 = sb("bo0", [T, D]); bo1 = sb("bo1", [T, D]); bk1 = sb("bk1", [T, D])
        wg1 = sb("wg1", [D, HID]); bg1 = sb("bg1", [HID, 1]); wg2 = sb("wg2", [HID + 1, E])
        We = sb("We", [D, E, D])
        beR = sb("beR", [128, D])
        beres = sb("beres", [128, D])
        BE = sb("BE", [128, PARTS, D], BF16)
        k0 = sb("k0", [D, 2, FF], U8); k1 = sb("k1", [128, FC, FF], U8); k2 = sb("k2", [128, FC, D], U8)
        w0 = sb("w0", [D, FF], F16); w1 = sb("w1", [128, FC, FF], F16); w2 = sb("w2", [128, FC, D], F16)
        gates = sb("gates", [128, 4]); tg = sb("tg", [128, 4])
        sc = sb("sc", [128, 3]); sg = sb("sg", [128, 3]); fac = sb("fac", [128, 3])
        idf = sb("idf", [128, 128]); idb = sb("idb", [128, 128], BF16); idh = sb("idh", [128, 128], F16)
        maskA = sb("maskA", [T, T], BF16)
        triT = sb("triT", [T, T])
        sel0 = sb("sel0", [128, 4, 4, 8]); sel1 = sb("sel1", [128, 2, 4, 8])
        SELE = sb("SELE", [128, E, 128], BF16)
        iotaI = sb("iotaI", [T, E], I32); rank = sb("rank", [T, E])
        xh, xl = Qst[0][:, 0, :], Qst[0][:, 1, :]
        u0h, u0l, u1h, u1l = (Kpad[0][:, k, :, :] for k in range(4))

        M0, M1, PA0, PA1, PB0, PB1, PO0, PO1 = (bank(n) for n in ("M0", "M1", "PA0", "PA1", "PB0", "PB1", "PO0", "PO1"))
        PA, PB, PO = [PA0, PA1], [PB0, PB1], [PO0, PO1]
        RING = [PA0, PA1, PB0, PB1]

        S = {}
        for name in ("x_first x_rest w_attn w_rest w_wo gates_in "
                     "pool_consts wo_clear kpad_clear kpad1_clear vpad_clear kq_const eps_const prep_q prep_wo prep_bo tanh_done bv_rep bo_ps "
                     "ctx0_in0 ctx0_in1 ctx1_in0 ctx1_in1 ln_var ln_rstd dve_step pool_step "
                     "xn_ready xnT_ps xnT_ready q_ps q_hi q_lo k_ps k_hi k_lo v_ps v_ready "
                     "pa_ps pa_free m_split m_ps m_T m_in0 m_in1 "
                     "pb_ps e_exp e_masked pv_done o_raw o_norm y_ps x1_ready xb_ready "
                     "n2_ready t2_ps t2_ready hid_ps hid_ready log_ps log_ready lmax lexp gates_done moe_consts "
                     "gt_ps gt_ready bc_ps xs_ready xs_used y3_T y3_tps x2_ready prep_rest "
                     "n3_ready t3_ps t3_ready q3_ps q3_min q3_exp q3_max q3_phi q3_hi q3_lo "
                     "v3_ps v3_hi v3_lo k3_ps k3_sum k3_min k3_exp k3_max k3_phi k3_ready z3_ps vclear "
                     "p4b_even p4b_odd p4_aD p4_cp p4_aP p4_pv p4_den p4_o p4_y x3_ready p4_xb "
                     "n4_ready t4_ps x4_hi x4_lo l1_ps u0_hi u0_lo l2_ps u1_hi u1_lo l3_ps out_ready out_done").split():
            S[name] = sem(name)
        STACKED = [[sem(f"stacked{u}_quad{q}") for q in range(QUADS)] for u in range(2)]
        PER_QUAD = 16 * (1 + PLACES)

        block = ctx.enter_context(nc.Block())
        W_ATTN, W_WO, W_REST = 16 * 8, 16 * 8, 16 * 17
        TRIPS = (GROUPS - 2) // 2

        def known(n, least):
            return isinstance(n, int) and n < least

        def attention_schedule(eng, body, step=None, steps=0):
            body(0, None, 0, None)
            body(1, 0, 1, None)
            with eng.Fori(0, TRIPS) as t:
                if step:
                    step.enter(t, 2 * steps)
                for half in range(2):
                    body(t * 2 + (half + 2), t * 2 + (half + 1), half, t)
            if step:
                step.leave(TRIPS)
            body(None, GROUPS - 1, 0, None)

        def group(tile, i, width=GB):
            return tile[:, i * width:(i + 1) * width] if isinstance(i, int) else tile[:, bass.ds(i * width, width)]

        @block.sync
        def _(sp):
            xg = a["x"].rearrange("b t d -> t b d")
            sp.dma_start(X[:, 0:2 * GB, :], xg[:, 0:2 * GB, :]).then_inc(S["x_first"], 16)
            sp.dma_start(ctxg[0][:, :], a["ctxT"][:, 0:W]).then_inc(S["ctx0_in0"], 16)
            sp.dma_start(ctxg[1][:, :], a["ctxT"][:, W:2 * W]).then_inc(S["ctx0_in1"], 16)
            sp.dma_start(X[:, 2 * GB:SEQS, :], xg[:, 2 * GB:SEQS, :]).then_inc(S["x_rest"], 16)

            def next_ctx(n, u, v_done, arrived):
                sp.wait_ge(S[v_done], n)
                sp.dma_start(ctxg[1 - u][:, :], group(a["ctxT"], n + 1, W)).then_inc(S[f"{arrived}{1 - u}"], 16)

            def stack_q(u, q):
                sp.dma_start(Qst[u][:, q, :], QS[u][32 * q:32 * q + 32, :, :]).then_inc(STACKED[u][q], 16)

            def stack_k(u, q):
                for i in range(PLACES):
                    p = 32 * q + 8 * i
                    sp.dma_start(Kpad[u][32 * i:32 * i + 32, q, i, :], KS[u][p:p + 8, :, :]).then_inc(STACKED[u][q], 16)

            def softmax_group(n, g, u, t):
                if n is None:
                    return
                if not known(n, 1):
                    next_ctx(n, u, "v_ps", "ctx0_in")
                sp.wait_ge(S["kpad_clear" if u == 0 else "kpad1_clear"], 1)
                sp.wait_ge(S["kq_const"], 1)
                if not known(n, 2):
                    sp.wait_ge(S["pv_done"], n * 16 - 16)
                sp.wait_ge(S["q_hi"], n + 1)
                sp.wait_ge(S["q_lo"], n + 1)
                sp.wait_ge(S["k_hi"], n + 1)
                sp.wait_ge(S["k_lo"], n + 1)
                for q in range(QUADS):
                    stack_q(u, q)
                    stack_k(u, q)
                sp.wait_ge(S["m_T"], n + 1)
                for i in range(PLACES):
                    sp.dma_start(Qst[u][32 * i + 3:32 * i + 8:4, :, :], mT[u][8 * i:8 * i + 8, :])\
                      .then_inc(S[f"m_in{u}"], 16)

            attention_schedule(sp, softmax_group)

            sp.wait_ge(S["ctx0_in0"], 16 * 5)
            sp.wait_ge(S["ctx0_in1"], 16 * 4)
            sp.wait_ge(S["v_ps"], GROUPS)
            sp.dma_start(ctxg[0][:, :], a["ctxT"][:, 0:W]).then_inc(S["ctx1_in0"], 16)
            sp.dma_start(ctxg[1][:, :], a["ctxT"][:, W:2 * W]).then_inc(S["ctx1_in1"], 16)

            def linear_group(n, g, u, t):
                if n is None:
                    return
                if not known(n, 1):
                    next_ctx(n, u, "k3_ps", "ctx1_in")
                if not known(n, 2):
                    sp.wait_ge(S["p4_pv"], n * 16 - 16)
                sp.wait_ge(S["v3_hi"], n + 1)
                sp.wait_ge(S["v3_lo"], n + 1)
                for q in range(QUADS):
                    stack_k(u, q)
                sp.wait_ge(S["q3_hi"], n + 1)
                sp.wait_ge(S["q3_lo"], n + 1)
                for q in range(QUADS):
                    stack_q(u, q)

            attention_schedule(sp, linear_group)
            sp.wait_ge(S["ctx1_in0"], 16 * 5)
            og = out.rearrange("b t d -> t b d")
            with sp.Fori(0, GROUPS) as n:
                sp.wait_ge(S["out_ready"], n + 1)
                sp.dma_start(og[:, bass.ds(n * GB, GB), :], X[:, bass.ds(n * GB, GB), :]).then_inc(S["out_done"], 16)
            sp.wait_ge(S["out_done"], 16 * GROUPS)

        @block.scalar
        def _(act):
            count = {"w_attn": 0, "w_wo": 0, "w_rest": 0}

            def load(dst, src, name):
                count[name] += 16
                act.dma_start(dst, src).then_inc(S[name], 16)

            def column(src, n=None):
                return a[src].rearrange("(p a) -> p a", a=1)

            for dst, src in ((Wq0, "WqT0"), (Wk0, "WkT0"), (Wv0, "WvT0")):
                load(dst[:, :], a[src], "w_attn")
            for j, src in enumerate(("bq0", "bk0", "bv0", "bq1", "bv1")):
                load(cols[:, j:j + 1], column(src), "w_attn")
            assert count["w_attn"] == W_ATTN
            act.dma_start(gates[:, 0:2], a["g_xattn"].partition_broadcast(128)).then_inc(S["gates_in"], 16)
            act.dma_start(gates[:, 2:4], a["g_ffn"].partition_broadcast(128)).then_inc(S["gates_in"], 16)
            for j, src in enumerate(("s0", "s1", "s2")):
                act.dma_start(sc[:, j:j + 1], a[src].partition_broadcast(128)).then_inc(S["gates_in"], 16)
            load(Wo0[:, :], a["WoT0"], "w_wo")
            load(bo0[:, :], a["bo0"].partition_broadcast(128), "w_wo")
            act.wait_ge(S["wo_clear"], 1)
            for c in range(6):
                rows = 3 * HD if c < 5 else HD
                load(Wo0R[32 * (c % 4):32 * (c % 4) + rows, c // 4, :], a["WoT0"][24 * c:24 * c + rows, :], "w_wo")
            assert count["w_wo"] == W_WO
            act.wait_ge(S["gates_in"], 80)
            nc.scalar.activation(tg[:, :], gates[:, :], ACT.Tanh)
            nc.scalar.activation(sg[:, :], sc[:, :], ACT.Sign).then_inc(S["tanh_done"], 1)

            def load_rest():
                act.wait_ge(S["prep_wo"], 1)
                for dst, src in ((Wq1, "Wq1"), (Wk1, "Wk1"), (Wv1, "Wv1"), (Wo1, "Wo1"), (wg1, "wg1")):
                    load(dst[:, :], a[src], "w_rest")
                load(bg1[:, :], column("bg1"), "w_rest")
                load(wg2[0:HID, :], a["wg2"][:, 0:E], "w_rest")
                load(wg2[HID:HID + 1, :], a["bg2"].rearrange("(a n) -> a n", a=1)[:, 0:E], "w_rest")
                load(We[:, :, :], a["We"].rearrange("e d n -> d e n"), "w_rest")
                for part in range(PARTS):
                    load(beR[32 * part:32 * part + E, :], a["be"], "w_rest")
                load(bo1[:, :], a["bo1"].partition_broadcast(128), "w_rest")
                load(bk1[:, :], a["bk1"].partition_broadcast(128), "w_rest")
                load(k0[:, :, :], a["k0"].rearrange("(c p) n -> p c n", p=128), "w_rest")
                load(k1[:, :, :], a["k1"].rearrange("(c p) n -> p c n", p=128), "w_rest")
                load(k2[:, :, :], a["k2"].rearrange("(c p) n -> p c n", p=128), "w_rest")
                assert count["w_rest"] == W_REST

            def parts_read(u, count):
                for q in range(QUADS):
                    act.wait_ge(STACKED[u][q], count)

            def normalised_t(n, count):
                act.wait_ge(S["xnT_ps"], count)
                if not known(n, 1):
                    act.wait_ge(S["q_ps"], n)
                nc.scalar.copy(xnT[:, :], M0[:, :]).then_inc(S["xnT_ready"], 1)

            def softmax_group(n, g, u, t):
                def values_by_token():
                    act.wait_ge(S["v_ps"], n + 1)
                    if known(n, 2):
                        act.wait_ge(S["vpad_clear"], 1)
                    else:
                        act.wait_ge(S["pv_done"], n * 16 - 16)
                    vin = M1[:, :].rearrange("t (b c) -> t b c", b=GB)
                    vout = Vpad[u][:, :, :, :].rearrange("t b h c -> t b (h c)")
                    for i, (lo, at) in enumerate(((0, 0), (8, 0), (8, 8))):
                        nc.scalar.copy(vout[:, :, 40 * i:40 * i + 480].rearrange("t b (c e) -> t b c e", e=96)[:, :, :, 0:HD],
                                       vin[:, :, lo:lo + 120].rearrange("t b (c e) -> t b c e", e=24)[:, :, :, at:at + HD])
                    nc.scalar.copy(Vpad[u][:, :, H - 1, 0:HD], vin[:, :, D - HD:D]).then_inc(S["v_ready"], 1)

                if n is not None:
                    act.wait_ge(S["q_ps"], n + 1)
                    if known(n, 1):
                        act.wait_ge(S["prep_q"], 1)
                    if not known(n, 2):
                        parts_read(u, (t + 1) * PER_QUAD)
                    nc.scalar.activation(QS[u][:, 0:3:2, :], M1[:, :].unsqueeze(1).broadcast_to([128, 2, W]),
                                         ACT.Identity, bias=cols[:, 5:6]).then_inc(S["q_hi"], 1)
                    act.wait_ge(S["k_ps"], n + 1)
                    nc.scalar.activation(KS[u][:, 0:2, :], M0[:, :].unsqueeze(1).broadcast_to([128, 2, W]),
                                         ACT.Identity, bias=cols[:, 1:2]).then_inc(S["k_hi"], 1)
                if n is not None:
                    values_by_token()
                if g is None:
                    load_rest()
                else:
                    for c in range(16):
                        act.wait_ge(S["pb_ps"], g * 16 + (c + 1))
                        if not (known(g, 1) and c < NE):
                            act.wait_ge(S["pv_done"], g * 16 + (c + 1 - NE))
                        nc.scalar.activation(Eq[c % NE][:, :, :].rearrange("s i t -> s (i t)"), PB[c % 2][:, :],
                                             ACT.Exp).then_inc(S["e_exp"], 1)
                if n is not None:
                    normalised_t(n + 1, n + 2)
                if g is not None:
                    act.wait_ge(S["pv_done"], g * 16 + 16)
                    if known(g, 1):
                        act.wait_ge(S["vpad_clear"], 1)
                    else:
                        act.wait_ge(S["o_norm"], g)
                    nc.scalar.copy(Oraw[:, 0, :], PO0[:, :])
                    nc.scalar.copy(Oraw[0:64, 1, :], PO1[0:64, :]).then_inc(S["o_raw"], 1)
                if n is not None:
                    act.wait_ge(S["m_ps"], n + 1)
                    if not known(n, 2):
                        act.wait_ge(S[f"m_in{u}"], (t + 1) * 64)
                    nc.scalar.copy(mT[u][:, :], M0[0:32, :]).then_inc(S["m_T"], 1)

            normalised_t(0, 1)
            attention_schedule(act, softmax_group)
            def gate_group(n):
                act.wait_ge(S["t2_ps"], n + 1)
                nc.scalar.copy(group(XN2T, n, W), M0[:, :]).then_inc(S["t2_ready"], 1)
                act.wait_ge(S["hid_ps"], n + 1)
                if known(n, 1):
                    act.wait_ge(S["w_rest"], W_REST)
                else:
                    act.wait_ge(S["log_ps"], n)
                nc.scalar.activation(hT[0:HID, :], M1[0:HID, :], ACT.Gelu, bias=bg1[:, :]).then_inc(S["hid_ready"], 1)

            gate_group(0)
            with act.Fori(1, GROUPS) as n:
                gate_group(n)
            act.wait_ge(S["lmax"], 1)
            nc.scalar.activation(PRB[:, :, :].rearrange("t s e -> t (s e)"), LOG[:, :, :].rearrange("t s e -> t (s e)"),
                                 ACT.Exp).then_inc(S["lexp"], 1)
            def gt_evac(g):
                act.wait_ge(S["gt_ps"], g + 1)
                if not known(g, 1):
                    act.wait_ge(S["bc_ps"], g * E)
                nc.scalar.copy(GT3[:, :], M0[:, :]).then_inc(S["gt_ready"], 1)

            def mix_group(g):
                gt_evac(g + 1)
                act.wait_ge(S["xs_used"], g * E + E)
                if not known(g, 1):
                    act.wait_ge(S["y3_tps"], g)
                nc.scalar.copy(yT[:, :], PO0[:, :]).then_inc(S["y3_T"], 1)

            gt_evac(0)
            mix_group(0)
            with act.Fori(1, GROUPS) as g:
                mix_group(g)
            def linear_t(n, count):
                act.wait_ge(S["t3_ps"], count)
                if not known(n, 1):
                    act.wait_ge(S["q3_ps"], n)
                nc.scalar.copy(xnT[:, :], M0[:, :]).then_inc(S["t3_ready"], 1)

            def linear_group(n, g, u, t):
                def q_hi():
                    act.wait_ge(S["q3_phi"], n + 1)
                    nc.scalar.activation(QS[u][:, 0:3:2, :], phiQ[u][:, :].unsqueeze(1).broadcast_to([128, 2, W]), ACT.Copy,
                                         scale=SCALE1).then_inc(S["q3_hi"], 1)

                def place_keys():
                    act.wait_ge(S["k3_phi"], n + 1)
                    if known(n, 2):
                        act.wait_ge(S["vclear"], 1)
                    else:
                        act.wait_ge(S["p4_pv"], n * 16 - 16)
                    vout = Vpad[u][:, :, :, :].rearrange("t b h c -> t b (h c)")
                    for i in range(PLACES):
                        at = 40 * i
                        last = nc.scalar.copy(
                            vout[:, :, 0:4 * D].rearrange("t b (q e) -> t b q e", e=D)[:, :, :, at:at + HD],
                            phiK[:, :, :].rearrange("t b (q e) -> t b q e", e=32)[:, :, :, 8 * i:8 * i + HD])
                    last.then_inc(S["k3_ready"], 1)

                if n is not None:
                    act.wait_ge(S["q3_min"], n + 1)
                    if not known(n, 1):
                        act.wait_ge(S["q3_phi"], n)
                    nc.scalar.activation(zexp["q"], zmin["q"], ACT.Exp).then_inc(S["q3_exp"], 1)
                    act.wait_ge(S["v3_ps"], n + 1)
                    parts_read(u, (GROUPS // 2 + (0 if t is None else t + 1)) * PER_QUAD)
                    nc.scalar.activation(KS[u][:, 0:2, :], M0[:, :].unsqueeze(1).broadcast_to([128, 2, W]),
                                         ACT.Identity, bias=cols[:, 4:5]).then_inc(S["v3_hi"], 1)
                    act.wait_ge(S["k3_min"], n + 1)
                    if not known(n, 1):
                        act.wait_ge(S["k3_phi"], n)
                    nc.scalar.activation(zexp["k"], zmin["k"], ACT.Exp).then_inc(S["k3_exp"], 1)
                if g is not None:
                    for c in range(16):
                        if c == 4 and n is not None:
                            q_hi()
                        if c == 10 and n is not None:
                            place_keys()
                        if c % 2 == 1:
                            act.wait_ge(S["p4b_odd"], g * 8 + (c // 2 + 1))
                            if not (known(g, 1) and c < NE):
                                act.wait_ge(S["p4_pv"], g * 16 + (c + 1 - NE))
                            nc.scalar.copy(Eq[c % NE][:, :, :].rearrange("s i t -> s (i t)"), PB1[:, :])\
                              .then_inc(S["p4_cp"], 1)
                else:
                    q_hi()
                    place_keys()
                if n is not None:
                    linear_t(n + 1, n + 2)

            linear_t(0, 1)
            attention_schedule(act, linear_group)
            def x_hi(n):
                act.wait_ge(S["t4_ps"], n + 1)
                nc.scalar.copy(xh[:, :], M0[:, :]).then_inc(S["x4_hi"], 1)

            def relu_hi(dst, ready, done, n):
                for f in range(FC):
                    act.wait_ge(S[ready], n * FC + (f + 1))
                    nc.scalar.activation(dst[:, f, :], RING[f][:, :], ACT.Relu).then_inc(S[done], 1)

            x_hi(0)
            relu_hi(u0h, "l1_ps", "u0_hi", 0)
            with act.Fori(0, GROUPS - 1) as n:
                relu_hi(u1h, "l2_ps", "u1_hi", n)
                x_hi(n + 1)
                relu_hi(u0h, "l1_ps", "u0_hi", n + 1)
            relu_hi(u1h, "l2_ps", "u1_hi", GROUPS - 1)

        @block.gpsimd
        def _(pool):
            g_ = nc.gpsimd
            step = Steps(pool, S["pool_step"])
            g_.memset(Wo0R[:, :, :], 0.0).then_inc(S["wo_clear"], 1)
            g_.memset(idf[:, :], 0.0)
            g_.memset(maskA[:, :], 0.0)
            step(g_.memset(triT[:, :], 1.0))
            step(g_.affine_select(out=idf[:, :], in_=idf[:, :], compare_op=ALU.not_equal, fill=1.0, base=0,
                                  pattern=[[-1, 128]], channel_multiplier=1))
            g_.affine_select(out=maskA[:, :], in_=maskA[:, :], compare_op=ALU.is_ge, fill=NEG, base=0,
                             pattern=[[-1, T]], channel_multiplier=1)
            g_.affine_select(out=triT[:, :], in_=triT[:, :], compare_op=ALU.is_ge, fill=0.0, base=0,
                             pattern=[[1, T]], channel_multiplier=-1)
            g_.tensor_copy(idb[:, :], idf[:, :])
            g_.tensor_copy(idh[:, :], idf[:, :]).then_inc(S["pool_consts"], 1)

            def mask_causal(e):
                last_query = slice(T - 1, T)
                g_.tensor_tensor(e[:, :, last_query], e[:, :, last_query],
                                 triT[:, last_query].unsqueeze(1).broadcast_to([T, PLACES, 1]), ALU.mult)
                return g_.affine_select(out=e[:, :, 0:T - 1], in_=e[:, :, 0:T - 1], compare_op=ALU.is_ge, fill=0.0, base=0,
                                        pattern=[[0, PLACES], [1, T - 1]], channel_multiplier=-1)

            def power(i):
                pool.wait_ge(S["ln_var"], i + 1)
                g_.tensor_tensor(rstd[:, :], veps[:, :], halfneg[:, :], ALU.pow).then_inc(S["ln_rstd"], 1)

            pool.wait_ge(S["eps_const"], 1)
            power(0)
            for u in range(2):
                g_.memset(QS[u][:, 3, :], 0.0)
                last = g_.memset(KS[u][:, 3, :], 1.0)
            last.then_inc(S["kq_const"], 1)
            g_.memset(Vpad[0][:, :, :, :], 0.0)
            step(g_.memset(Vpad[1][:, :, :, :], 0.0))
            for u in range(2):
                flat = Vpad[u][:, :, :, :].rearrange("t b h c -> t b (h c)").rearrange("t b (c e) -> t b c e", e=96)
                for i in range(3):
                    g_.memset(flat[:, :, 0:6 if i == 0 else 5, 33 * i + 24:33 * i + 25], 1.0)
            g_.memset(Oraw[:, 1, :], 0.0)
            g_.memset(On[:, 1, :], 0.0).then_inc(S["vpad_clear"], 1)

            g_.memset(sel0[:, :, :, :], 0.0)
            step(g_.memset(sel1[:, :, :, :], 0.0))

            def pick(dst, base, pattern):
                step(g_.affine_select(out=dst, in_=dst, compare_op=ALU.not_equal, fill=1.0, base=base,
                                      pattern=pattern, channel_multiplier=1))

            pick(sel0[:, :, 0:3, :], -24, [[-32, 4], [-1, 3], [0, 8]])
            pick(sel0[:, :, 3, :], -24, [[-32, 4], [0, 8]])
            pick(sel1[:, 0, 0:3, :], -24, [[-1, 3], [0, 8]])
            pick(sel1[:, 0, 3, :], -24, [[0, 8]])
            g_.affine_select(out=sel1[:, 1, :, :], in_=sel1[:, 1, :, :], compare_op=ALU.not_equal, fill=1.0, base=-56,
                             pattern=[[0, 4], [0, 8]], channel_multiplier=1).then_inc(S["pool_consts"], 1)

            def xb_add(bias, g, used, ready):
                if not known(g, 1):
                    pool.wait_ge(S[used], g)
                g_.tensor_tensor(XB[:, :, :], group(X, g), bias[:, :].unsqueeze(1).broadcast_to([T, GB, D]), ALU.add)\
                  .then_inc(S[ready], 1)

            def softmax_group(n, g, u, t):
                if n is not None:
                    power(n + 1)
                if g is not None and not known(g, 1):
                    xb_add(bo0, g - 1, "x1_ready", "xb_ready")
                if g is not None:
                    for c in range(16):
                        pool.wait_ge(S["e_exp"], g * 16 + (c + 1))
                        mask_causal(Eq[c % NE]).then_inc(S["e_masked"], 1)

            pool.wait_ge(S["prep_bo"], 1)
            attention_schedule(pool, softmax_group)
            xb_add(bo0, GROUPS - 1, "x1_ready", "xb_ready")
            step(g_.memset(SELE[:, :, :], 0.0))
            step(g_.memset(hT[HID:HID + 1, :], 1.0))
            step(g_.memset(G3[:, :, :], 0.0))
            for part in range(PARTS):
                pick(SELE[:, :, :], -32 * part, [[-1, E], [0, 128]])
            step(g_.iota(iotaI[:, :], [[-1, E]], base=E, channel_multiplier=0))
            g_.tensor_copy(rank[:, :], iotaI[:, :]).then_inc(S["moe_consts"], 1)
            LN2 = GROUPS + EXTRA
            with pool.Fori(LN2, 2 * LN2) as n:
                power(n)
            pool.wait_ge(S["gates_done"], 1)
            g_.memset(Vpad[0][:, :, :, :], 0.0)
            g_.memset(Vpad[1][:, :, :, :], 0.0).then_inc(S["vclear"], 1)
            power(2 * LN2)

            def linear_group(n, g, u, t):
                if n is not None:
                    power(n + (2 * LN2 + 1))
                    for z, phi in (("q", phiQ[u][:, :]), ("k", phiK[:, :, :].rearrange("t b d -> t (b d)"))):
                        pool.wait_ge(S[f"{z}3_exp"], n + 1)
                        pool.wait_ge(S[f"{z}3_max"], n + 1)
                        if z == "q":
                            if not known(n, 2):
                                pool.wait_ge(S["p4_den"], n - 1)
                        elif not known(n, 1):
                            pool.wait_ge(S["k3_ready"], n)
                            pool.wait_ge(S["z3_ps"], n)
                        g_.tensor_tensor(phi, zmax[z], zexp[z], ALU.add).then_inc(S[f"{z}3_phi"], 1)
                if g is not None:
                    for c in range(1, 16, 2):
                        if c == 7 and not known(g, 1):
                            xb_add(bo1, g - 1, "x3_ready", "p4_xb")
                        pool.wait_ge(S["p4_cp"], g * 8 + (c // 2 + 1))
                        mask_causal(Eq[c % NE]).then_inc(S["p4_aP"], 1)

            pool.wait_ge(S["prep_rest"], 1)
            attention_schedule(pool, linear_group)
            xb_add(bo1, GROUPS - 1, "x3_ready", "p4_xb")
            with pool.Fori(3 * LN2, 3 * LN2 + GROUPS) as n:
                power(n)

        @block.vector
        def _(dve):
            v = nc.vector
            step = Steps(dve, S["dve_step"])

            def ln_stats(i):
                src = group(X, i)
                for b in range(GB):
                    last = v.bn_stats(stats[:, b, :], src[:, b, :])
                step(last)
                v.memset(veps[:, :], EPS)
                for b in range(GB):
                    last = v.bn_aggr(mv[:, b, :], stats[:, b, :])
                step(last)
                v.tensor_tensor(veps[:, :], veps[:, :], mv[:, :, 1], ALU.add).then_inc(S["ln_var"], 1)

            def ln_norm(i, count, read, reads, ready):
                dve.wait_ge(S["ln_rstd"], count)
                if reads is not None:
                    dve.wait_ge(S[read], reads)
                src = group(X, i)
                for b in range(GB):
                    last = v.tensor_scalar(xn[:, b, :], src[:, b, :], mv[:, b, 0:1], rstd[:, b:b + 1],
                                           ALU.subtract, ALU.mult)
                last.then_inc(S[ready], 1)

            v.memset(halfneg[:, :], -0.5).then_inc(S["eps_const"], 1)
            dve.wait_ge(S["x_first"], 16)
            ln_stats(0)
            v.memset(Kpad[0][:, :, :, :].rearrange("p q i n -> p (q i n)").bitcast(F32), 0.0).then_inc(S["kpad_clear"], 1)
            v.memset(X[:, SEQS:SEQS + GB, :], 0.0)
            dve.wait_ge(S["w_attn"], W_ATTN)
            s = float(1.0 / np.sqrt(np.float32(HD)))
            v.tensor_scalar_mul(Wq0[:, :], Wq0[:, :], s)
            v.tensor_scalar_mul(cols[:, 5:6], cols[:, 0:1], s).then_inc(S["prep_q"], 1)
            v.tensor_copy(bvrep[:, :], cols[:, 2:3].broadcast_to([D, T])).then_inc(S["bv_rep"], 1)
            ln_norm(0, 1, None, None, "xn_ready")
            v.memset(Kpad[1][:, :, :, :].rearrange("p q i n -> p (q i n)").bitcast(F32), 0.0).then_inc(S["kpad1_clear"], 1)
            v.memset(XN2T[:, GROUPS * W:], 0.0)
            v.memset(beR[:, :], 0.0)
            dve.wait_ge(S["tanh_done"], 1)
            dve.wait_ge(S["w_wo"], W_WO)
            v.tensor_scalar_mul(Wo0R[:, :, :], Wo0R[:, :, :], tg[:, 0:1]).then_inc(S["prep_wo"], 1)
            dve.wait_ge(S["bo_ps"], 1)
            step(v.tensor_tensor(bo0[:, :], bo0[:, :], PO1[:, 0:D], ALU.add))
            v.tensor_scalar_mul(bo0[:, :], bo0[:, :], tg[:, 0:1]).then_inc(S["prep_bo"], 1)

            def normalise(g, earlier=0):
                at = g * 18 + (32 + earlier)
                dve.wait_ge(S["pa_ps"], at + 1)
                v.reciprocal(Rden[:, 0, :], PA0[:, :]).then_inc(S["pa_free"], 1)
                dve.wait_ge(S["pa_ps"], at + 2)
                v.reciprocal(Rden[0:64, 1, :], PA1[0:64, :]).then_inc(S["pa_free"], 1)
                dve.wait_ge(S["pa_free"], at + 2)
                if not known(g, 1):
                    dve.wait_ge(S["y_ps"], g)
                v.tensor_tensor(On[:, 0, :], Oraw[:, 0, :], Rden[:, 0, :], ALU.mult)
                v.tensor_tensor(On[0:64, 1, :], Oraw[0:64, 1, :], Rden[0:64, 1, :], ALU.mult).then_inc(S["o_norm"], 1)

            def softmax_group(n, g, u, t):
                if n is not None:
                    base = 0 if known(n, 1) else n * 18 - 2
                    if known(n, 2) and n == 1:
                        dve.wait_ge(S["x_rest"], 16)
                    ln_stats(n + 1)
                    dve.wait_ge(S["q_hi"], n + 1)
                    v.scalar_tensor_tensor(QS[u][:, 1, :], M1[:, :], cols[:, 5:6], QS[u][:, 0, :], ALU.add, ALU.subtract)\
                     .then_inc(S["q_lo"], 1)
                    dve.wait_ge(S["k_hi"], n + 1)
                    v.scalar_tensor_tensor(KS[u][:, 2, :], M0[:, :], cols[:, 1:2], KS[u][:, 0, :], ALU.add, ALU.subtract)\
                     .then_inc(S["k_lo"], 1)
                if g is not None and not known(g, 1):
                    normalise(g - 1)
                if n is None:
                    add_y(g - 1)
                else:
                    for c in range(16):
                        if c == 12 and g is not None and not known(g, 1):
                            add_y(g - 1)
                        if c == 4:
                            ln_norm(n + 1, n + 2, "xnT_ps", n + 1, "xn_ready")
                        dve.wait_ge(S["pa_ps"], base + (c + 1))
                        v.reduce_max(rowmax[:, c % 4, :, c // 4], PA[c % 2][:, :].rearrange("t (i s) -> t i s", i=PLACES),
                                     AX.X).then_inc(S["pa_free"], 1)
                    dve.wait_ge(S["pa_free"], base + 16)
                    if not known(n, 1):
                        dve.wait_ge(S["m_ps"], n)
                    mx = rowmax[:, :, :, :].rearrange("t b i q -> t (b i) q")
                    mp = mparts[:, :, :, :, :].rearrange("t b i r q -> t (b i) r q")
                    step(v.tensor_scalar_mul(mp[:, :, 0, :], mx, -1.0))
                    v.scalar_tensor_tensor(mp[:, :, 1, :], mx, -1.0, mp[:, :, 0, :], ALU.mult, ALU.subtract)\
                     .then_inc(S["m_split"], 1)

            def add_y(g):
                dve.wait_ge(S["xb_ready"], g + 1)
                dve.wait_ge(S["y_ps"], g + 1)
                v.tensor_tensor(group(X, g).rearrange("t b d -> t (b d)"), XB[:, :, :].rearrange("t b d -> t (b d)"),
                                M1[:, :], ALU.add).then_inc(S["x1_ready"], 1)

            attention_schedule(dve, softmax_group, step, 3)
            normalise(GROUPS - 1, -16)
            add_y(GROUPS - 1)
            dve.wait_ge(S["w_rest"], W_REST)
            v.tensor_scalar_mul(Wo1[:, :], Wo1[:, :], tg[:, 1:2])
            v.tensor_scalar_mul(bo1[:, :], bo1[:, :], tg[:, 1:2]).then_inc(S["prep_rest"], 1)
            v.tensor_scalar_mul(sg[:, 2:3], sg[:, 0:1], 2.0)
            v.tensor_scalar_mul(fac[:, 2:3], sg[:, 1:2], 0.125)
            step(v.tensor_scalar_mul(fac[:, 1:2], sg[:, 1:2], 0.25))
            step(v.tensor_tensor(w0[:, :], k0[:, 0, :], k0[:, 1, :], ALU.subtract))
            v.tensor_scalar_mul(w0[:, :], w0[:, :], sg[:, 2:3])
            v.tensor_scalar(w1[:, :, :], k1[:, :, :], fac[:, 1:2], fac[:, 2:3], ALU.mult, ALU.subtract)
            v.tensor_scalar(w2[:, :, :], k2[:, :, :], 2.0, -1.0, ALU.mult, ALU.add)
            step(v.tensor_tensor(sc[:, 0:2], sc[:, 0:2], sg[:, 0:2], ALU.mult))
            step(v.tensor_tensor(fac[:, 0:1], sc[:, 0:1], sc[:, 1:2], ALU.mult))
            step(v.tensor_tensor(fac[:, 0:1], fac[:, 0:1], sc[:, 2:3], ALU.mult))
            step(v.tensor_scalar(fac[:, 0:1], fac[:, 0:1], tg[:, 3:4], 32.0, ALU.mult, ALU.mult))
            step(v.tensor_copy(BE[:, 0, :], beR[:, :]))
            step(v.tensor_tensor(beres[:, :], beR[:, :], BE[:, 0, :], ALU.subtract))
            step(v.tensor_copy(BE[:, 1, :], beres[:, :]))
            step(v.tensor_tensor(beres[:, :], beres[:, :], BE[:, 1, :], ALU.subtract))
            v.tensor_copy(BE[:, 2, :], beres[:, :]).then_inc(S["prep_rest"], 1)

            LN2 = GROUPS + EXTRA

            def logits(n):
                dve.wait_ge(S["log_ps"], n + 1)
                v.tensor_copy(group(LOG, n), PO1[:, 0:GB * E].rearrange("t (b e) -> t b e", b=GB)).then_inc(S["log_ready"], 1)

            ln_stats(0)
            ln_norm(0, LN2 + 1, None, None, "n2_ready")
            ln_stats(1)
            ln_norm(1, LN2 + 2, "t2_ps", 1, "n2_ready")
            logits(0)
            with dve.Fori(1, GROUPS) as n:
                step.enter(n - 1, 2)
                ln_stats(n + 1)
                ln_norm(n + 1, n + (LN2 + 2), "t2_ps", n + 1, "n2_ready")
                logits(n)
            step.leave(GROUPS - 1)

            def over(x):
                return x[:, :].unsqueeze(2).broadcast_to([T, SEQS, E])

            ranks = rank[:, :].unsqueeze(1).broadcast_to([T, SEQS, E])
            dve.wait_ge(S["log_ready"], GROUPS)
            step(v.reduce_max(red[:, :], LOG[:, :, :], AX.X))
            v.tensor_tensor(LOG[:, :, :], LOG[:, :, :], over(red), ALU.subtract).then_inc(S["lmax"], 1)
            dve.wait_ge(S["lexp"], 1)
            step(v.reduce_sum(red[:, :], PRB[:, :, :], AX.X))
            step(v.reciprocal(red[:, :], red[:, :]))
            step(v.tensor_tensor(PRB[:, :, :], PRB[:, :, :], over(red), ALU.mult))
            dve.wait_ge(S["moe_consts"], 1)

            def first_of_max(one, values):
                step(v.reduce_max(red[:, :], values[:, :, :], AX.X))
                step(v.tensor_tensor(one[:, :, :], values[:, :, :], over(red), ALU.is_equal))
                step(v.tensor_tensor(one[:, :, :], one[:, :, :], ranks, ALU.mult))
                step(v.reduce_max(red[:, :], one[:, :, :], AX.X))
                step(v.tensor_tensor(one[:, :, :], ranks, over(red), ALU.is_equal))

            flat = "t s e -> t (s e)"
            first_of_max(ONE1, PRB)
            step(v.scalar_tensor_tensor(TMP[:, :, :].rearrange(flat), ONE1[:, :, :].rearrange(flat), -2.0,
                                        PRB[:, :, :].rearrange(flat), ALU.mult, ALU.add))
            first_of_max(ONE2, TMP)
            step(v.tensor_tensor(ONE1[:, :, :], ONE1[:, :, :], ONE2[:, :, :], ALU.add))
            step(v.tensor_tensor(PRB[:, :, :], PRB[:, :, :], ONE1[:, :, :], ALU.mult))
            step(v.tensor_scalar_mul(PRB[:, :, :], PRB[:, :, :], tg[:, 2:3]))
            part = [G3[:, 0:SEQS, 32 * r:32 * r + E] for r in range(PARTS)]
            step(v.tensor_copy(part[0], PRB[:, :, :]))
            step(v.tensor_tensor(TMP[:, :, :], PRB[:, :, :], part[0], ALU.subtract))
            step(v.tensor_copy(part[1], TMP[:, :, :]))
            step(v.tensor_tensor(TMP[:, :, :], TMP[:, :, :], part[1], ALU.subtract))
            v.tensor_copy(part[2], TMP[:, :, :]).then_inc(S["gates_done"], 1)
            def add_mix(g):
                dve.wait_ge(S["y3_tps"], g + 1)
                x = group(X, g).rearrange("t b d -> t (b d)")
                v.tensor_tensor(x, x, M1[:, :], ALU.add).then_inc(S["x2_ready"], 1)

            def mix_group(g):
                for e in range(E):
                    dve.wait_ge(S["bc_ps"], g * E + (e + 1))
                    if not (known(g, 1) and e < 4):
                        dve.wait_ge(S["xs_used"], g * E + (e - 3))
                    v.tensor_tensor(xs[e % 4], group(XN2T, g, W), RING[e % 4][:, :], ALU.mult)\
                     .then_inc(S["xs_ready"], 1)
                    if e == 4 and not known(g, 1):
                        add_mix(g - 1)

            mix_group(0)
            with dve.Fori(1, GROUPS) as g:
                mix_group(g)
            add_mix(GROUPS - 1)
            LN3 = 2 * LN2
            def add_y4(g):
                dve.wait_ge(S["p4_xb"], g + 1)
                dve.wait_ge(S["p4_y"], g + 1)
                v.tensor_tensor(group(X, g).rearrange("t b d -> t (b d)"), XB[:, :, :].rearrange("t b d -> t (b d)"),
                                M1[:, :], ALU.add).then_inc(S["x3_ready"], 1)

            def denominators(g, u):
                dve.wait_ge(S["z3_ps"], g + 1)
                v.tensor_tensor(den[:, :], phiQ[u][:, :], PA[u][:, :], ALU.mult).then_inc(S["p4_den"], 1)
                dve.wait_ge(S["p4_den"], g + 1)
                step(v.tensor_scalar(den[:, :], den[:, :], 1e-6, SCALE1, ALU.add, ALU.mult))

            def invert(lo, hi):
                step(v.reciprocal(den[:, lo * T:hi * T], den[:, lo * T:hi * T]))

            def normalise4(g, u):
                dve.wait_ge(S["p4_pv"], g * 16 + 16)
                if not known(g, 1):
                    dve.wait_ge(S["p4_y"], g)
                v.tensor_tensor(On[:, 0, :], den[:, :], PO[u][:, :], ALU.mult).then_inc(S["p4_o"], 1)

            def linear_group(n, g, u, t):
                before = g is not None and not known(g, 1)
                if before:
                    denominators(g - 1, u)
                if n is not None:
                    ln_stats(n + 1)
                    dve.wait_ge(S["q3_ps"], n + 1)
                    if not known(n, 1):
                        dve.wait_ge(S["q3_exp"], n)
                        dve.wait_ge(S["q3_phi"], n)
                    v.tensor_scalar(zmin["q"], M1[:, :], cols[:, 3:4], 0.0, ALU.add, ALU.min).then_inc(S["q3_min"], 1)
                    v.tensor_scalar(zmax["q"], M1[:, :], cols[:, 3:4], 0.0, ALU.add, ALU.max).then_inc(S["q3_max"], 1)
                    dve.wait_ge(S["v3_hi"], n + 1)
                    v.scalar_tensor_tensor(KS[u][:, 2, :], M0[:, :], cols[:, 4:5], KS[u][:, 0, :], ALU.add, ALU.subtract)\
                     .then_inc(S["v3_lo"], 1)
                    dve.wait_ge(S["k3_ps"], n + 1)
                    v.tensor_tensor(ksum[:, :, :], M1[:, :].rearrange("t (b d) -> t b d", b=GB),
                                    bk1[:, :].unsqueeze(1).broadcast_to([T, GB, D]), ALU.add).then_inc(S["k3_sum"], 1)
                    dve.wait_ge(S["k3_sum"], n + 1)
                    if not known(n, 1):
                        dve.wait_ge(S["k3_exp"], n)
                        dve.wait_ge(S["k3_phi"], n)
                    z = ksum[:, :, :].rearrange("t b d -> t (b d)")
                    v.tensor_scalar_min(zmin["k"], z, 0.0).then_inc(S["k3_min"], 1)
                    v.tensor_scalar_max(zmax["k"], z, 0.0).then_inc(S["k3_max"], 1)
                for c in range(16):
                    if g is not None and c % 2 == 0:
                        dve.wait_ge(S["p4b_even"], g * 8 + (c // 2 + 1))
                        if not (known(g, 1) and c < NE):
                            dve.wait_ge(S["p4_pv"], g * 16 + (c + 1 - NE))
                        v.tensor_tensor(Eq[c % NE][:, :, :], PB0[:, :].rearrange("s (i t) -> s i t", i=PLACES),
                                        triT[:, :].unsqueeze(1).broadcast_to([T, PLACES, T]), ALU.mult)\
                         .then_inc(S["p4_aD"], 1)
                    if before and c in (2, 4, 6, 8):
                        invert(c // 2 - 1, c // 2)
                    if before and c == 10:
                        normalise4(g - 1, u)
                    if before and c == 13:
                        add_y4(g - 1)
                    if c == 6 and n is not None:
                        dve.wait_ge(S["q3_hi"], n + 1)
                        v.scalar_tensor_tensor(QS[u][:, 1, :], phiQ[u][:, :], SCALE1, QS[u][:, 0, :], ALU.mult, ALU.subtract)\
                         .then_inc(S["q3_lo"], 1)
                    if c == 8 and n is not None:
                        ln_norm(n + 1, n + (LN3 + 2), "t3_ps", n + 1, "n3_ready")

            ln_stats(0)
            ln_norm(0, LN3 + 1, None, None, "n3_ready")
            attention_schedule(dve, linear_group, step, 7)
            denominators(GROUPS - 1, (GROUPS - 1) % 2)
            invert(0, GB)
            normalise4(GROUPS - 1, (GROUPS - 1) % 2)
            add_y4(GROUPS - 1)
            LN4 = 3 * LN2

            def x_lo(n):
                dve.wait_ge(S["x4_hi"], n + 1)
                v.tensor_tensor(xl[:, :], M0[:, :], xh[:, :], ALU.subtract).then_inc(S["x4_lo"], 1)

            def relu_lo(dst, hi, hi_done, done, n):
                for f in range(FC):
                    dve.wait_ge(S[hi_done], n * FC + (f + 1))
                    v.scalar_tensor_tensor(dst[:, f, :], RING[f][:, :], 0.0, hi[:, f, :], ALU.max, ALU.subtract)\
                     .then_inc(S[done], 1)

            ln_stats(0)
            ln_norm(0, LN4 + 1, None, None, "n4_ready")
            ln_stats(1)
            ln_norm(1, LN4 + 2, "t4_ps", 1, "n4_ready")
            x_lo(0)
            relu_lo(u0l, u0h, "u0_hi", "u0_lo", 0)

            def mlp_out(n):
                dve.wait_ge(S["l3_ps"], n + 1)
                x = group(X, n).rearrange("t b d -> t (b d)")
                v.scalar_tensor_tensor(x, M1[:, :], fac[:, 0:1], x, ALU.mult, ALU.add).then_inc(S["out_ready"], 1)

            def mlp_group(n, more):
                if more:
                    ln_stats(n + 2)
                relu_lo(u1l, u1h, "u1_hi", "u1_lo", n)
                x_lo(n + 1)
                if more:
                    ln_norm(n + 2, n + (LN4 + 3), "t4_ps", n + 2, "n4_ready")
                relu_lo(u0l, u0h, "u0_hi", "u0_lo", n + 1)
                mlp_out(n)

            with dve.Fori(0, GROUPS - 2) as n:
                step.enter(n, 2)
                mlp_group(n, True)
            step.leave(GROUPS - 2)
            mlp_group(GROUPS - 2, False)
            relu_lo(u1l, u1h, "u1_hi", "u1_lo", GROUPS - 1)
            mlp_out(GROUPS - 1)

        @block.tensor
        def _(pe):
            mm = nc.tensor.matmul

            def transposes(dst, src, done):
                for b in range(GB):
                    last = nc.tensor.transpose(dst[:, b * T:(b + 1) * T], src[:, b, :], idf[:, :])
                last.then_inc(S[done], 1)

            def cols_of(b):
                return slice(b * T, (b + 1) * T)

            pe.wait_ge(S["w_wo"], W_WO)
            pe.wait_ge(S["bv_rep"], 1)
            mm(PO1[:, 0:D], bvrep[:, :], Wo0[:, :], start=True, stop=True).then_inc(S["bo_ps"], 1)
            pe.wait_ge(S["pool_consts"], 1)

            def project_by_token(u, wv, done):
                for b in range(GB):
                    last = mm(M1[:, cols_of(b)], ctxg[u][:, cols_of(b)], wv[:, :], start=True, stop=True)
                last.then_inc(S[done], 1)

            def key_scores(u, c, dst, done):
                b, q = c // 4, c % 4
                for i in range(PLACES):
                    last = mm(dst[:, i * T:(i + 1) * T], Kpad[u][:, q, i, cols_of(b)], Qst[u][:, q, cols_of(b)],
                              start=True, stop=True)
                last.then_inc(S[done], 1)


            def turn(u_of_n, t, j_static):
                return j_static + 1 if t is None else t + u_of_n

            def transposed(n, free, frees, src_ready, done):
                pe.wait_ge(S[src_ready], n + 1)
                if not known(n, 1):
                    pe.wait_ge(S[free], frees)
                transposes(M0, xn, done)

            def next_normalised(n):
                pe.wait_ge(S["xn_ready"], n + 2)
                pe.wait_ge(S["k_lo"], n + 1)
                transposes(M0, xn, "xnT_ps")

            LAG = 4

            def softmax_group(n, g, u, t):
                last_g = n is None
                ug = 1 - u
                base = GROUPS * 18 - 2 if last_g else (0 if known(n, 1) else n * 18 - 2)
                jn = 1 if t is None else t + 2
                jg = (1 if known(g, 1) else GROUPS // 2) if t is None else (t + 1 if u == 0 else t + 2)

                def maxima_scores(c):
                    b, q = c % 4, c // 4
                    if b == 0:
                        pe.wait_ge(STACKED[u][q], jn * PER_QUAD)
                    if not (known(n, 1) and c < 2):
                        pe.wait_ge(S["pa_free"], base + (c - 1))
                    mm(PA[c % 2][:, :], idb[:, :], maskA[:, :].unsqueeze(1).broadcast_to([T, PLACES, T]), start=True, stop=False)
                    mm(PA[c % 2][:, :], Qst[u][:, q, cols_of(b)], Kpad[u][:, q, :, cols_of(b)], start=False, stop=True)\
                        .then_inc(S["pa_ps"], 1)

                def weigh_values(c):
                    b, q = c // 4, c % 4
                    pe.wait_ge(S["e_masked"], g * 16 + (c + 1))
                    if c == 0:
                        if known(g, 1):
                            pe.wait_ge(S["prep_bo"], 1)
                        else:
                            pe.wait_ge(S["o_raw"], g)
                    for i in range(PLACES):
                        h = 4 * q + i
                        at = 32 * ((h // 3) % 4)
                        last = mm(PO[h // 12][at:at + 32, cols_of(b)], Vpad[ug][:, b, h, :], Eq[c % NE][:, i, :],
                                  start=h % 3 == 0, stop=h % 3 == 2 or h == H - 1, tile_position=(0, at))
                    last.then_inc(S["pv_done"], 1)

                def attend(c):
                    if c < 16:
                        if c == 0:
                            pe.wait_ge(S[f"m_in{ug}"], jg * 64)
                            pe.wait_ge(S["v_ready"], g + 1)
                        if not (known(g, 1) and c < 2):
                            pe.wait_ge(S["e_exp"], g * 16 + (c - 1))
                        key_scores(ug, c, PB[c % 2], "pb_ps")
                    if c >= 2:
                        weigh_values(c - 2)

                if n is not None:
                    pe.wait_ge(S["xnT_ready"], n + 1)
                    if known(n, 1):
                        pe.wait_ge(S["prep_q"], 1)
                    else:
                        pe.wait_ge(S["v_ready"], n)
                    mm(M1[:, :], Wq0[:, :], xnT[:, :], start=True, stop=True).then_inc(S["q_ps"], 1)
                    pe.wait_ge(S[f"ctx0_in{u}"], jn * 16)
                    if not known(n, 1):
                        pe.wait_ge(S["m_T"], n)
                    mm(M0[:, :], Wk0[:, :], ctxg[u][:, :], start=True, stop=True).then_inc(S["k_ps"], 1)

                def values():
                    pe.wait_ge(S["q_lo"], n + 1)
                    project_by_token(u, Wv0, "v_ps")

                if n is not None:
                    values()
                if g is None:
                    for c in range(16):
                        maxima_scores(c)
                    next_normalised(n)
                else:
                    for c in range(16 + LAG):
                        if c < 18:
                            attend(c)
                        if c >= LAG and n is not None:
                            maxima_scores(c - LAG)
                        if c == 11 and not known(g, 1):
                            project_out(g - 1, GROUPS if last_g else n + 1)
                        if c == 15 + LAG - 3 and n is not None:
                            next_normalised(n)
                    at = base if last_g else base + 16
                    pe.wait_ge(S["o_raw"], g + 1)
                    if known(g, 1):
                        pe.wait_ge(S["pool_consts"], 2)
                    pe.wait_ge(S["pa_free"], at - 1)
                    mm(PA0[:, :], sel0[:, :, :, :].rearrange("p a i d -> p (a i d)"), Oraw[:, 0, :], start=True, stop=True)\
                        .then_inc(S["pa_ps"], 1)
                    pe.wait_ge(S["pa_free"], at)
                    mm(PA1[0:64, :], sel1[:, :, :, :].rearrange("p a i d -> p (a i d)"), Oraw[:, 1, :], start=True, stop=True)\
                        .then_inc(S["pa_ps"], 1)
                if n is not None:
                    pe.wait_ge(S["m_split"], n + 1)
                    pe.wait_ge(S["xnT_ready"], n + 2)
                    for b in range(GB):
                        last = mm(M0[0:32, cols_of(b)], mparts[:, b, :, :, :].rearrange("t i r q -> t (i r q)"), idh[:, :],
                                  start=True, stop=True)
                    last.then_inc(S["m_ps"], 1)

            def project_out(g, v_ready):
                pe.wait_ge(S["o_norm"], g + 1)
                pe.wait_ge(S["v_ready"], v_ready)
                if known(g, 1):
                    pe.wait_ge(S["prep_wo"], 1)
                for b in range(GB):
                    mm(M1[:, cols_of(b)], On[:, 0, cols_of(b)], Wo0R[:, 0, :], start=True, stop=False)
                    last = mm(M1[:, cols_of(b)], On[:, 1, cols_of(b)], Wo0R[:, 1, :], start=False, stop=True)
                last.then_inc(S["y_ps"], 1)

            pe.wait_ge(S["w_attn"], W_ATTN)
            pe.wait_ge(S["xn_ready"], 1)
            transposes(M0, xn, "xnT_ps")
            attention_schedule(pe, softmax_group)
            pe.wait_ge(S["x1_ready"], GROUPS - 1)
            project_out(GROUPS - 1, GROUPS)
            def gate_group(n):
                transposed(n, "t2_ready", n, "n2_ready", "t2_ps")
                pe.wait_ge(S["t2_ready"], n + 1)
                if known(n, 1):
                    pe.wait_ge(S["w_rest"], W_REST)
                    pe.wait_ge(S["x1_ready"], GROUPS)
                else:
                    pe.wait_ge(S["hid_ready"], n)
                mm(M1[0:HID, :], wg1[:, :], group(XN2T, n, W), start=True, stop=True).then_inc(S["hid_ps"], 1)
                pe.wait_ge(S["hid_ready"], n + 1)
                if known(n, 1):
                    pe.wait_ge(S["moe_consts"], 1)
                else:
                    pe.wait_ge(S["log_ready"], n)
                for b in range(GB):
                    last = mm(PO1[:, b * E:(b + 1) * E], hT[:, cols_of(b)], wg2[:, :], start=True, stop=True)
                last.then_inc(S["log_ps"], 1)

            pe.wait_ge(S["m_T"], GROUPS)
            gate_group(0)
            with pe.Fori(1, GROUPS) as n:
                gate_group(n)
            def transpose_gates(g):
                if not known(g, 1):
                    pe.wait_ge(S["gt_ready"], g)
                for b in range(GB):
                    src = G3[:, g * GB + b, :] if isinstance(g, int) else \
                        G3[:, bass.ds(g * GB + b, 1), :].rearrange("t s c -> t (s c)")
                    last = mm(M0[:, cols_of(b)], src, idb[:, :], start=True, stop=True)
                last.then_inc(S["gt_ps"], 1)

            def mix_group(g):
                def spread_gate(e):
                    if not (known(g, 1) and e < 4):
                        pe.wait_ge(S["xs_ready"], g * E + (e - 3))
                    mm(RING[e % 4][:, :], SELE[:, e, :], GT3[:, :], start=True, stop=True).then_inc(S["bc_ps"], 1)

                pe.wait_ge(S["gt_ready"], g + 1)
                for e in range(3):
                    spread_gate(e)
                if not known(g, 1):
                    transpose_mix(g - 1)
                if known(g, 1):
                    pe.wait_ge(S["prep_rest"], 2)
                for part in range(PARTS):
                    mm(PO0[:, :], BE[:, part, :], GT3[:, :], start=part == 0, stop=False)
                for e in range(E):
                    if e + 3 < E:
                        spread_gate(e + 3)
                    if e == 10:
                        transpose_gates(g + 1)
                    pe.wait_ge(S["xs_ready"], g * E + (e + 1))
                    mm(PO0[:, :], We[:, e, :], xs[e % 4], start=False, stop=e == E - 1).then_inc(S["xs_used"], 1)

            def transpose_mix(g):
                pe.wait_ge(S["y3_T"], g + 1)
                if not known(g, 1):
                    pe.wait_ge(S["x2_ready"], g)
                for b in range(GB):
                    last = nc.tensor.transpose(M1[:, cols_of(b)], yT[:, cols_of(b)], idf[:, :])
                last.then_inc(S["y3_tps"], 1)

            pe.wait_ge(S["gates_done"], 1)
            transpose_gates(0)
            mix_group(0)
            with pe.Fori(1, GROUPS) as g:
                mix_group(g)
            transpose_mix(GROUPS - 1)
            def linear_group(n, g, u, t):
                ug = 1 - u
                jn = 1 if t is None else t + 2
                jg = (1 if known(g, 1) else GROUPS // 2) if t is None else (t + 1 if u == 0 else t + 2)
                if n is not None:
                    pe.wait_ge(S["t3_ready"], n + 1)
                    if known(n, 1):
                        pe.wait_ge(S["x2_ready"], GROUPS)
                    else:
                        pe.wait_ge(S["k3_sum"], n)
                    mm(M1[:, :], Wq1[:, :], xnT[:, :], start=True, stop=True).then_inc(S["q3_ps"], 1)
                    pe.wait_ge(S[f"ctx1_in{u}"], jn * 16)
                    mm(M0[:, :], Wv1[:, :], ctxg[u][:, :], start=True, stop=True).then_inc(S["v3_ps"], 1)
                    pe.wait_ge(S["q3_max"], n + 1)
                    project_by_token(u, Wk1, "k3_ps")

                def key_sums():
                    pe.wait_ge(S["k3_phi"], n + 1)
                    if not known(n, 2):
                        pe.wait_ge(S["p4_den"], n - 1)
                    for b in range(GB):
                        last = mm(PA[u][:, cols_of(b)], phiK[:, b, :], triT[:, :], start=True, stop=True)
                    last.then_inc(S["z3_ps"], 1)

                def next_transposed():
                    pe.wait_ge(S["n3_ready"], n + 2)
                    pe.wait_ge(S["v3_lo"], n + 1)
                    transposes(M0, xn, "t3_ps")

                if g is None:
                    key_sums()
                    next_transposed()
                    return
                for c in range(18):
                    if c < 16:
                        if c == 0:
                            for q in range(QUADS):
                                pe.wait_ge(STACKED[ug][q], (GROUPS // 2 + jg) * PER_QUAD)
                            pe.wait_ge(S["k3_ready"], g + 1)
                        if not (known(g, 1) and c < 2):
                            pe.wait_ge(S["p4_cp" if c % 2 else "p4_aD"], g * 8 + c // 2)
                        key_scores(ug, c, PB[c % 2], "p4b_odd" if c % 2 else "p4b_even")
                    if c >= 2:
                        m = c - 2
                        b, q = m // 4, m % 4
                        pe.wait_ge(S["p4_aP" if m % 2 else "p4_aD"], g * 8 + (m // 2 + 1))
                        if m == 0:
                            if known(g, 2):
                                pe.wait_ge(S["y3_T"], GROUPS)
                            else:
                                pe.wait_ge(S["p4_o"], g - 1)
                        for i in range(PLACES):
                            last = mm(PO[ug][32 * q:32 * q + 32, cols_of(b)], Vpad[ug][:, b, 4 * q + i, :], Eq[m % NE][:, i, :],
                                      start=i == 0, stop=i == PLACES - 1, tile_position=(0, 32 * q))
                        last.then_inc(S["p4_pv"], 1)
                    if c == 13 and not known(g, 1):
                        linear_out(g - 1, GROUPS if n is None else n + 1)
                    if c == 12 and n is not None:
                        key_sums()
                    if c == 15 and n is not None:
                        next_transposed()

            def linear_out(g, keys_read):
                pe.wait_ge(S["p4_o"], g + 1)
                pe.wait_ge(S["k3_sum"], keys_read)
                if known(g, 1):
                    pe.wait_ge(S["prep_rest"], 1)
                for b in range(GB):
                    last = mm(M1[:, cols_of(b)], On[:, 0, cols_of(b)], Wo1[:, :], start=True, stop=True)
                last.then_inc(S["p4_y"], 1)

            pe.wait_ge(S["gt_ready"], GROUPS + 1)
            pe.wait_ge(S["n3_ready"], 1)
            transposes(M0, xn, "t3_ps")
            attention_schedule(pe, linear_group)
            pe.wait_ge(S["x3_ready"], GROUPS - 1)
            linear_out(GROUPS - 1, GROUPS)
            def mlp_first(n):
                pe.wait_ge(S["x4_lo"], n + 1)
                for f in range(FC):
                    if not known(n, 1):
                        pe.wait_ge(S["u1_lo"], n * FC + (f + 1 - FC))
                    cols_f = slice(f * 128, (f + 1) * 128)
                    mm(RING[f][:, :], w0[:, cols_f], xh[:, :], start=True, stop=False)
                    mm(RING[f][:, :], w0[:, cols_f], xl[:, :], start=False, stop=True).then_inc(S["l1_ps"], 1)

            def mlp_second(n):
                pe.wait_ge(S["u0_lo"], n * FC + FC)
                for f in range(FC):
                    for k in range(FC):
                        w = w1[:, k, f * 128:(f + 1) * 128]
                        mm(RING[f][:, :], w, u0h[:, k, :], start=k == 0, stop=False)
                        last = mm(RING[f][:, :], w, u0l[:, k, :], start=False, stop=k == FC - 1)
                    last.then_inc(S["l2_ps"], 1)

            def mlp_third(n):
                pe.wait_ge(S["u1_lo"], n * FC + FC)
                if known(n, 1):
                    pe.wait_ge(S["x3_ready"], GROUPS)
                else:
                    pe.wait_ge(S["out_ready"], n)
                for b in range(GB):
                    for k in range(FC):
                        mm(M1[:, cols_of(b)], u1h[:, k, cols_of(b)], w2[:, k, :], start=k == 0, stop=False)
                        last = mm(M1[:, cols_of(b)], u1l[:, k, cols_of(b)], w2[:, k, :], start=False, stop=k == FC - 1)
                last.then_inc(S["l3_ps"], 1)

            pe.wait_ge(S["v3_lo"], GROUPS)
            transposed(0, None, None, "n4_ready", "t4_ps")
            mlp_first(0)

            def mlp_group(n):
                mlp_second(n)
                transposed(n + 1, "x4_lo", n + 1, "n4_ready", "t4_ps")
                mlp_first(n + 1)
                mlp_third(n)

            mlp_group(0)
            with pe.Fori(1, GROUPS - 1) as n:
                mlp_group(n)
            mlp_second(GROUPS - 1)
            mlp_third(GROUPS - 1)


ARRAYS = {"x": "x", "g_xattn": "g_xattn", "g_ffn": "g_ffn",
          "bq0": "L0_xattn_bq", "bk0": "L0_xattn_bk", "bv0": "L0_xattn_bv", "bo0": "L0_xattn_bo",
          "wg1": "L0_ffn_wg1", "bg1": "L0_ffn_bg1", "wg2": "L0_ffn_wg2", "bg2": "L0_ffn_bg2", "We": "L0_ffn_We", "be": "L0_ffn_be",
          "Wq1": "L1_xattn_Wq", "Wk1": "L1_xattn_Wk", "Wv1": "L1_xattn_Wv", "Wo1": "L1_xattn_Wo",
          "bq1": "L1_xattn_bq", "bk1": "L1_xattn_bk", "bv1": "L1_xattn_bv", "bo1": "L1_xattn_bo"}


def kernel(**inputs):
    from concourse import bacc
    from concourse.bass_utils import run_bass_kernel_spmd
    i = {name: np.asarray(value) for name, value in inputs.items()}
    arrays = {short: i[name] for short, name in ARRAYS.items()}
    ctx_t = np.zeros((D, (GROUPS + EXTRA) * W), np.float32)
    ctx_t[:, :GROUPS * W] = i["ctx_1024"].transpose(2, 0, 1).reshape(D, GROUPS * W)
    arrays["ctxT"] = ctx_t
    for w in "qkvo":
        arrays[f"W{w}T0"] = i[f"L0_xattn_W{w}"].T
    for k in range(3):
        arrays[f"k{k}"] = i[f"L1_ffn_k{k}"]
        arrays[f"s{k}"] = i[f"L1_ffn_s{k}"].reshape(1)
    arrays = {name: np.ascontiguousarray(value) for name, value in arrays.items()}

    nc = bacc.Bacc("TRN2", target_bir_lowering=False, num_devices=1)
    aps = {name: nc.dram_tensor(f"in_{name}", list(value.shape), mybir.dt.from_np(value.dtype), kind="ExternalInput").ap()
           for name, value in arrays.items()}
    out = nc.dram_tensor("out_x", [SEQS, T, D], F32, kind="ExternalOutput").ap()
    build(nc, aps, out)
    result = run_bass_kernel_spmd(nc, [{f"in_{name}": value for name, value in arrays.items()}], core_ids=[0])
    return result.results[0]["out_x"]
```

```python
from contextlib import ExitStack

import numpy as np

import concourse.bass as bass
from concourse import mybir

F32 = mybir.dt.float32
F16 = mybir.dt.float16
BF16 = mybir.dt.bfloat16
U8 = mybir.dt.uint8
I32 = mybir.dt.int32
ALU = mybir.AluOpType
ACT = mybir.ActivationFunctionType
AX = mybir.AxisListType

SEQS, T, D = 32, 128, 128
GB = 4
GROUPS = SEQS // GB
W = GB * T
H, HD = 16, 8
QUADS, PLACES = 4, 4
E = 20
HID = 32
FF = 512
FC = FF // 128
PARTS = 3
EPS = 1e-5
NEG = -1e30
EXTRA = 1
NE = 4
VH = 18
SCALE1 = 32.0


class Steps:

    def __init__(self, eng, sem):
        self.eng, self.sem, self.n, self.reg, self.stride = eng, sem, 0, None, 0

    def __call__(self, ins):
        self.n += 1
        ins.then_inc(self.sem, 1)
        self.eng.wait_ge(self.sem, self.n if self.reg is None else self.reg * self.stride + self.n)

    def enter(self, reg, stride):
        self.reg, self.stride, self.start = reg, stride, self.n

    def leave(self, trips):
        assert self.n - self.start == self.stride, (self.n - self.start, self.stride)
        self.n, self.reg = self.start + trips * self.stride, None


def build(nc, a, out):
    ctx = ExitStack()
    with ctx:
        def sb(name, shape, dt=F32):
            return ctx.enter_context(nc.sbuf_tensor(name, shape, dt))

        def bank(name):
            return ctx.enter_context(nc.psum_tensor(name, [128, W], F32))

        def sem(name):
            return ctx.enter_context(nc.semaphore(name))

        X = sb("X", [T, SEQS + GB * EXTRA, D])
        XB = sb("XB", [T, GB, D])
        stats = sb("stats", [T, GB, 6])
        mv = sb("mv", [T, GB, 2])
        veps = sb("veps", [T, GB])
        rstd = sb("rstd", [T, GB])
        xn = sb("xn", [T, GB, D])
        xnT = sb("xnT", [D, W])
        XN2T = sb("XN2T", [D, GROUPS * W])
        ctxg = [sb(f"ctxg{u}", [D, W]) for u in range(2)]
        QS = [sb(f"QS{u}", [D, 4, W], F16) for u in range(2)]
        KS = [sb(f"KS{u}", [D, 4, W], F16) for u in range(2)]
        Qst = [sb(f"Qst{u}", [128, QUADS, W], F16) for u in range(2)]
        Kpad = [sb(f"Kpad{u}", [128, QUADS, PLACES, W], F16) for u in range(2)]
        Vpad = [sb(f"Vpad{u}", [T, GB, VH, 32]) for u in range(2)]
        Eq = [sb(f"Eq{k}", [T, PLACES, T]) for k in range(NE)]
        rowmax = sb("rowmax", [T, GB, PLACES, QUADS])
        halfneg = sb("halfneg", [T, GB])
        mparts = sb("mparts", [T, GB, PLACES, 2, QUADS], F16)
        mT = [sb(f"mT{u}", [32, W], F16) for u in range(2)]
        Oraw = sb("Oraw", [128, 2, W])
        Rden = sb("Rden", [128, 2, W])
        On = sb("On", [128, 2, W])
        hT = sb("hT", [HID + 1, W])
        LOG, PRB, TMP, ONE1, ONE2 = (sb(name, [T, GB, E]) for name in ("LOG", "PRB", "TMP", "ONE1", "ONE2"))
        red = sb("red", [T, GB])
        G3 = sb("G3", [T, GB, 128], BF16)
        GT3 = sb("GT3", [128, GROUPS * W], BF16)
        xs = [Eq[k][:, :, :].rearrange("d i t -> d (i t)") for k in range(4)]
        yT = sb("yT", [D, W])
        scratch = [XN2T[:, k * W:(k + 1) * W] for k in range(6)]
        zmin, zexp, zmax = ({"q": scratch[2 * k], "k": scratch[2 * k + 1]} for k in range(3))
        den = sb("den", [128, W])
        phiQ = [sb(f"phiQ{u}", [128, W]) for u in range(2)]
        phiK = sb("phiK", [T, GB, D])
        ksum = sb("ksum", [T, GB, D])
        Wq0 = sb("Wq0", [D, D]); Wk0 = sb("Wk0", [D, D]); Wv0 = sb("Wv0", [D, D]); Wo0 = sb("Wo0", [D, D])
        Wo0R = sb("Wo0R", [128, 2, D])
        Wq1 = sb("Wq1", [D, D]); Wk1 = sb("Wk1", [D, D]); Wv1 = sb("Wv1", [D, D]); Wo1 = sb("Wo1", [D, D])
        cols = sb("cols", [128, 6])
        bvrep = sb("bvrep", [D, T])
        bo0 = sb("bo0", [T, D]); bo1 = sb("bo1", [T, D]); bk1 = sb("bk1", [T, D])
        wg1 = sb("wg1", [D, HID]); bg1 = sb("bg1", [HID, 1]); wg2 = sb("wg2", [HID + 1, E])
        We = sb("We", [D, E, D])
        beR = sb("beR", [128, D])
        beres = sb("beres", [128, D])
        BE = sb("BE", [128, PARTS, D], BF16)
        k0 = sb("k0", [D, 2, FF], U8); k1 = sb("k1", [128, FC, FF], U8); k2 = sb("k2", [128, FC, D], U8)
        w0 = sb("w0", [D, FF], F16); w1 = sb("w1", [128, FC, FF], F16); w2 = sb("w2", [128, FC, D], F16)
        gates = sb("gates", [128, 4]); tg = sb("tg", [128, 4])
        sc = sb("sc", [128, 3]); sg = sb("sg", [128, 3]); fac = sb("fac", [128, 3])
        idf = sb("idf", [128, 128]); idb = sb("idb", [128, 128], BF16); idh = sb("idh", [128, 128], F16)
        maskA = sb("maskA", [T, T], BF16)
        triT = sb("triT", [T, T])
        sel0 = sb("sel0", [128, 4, 4, 8]); sel1 = sb("sel1", [128, 2, 4, 8])
        SELE = sb("SELE", [128, E, 128], BF16); expert_rows = sb("expert_rows", [128, E])
        iotaI = sb("iotaI", [T, E], I32); rank = sb("rank", [T, E])
        xh, xl = Qst[0][:, 0, :], Qst[0][:, 1, :]
        u0h, u0l, u1h, u1l = (Kpad[0][:, k, :, :] for k in range(4))

        M0, M1, PA0, PA1, PB0, PB1, PO0, PO1 = (bank(n) for n in ("M0", "M1", "PA0", "PA1", "PB0", "PB1", "PO0", "PO1"))
        PA, PB, PO = [PA0, PA1], [PB0, PB1], [PO0, PO1]
        RING = [PA0, PA1, PB0, PB1]

        S = {}
        for name in ("x_first x_rest w_attn w_rest w_wo gates_in "
                     "pool_consts expert_rows wo_clear kpad_clear kpad1_clear vpad_clear kq_const eps_const prep_q prep_wo prep_bo tanh_done bv_rep bo_ps "
                     "ctx0_in0 ctx0_in1 ctx1_in0 ctx1_in1 ln_var ln_rstd dve_step pool_step "
                     "xn_ready xnT_ps xnT_ready q_ps q_hi q_lo k_ps k_hi k_lo v_ps v_ready "
                     "pa_ps pa_free m_split m_ps m_T m_in0 m_in1 "
                     "pb_ps e_exp e_masked pv_done o_raw o_norm y_ps x1_ready xb_ready "
                     "n2_ready t2_ps t2_ready hid_ps hid_ready log_ps lmax lexp gates_done moe_consts "
                     "gt_ps gt_ready bc_ps xs_ready xs_used y3_T y3_tps x2_ready prep_rest "
                     "n3_ready t3_ps t3_ready q3_ps q3_min q3_exp q3_max q3_phi q3_hi q3_lo "
                     "v3_ps v3_hi v3_lo k3_ps k3_sum k3_min k3_exp k3_max k3_phi k3_ready z3_ps vclear "
                     "p4b_even p4b_odd p4_aD p4_cp p4_aP p4_pv p4_den p4_o p4_y x3_ready p4_xb "
                     "n4_ready t4_ps x4_hi x4_lo l1_ps u0_hi u0_lo l2_ps u1_hi u1_lo l3_ps out_ready out_done").split():
            S[name] = sem(name)
        STACKED = [[sem(f"stacked{u}_quad{q}") for q in range(QUADS)] for u in range(2)]
        PER_QUAD = 16 * (1 + PLACES)

        block = ctx.enter_context(nc.Block())
        W_ATTN, W_WO, W_REST = 16 * 8, 16 * 8, 16 * 17
        LN2 = GROUPS + EXTRA
        LN3 = LN2 + GROUPS
        LN4 = LN3 + GROUPS + EXTRA
        TRIPS = (GROUPS - 2) // 2

        def known(n, least):
            return isinstance(n, int) and n < least

        def attention_schedule(eng, body, step=None, steps=0):
            body(0, None, 0, None)
            body(1, 0, 1, None)
            with eng.Fori(0, TRIPS) as t:
                if step:
                    step.enter(t, 2 * steps)
                for half in range(2):
                    body(t * 2 + (half + 2), t * 2 + (half + 1), half, t)
            if step:
                step.leave(TRIPS)
            body(None, GROUPS - 1, 0, None)

        def column(src):
            return a[src].rearrange("(p a) -> p a", a=1)

        def group(tile, i, width=GB):
            return tile[:, i * width:(i + 1) * width] if isinstance(i, int) else tile[:, bass.ds(i * width, width)]

        @block.sync
        def _(sp):
            xg = a["x"].rearrange("b t d -> t b d")
            sp.dma_start(X[:, 0:2 * GB, :], xg[:, 0:2 * GB, :]).then_inc(S["x_first"], 16)
            sp.dma_start(ctxg[0][:, :], a["ctxT"][:, 0:W]).then_inc(S["ctx0_in0"], 16)
            sp.dma_start(ctxg[1][:, :], a["ctxT"][:, W:2 * W]).then_inc(S["ctx0_in1"], 16)
            sp.dma_start(X[:, 2 * GB:SEQS, :], xg[:, 2 * GB:SEQS, :]).then_inc(S["x_rest"], 16)

            def next_ctx(n, u, v_done, arrived):
                sp.wait_ge(S[v_done], n)
                sp.dma_start(ctxg[1 - u][:, :], group(a["ctxT"], n + 1, W)).then_inc(S[f"{arrived}{1 - u}"], 16)

            def stack_q(u, q):
                sp.dma_start(Qst[u][:, q, :], QS[u][32 * q:32 * q + 32, :, :]).then_inc(STACKED[u][q], 16)

            def stack_k(u, q):
                for i in range(PLACES):
                    p = 32 * q + 8 * i
                    sp.dma_start(Kpad[u][32 * i:32 * i + 32, q, i, :], KS[u][p:p + 8, :, :]).then_inc(STACKED[u][q], 16)

            def softmax_group(n, g, u, t):
                if n is None:
                    return
                if not known(n, 1):
                    next_ctx(n, u, "v_ps", "ctx0_in")
                sp.wait_ge(S["kpad_clear" if u == 0 else "kpad1_clear"], 1)
                sp.wait_ge(S["kq_const"], 1)
                if not known(n, 2):
                    sp.wait_ge(S["pv_done"], n * 16 - 16)
                sp.wait_ge(S["q_hi"], n + 1)
                sp.wait_ge(S["q_lo"], n + 1)
                sp.wait_ge(S["k_hi"], n + 1)
                sp.wait_ge(S["k_lo"], n + 1)
                for q in range(QUADS):
                    stack_q(u, q)
                    stack_k(u, q)
                sp.wait_ge(S["m_T"], n + 1)
                for i in range(PLACES):
                    sp.dma_start(Qst[u][32 * i + 3:32 * i + 8:4, :, :], mT[u][8 * i:8 * i + 8, :])\
                      .then_inc(S[f"m_in{u}"], 16)

            attention_schedule(sp, softmax_group)

            sp.wait_ge(S["ctx0_in0"], 16 * 5)
            sp.wait_ge(S["ctx0_in1"], 16 * 4)
            sp.wait_ge(S["v_ps"], GROUPS)
            sp.dma_start(ctxg[0][:, :], a["ctxT"][:, 0:W]).then_inc(S["ctx1_in0"], 16)
            sp.dma_start(ctxg[1][:, :], a["ctxT"][:, W:2 * W]).then_inc(S["ctx1_in1"], 16)

            def linear_group(n, g, u, t):
                if n is None:
                    return
                if not known(n, 1):
                    next_ctx(n, u, "k3_ps", "ctx1_in")
                if not known(n, 2):
                    sp.wait_ge(S["p4_pv"], n * 16 - 16)
                sp.wait_ge(S["v3_hi"], n + 1)
                sp.wait_ge(S["v3_lo"], n + 1)
                for q in range(QUADS):
                    stack_k(u, q)
                sp.wait_ge(S["q3_hi"], n + 1)
                sp.wait_ge(S["q3_lo"], n + 1)
                for q in range(QUADS):
                    stack_q(u, q)

            attention_schedule(sp, linear_group)
            sp.wait_ge(S["ctx1_in0"], 16 * 5)
            og = out.rearrange("b t d -> t b d")
            with sp.Fori(0, GROUPS) as n:
                sp.wait_ge(S["out_ready"], n + 1)
                sp.dma_start(og[:, bass.ds(n * GB, GB), :], X[:, bass.ds(n * GB, GB), :]).then_inc(S["out_done"], 16)
            sp.wait_ge(S["out_done"], 16 * GROUPS)

        @block.scalar
        def _(act):
            count = {"w_attn": 0, "w_wo": 0}

            def load(dst, src, name):
                count[name] += 16
                act.dma_start(dst, src).then_inc(S[name], 16)

            for dst, src in ((Wq0, "WqT0"), (Wk0, "WkT0"), (Wv0, "WvT0")):
                load(dst[:, :], a[src], "w_attn")
            for j, src in enumerate(("bq0", "bk0", "bv0", "bq1", "bv1")):
                load(cols[:, j:j + 1], column(src), "w_attn")
            assert count["w_attn"] == W_ATTN
            act.dma_start(gates[:, 0:2], a["g_xattn"].partition_broadcast(128)).then_inc(S["gates_in"], 16)
            act.dma_start(gates[:, 2:4], a["g_ffn"].partition_broadcast(128)).then_inc(S["gates_in"], 16)
            for j, src in enumerate(("s0", "s1", "s2")):
                act.dma_start(sc[:, j:j + 1], a[src].partition_broadcast(128)).then_inc(S["gates_in"], 16)
            load(Wo0[:, :], a["WoT0"], "w_wo")
            load(bo0[:, :], a["bo0"].partition_broadcast(128), "w_wo")
            act.wait_ge(S["wo_clear"], 1)
            for c in range(6):
                rows = 3 * HD if c < 5 else HD
                load(Wo0R[32 * (c % 4):32 * (c % 4) + rows, c // 4, :], a["WoT0"][24 * c:24 * c + rows, :], "w_wo")
            assert count["w_wo"] == W_WO
            act.wait_ge(S["gates_in"], 80)
            nc.scalar.activation(tg[:, :], gates[:, :], ACT.Tanh)
            nc.scalar.activation(sg[:, :], sc[:, :], ACT.Sign).then_inc(S["tanh_done"], 1)

            def parts_read(u, count):
                for q in range(QUADS):
                    act.wait_ge(STACKED[u][q], count)

            def normalised_t(n, count):
                act.wait_ge(S["xnT_ps"], count)
                if not known(n, 1):
                    act.wait_ge(S["q_ps"], n)
                nc.scalar.copy(xnT[:, :], M0[:, :]).then_inc(S["xnT_ready"], 1)

            def gate_input(n):
                act.wait_ge(S["t2_ps"], n + 1)
                nc.scalar.copy(group(XN2T, n, W), M0[:, :]).then_inc(S["t2_ready"], 1)

            def gate_gelu(n):
                act.wait_ge(S["hid_ps"], n + 1)
                if known(n, 1):
                    act.wait_ge(S["w_rest"], W_REST)
                else:
                    act.wait_ge(S["log_ps"], n)
                nc.scalar.activation(hT[0:HID, :], M0[0:HID, :], ACT.Gelu, bias=bg1[:, :]).then_inc(S["hid_ready"], 1)

            def gate_exp(n):
                act.wait_ge(S["lmax"], n + 1)
                nc.scalar.activation(PRB[:, :, :].rearrange("t s e -> t (s e)"), LOG[:, :, :].rearrange("t s e -> t (s e)"),
                                     ACT.Exp).then_inc(S["lexp"], 1)

            def gates_by_expert(n):
                act.wait_ge(S["gt_ps"], n + 1)
                nc.scalar.copy(group(GT3, n, W), M0[:, :]).then_inc(S["gt_ready"], 1)

            def softmax_group(n, g, u, t):
                def values_by_token():
                    act.wait_ge(S["v_ps"], n + 1)
                    if known(n, 2):
                        act.wait_ge(S["vpad_clear"], 1)
                    else:
                        act.wait_ge(S["pv_done"], n * 16 - 16)
                    vin = M1[:, :].rearrange("t (b c) -> t b c", b=GB)
                    vout = Vpad[u][:, :, :, :].rearrange("t b h c -> t b (h c)")
                    for i, (lo, at) in enumerate(((0, 0), (8, 0), (8, 8))):
                        nc.scalar.copy(vout[:, :, 40 * i:40 * i + 480].rearrange("t b (c e) -> t b c e", e=96)[:, :, :, 0:HD],
                                       vin[:, :, lo:lo + 120].rearrange("t b (c e) -> t b c e", e=24)[:, :, :, at:at + HD])
                    nc.scalar.copy(Vpad[u][:, :, H - 1, 0:HD], vin[:, :, D - HD:D]).then_inc(S["v_ready"], 1)

                if n is not None:
                    act.wait_ge(S["q_ps"], n + 1)
                    if known(n, 1):
                        act.wait_ge(S["prep_q"], 1)
                    if not known(n, 2):
                        parts_read(u, (t + 1) * PER_QUAD)
                    nc.scalar.activation(QS[u][:, 0:3:2, :], M1[:, :].unsqueeze(1).broadcast_to([128, 2, W]),
                                         ACT.Identity, bias=cols[:, 5:6]).then_inc(S["q_hi"], 1)
                    act.wait_ge(S["k_ps"], n + 1)
                    nc.scalar.activation(KS[u][:, 0:2, :], M0[:, :].unsqueeze(1).broadcast_to([128, 2, W]),
                                         ACT.Identity, bias=cols[:, 1:2]).then_inc(S["k_hi"], 1)
                if n is not None:
                    values_by_token()
                if g is not None:
                    for c in range(16):
                        act.wait_ge(S["pb_ps"], g * 16 + (c + 1))
                        if not (known(g, 1) and c < NE):
                            act.wait_ge(S["pv_done"], g * 16 + (c + 1 - NE))
                        nc.scalar.activation(Eq[c % NE][:, :, :].rearrange("s i t -> s (i t)"), PB[c % 2][:, :],
                                             ACT.Exp).then_inc(S["e_exp"], 1)
                        if n is None and c == 10:
                            gate_input(0)
                if n is not None:
                    normalised_t(n + 1, n + 2)
                else:
                    gate_gelu(0)
                if g is not None:
                    act.wait_ge(S["pv_done"], g * 16 + 16)
                    if known(g, 1):
                        act.wait_ge(S["vpad_clear"], 1)
                    else:
                        act.wait_ge(S["o_norm"], g)
                    nc.scalar.copy(Oraw[:, 0, :], PO0[:, :])
                    nc.scalar.copy(Oraw[0:64, 1, :], PO1[0:64, :]).then_inc(S["o_raw"], 1)
                if n is not None:
                    act.wait_ge(S["m_ps"], n + 1)
                    if not known(n, 2):
                        act.wait_ge(S[f"m_in{u}"], (t + 1) * 64)
                    nc.scalar.copy(mT[u][:, :], M0[0:32, :]).then_inc(S["m_T"], 1)
                if known(g, 1):
                    act.wait_ge(S["expert_rows"], 1)
                    nc.scalar.copy(SELE[:, :, :], expert_rows[:, :].unsqueeze(2).broadcast_to([128, E, 128]))\
                      .then_inc(S["moe_consts"], 1)

            normalised_t(0, 1)
            attention_schedule(act, softmax_group)
            def linear_t(n, count):
                act.wait_ge(S["t3_ps"], count)
                if not known(n, 1):
                    act.wait_ge(S["q3_ps"], n)
                nc.scalar.copy(xnT[:, :], M0[:, :]).then_inc(S["t3_ready"], 1)

            def mix_group(g, gates, inputs):
                if gates:
                    gate_gelu(g + 1)
                    gate_exp(g + 1)
                else:
                    linear_t(0, 1)
                if inputs:
                    gate_input(g + 2)
                if gates:
                    gates_by_expert(g + 1)
                act.wait_ge(S["xs_used"], g * E + E)
                if not known(g, 1):
                    act.wait_ge(S["y3_tps"], g)
                nc.scalar.copy(yT[:, :], PO0[:, :]).then_inc(S["y3_T"], 1)

            gate_exp(0)
            gate_input(1)
            gates_by_expert(0)
            mix_group(0, True, True)
            with act.Fori(1, GROUPS - 2) as g:
                mix_group(g, True, True)
            mix_group(GROUPS - 2, True, False)
            mix_group(GROUPS - 1, False, False)
            def linear_group(n, g, u, t):
                def q_hi():
                    act.wait_ge(S["q3_phi"], n + 1)
                    nc.scalar.activation(QS[u][:, 0:3:2, :], phiQ[u][:, :].unsqueeze(1).broadcast_to([128, 2, W]), ACT.Copy,
                                         scale=SCALE1).then_inc(S["q3_hi"], 1)

                def place_keys():
                    act.wait_ge(S["k3_phi"], n + 1)
                    if known(n, 2):
                        act.wait_ge(S["vclear"], 1)
                    else:
                        act.wait_ge(S["p4_pv"], n * 16 - 16)
                    vout = Vpad[u][:, :, :, :].rearrange("t b h c -> t b (h c)")
                    for i in range(PLACES):
                        at = 40 * i
                        last = nc.scalar.copy(
                            vout[:, :, 0:4 * D].rearrange("t b (q e) -> t b q e", e=D)[:, :, :, at:at + HD],
                            phiK[:, :, :].rearrange("t b (q e) -> t b q e", e=32)[:, :, :, 8 * i:8 * i + HD])
                    last.then_inc(S["k3_ready"], 1)

                if n is not None:
                    act.wait_ge(S["q3_min"], n + 1)
                    if not known(n, 1):
                        act.wait_ge(S["q3_phi"], n)
                    nc.scalar.activation(zexp["q"], zmin["q"], ACT.Exp).then_inc(S["q3_exp"], 1)
                    act.wait_ge(S["v3_ps"], n + 1)
                    parts_read(u, (GROUPS // 2 + (0 if t is None else t + 1)) * PER_QUAD)
                    nc.scalar.activation(KS[u][:, 0:2, :], M0[:, :].unsqueeze(1).broadcast_to([128, 2, W]),
                                         ACT.Identity, bias=cols[:, 4:5]).then_inc(S["v3_hi"], 1)
                    act.wait_ge(S["k3_min"], n + 1)
                    if not known(n, 1):
                        act.wait_ge(S["k3_phi"], n)
                    nc.scalar.activation(zexp["k"], zmin["k"], ACT.Exp).then_inc(S["k3_exp"], 1)
                if g is not None:
                    for c in range(16):
                        if c == 4 and n is not None:
                            q_hi()
                        if c == 10 and n is not None:
                            place_keys()
                        if c % 2 == 1:
                            act.wait_ge(S["p4b_odd"], g * 8 + (c // 2 + 1))
                            if not (known(g, 1) and c < NE):
                                act.wait_ge(S["p4_pv"], g * 16 + (c + 1 - NE))
                            nc.scalar.copy(Eq[c % NE][:, :, :].rearrange("s i t -> s (i t)"), PB1[:, :])\
                              .then_inc(S["p4_cp"], 1)
                else:
                    q_hi()
                    place_keys()
                if n is not None:
                    linear_t(n + 1, n + 2)

            attention_schedule(act, linear_group)
            def x_hi(n):
                act.wait_ge(S["t4_ps"], n + 1)
                nc.scalar.copy(xh[:, :], M0[:, :]).then_inc(S["x4_hi"], 1)

            def relu_hi(dst, ready, done, n, chunks=range(FC)):
                for f in chunks:
                    act.wait_ge(S[ready], n * FC + (f + 1))
                    nc.scalar.activation(dst[:, f, :], RING[f][:, :], ACT.Relu).then_inc(S[done], 1)

            x_hi(0)
            relu_hi(u0h, "l1_ps", "u0_hi", 0)
            with act.Fori(0, GROUPS - 1) as n:
                relu_hi(u1h, "l2_ps", "u1_hi", n, range(FC - 1))
                x_hi(n + 1)
                relu_hi(u1h, "l2_ps", "u1_hi", n, [FC - 1])
                relu_hi(u0h, "l1_ps", "u0_hi", n + 1)
            relu_hi(u1h, "l2_ps", "u1_hi", GROUPS - 1)

        @block.gpsimd
        def _(pool):
            g_ = nc.gpsimd
            step = Steps(pool, S["pool_step"])
            g_.memset(Wo0R[:, :, :], 0.0).then_inc(S["wo_clear"], 1)
            g_.memset(idf[:, :], 0.0)
            g_.memset(maskA[:, :], 0.0)
            step(g_.memset(triT[:, :], 1.0))
            step(g_.affine_select(out=idf[:, :], in_=idf[:, :], compare_op=ALU.not_equal, fill=1.0, base=0,
                                  pattern=[[-1, 128]], channel_multiplier=1))
            g_.affine_select(out=maskA[:, :], in_=maskA[:, :], compare_op=ALU.is_ge, fill=NEG, base=0,
                             pattern=[[-1, T]], channel_multiplier=1)
            g_.affine_select(out=triT[:, :], in_=triT[:, :], compare_op=ALU.is_ge, fill=0.0, base=0,
                             pattern=[[1, T]], channel_multiplier=-1)
            g_.tensor_copy(idb[:, :], idf[:, :])
            g_.tensor_copy(idh[:, :], idf[:, :]).then_inc(S["pool_consts"], 1)

            def mask_causal(e):
                last_query = slice(T - 1, T)
                g_.tensor_tensor(e[:, :, last_query], e[:, :, last_query],
                                 triT[:, last_query].unsqueeze(1).broadcast_to([T, PLACES, 1]), ALU.mult)
                return g_.affine_select(out=e[:, :, 0:T - 1], in_=e[:, :, 0:T - 1], compare_op=ALU.is_ge, fill=0.0, base=0,
                                        pattern=[[0, PLACES], [1, T - 1]], channel_multiplier=-1)

            def power(i):
                pool.wait_ge(S["ln_var"], i + 1)
                g_.tensor_tensor(rstd[:, :], veps[:, :], halfneg[:, :], ALU.pow).then_inc(S["ln_rstd"], 1)

            pool.wait_ge(S["eps_const"], 1)
            power(0)
            for u in range(2):
                g_.memset(QS[u][:, 3, :], 0.0)
                last = g_.memset(KS[u][:, 3, :], 1.0)
            last.then_inc(S["kq_const"], 1)
            g_.memset(Vpad[0][:, :, :, :], 0.0)
            step(g_.memset(Vpad[1][:, :, :, :], 0.0))
            for u in range(2):
                flat = Vpad[u][:, :, :, :].rearrange("t b h c -> t b (h c)").rearrange("t b (c e) -> t b c e", e=96)
                for i in range(3):
                    g_.memset(flat[:, :, 0:6 if i == 0 else 5, 33 * i + 24:33 * i + 25], 1.0)
            g_.memset(Oraw[:, 1, :], 0.0)
            g_.memset(On[:, 1, :], 0.0).then_inc(S["vpad_clear"], 1)

            g_.memset(sel0[:, :, :, :], 0.0)
            step(g_.memset(sel1[:, :, :, :], 0.0))

            def pick(dst, base, pattern):
                step(g_.affine_select(out=dst, in_=dst, compare_op=ALU.not_equal, fill=1.0, base=base,
                                      pattern=pattern, channel_multiplier=1))

            pick(sel0[:, :, 0:3, :], -24, [[-32, 4], [-1, 3], [0, 8]])
            pick(sel0[:, :, 3, :], -24, [[-32, 4], [0, 8]])
            pick(sel1[:, 0, 0:3, :], -24, [[-1, 3], [0, 8]])
            pick(sel1[:, 0, 3, :], -24, [[0, 8]])
            g_.affine_select(out=sel1[:, 1, :, :], in_=sel1[:, 1, :, :], compare_op=ALU.not_equal, fill=1.0, base=-56,
                             pattern=[[0, 4], [0, 8]], channel_multiplier=1).then_inc(S["pool_consts"], 1)

            def xb_add(bias, g, used, ready):
                if not known(g, 1):
                    pool.wait_ge(S[used], g)
                g_.tensor_tensor(XB[:, :, :], group(X, g), bias[:, :].unsqueeze(1).broadcast_to([T, GB, D]), ALU.add)\
                  .then_inc(S[ready], 1)

            def mixture_constants():
                step(g_.memset(G3[:, :, :].rearrange("t s c -> t (s c)"), 0.0))
                step(g_.memset(hT[HID:HID + 1, :], 1.0))
                step(g_.tensor_tensor(expert_rows[:, :], idf[:, 0:E], idf[:, 32:32 + E], ALU.add))
                g_.tensor_tensor(expert_rows[:, :], expert_rows[:, :], idf[:, 64:64 + E], ALU.add).then_inc(S["expert_rows"], 1)
                step(g_.iota(iotaI[:, :], [[-1, E]], base=E, channel_multiplier=0))
                g_.tensor_copy(rank[:, :], iotaI[:, :]).then_inc(S["moe_consts"], 1)

            rest = []

            def load(dst, src):
                rest.append(pool.dma_start(dst, src).then_inc(S["w_rest"], 16))

            def load_small():
                for dst, src in ((Wq1, "Wq1"), (Wk1, "Wk1"), (Wv1, "Wv1"), (Wo1, "Wo1"), (wg1, "wg1")):
                    load(dst[:, :], a[src])
                load(bg1[:, :], column("bg1"))
                load(wg2[0:HID, :], a["wg2"][:, 0:E])
                load(wg2[HID:HID + 1, :], a["bg2"].rearrange("(a n) -> a n", a=1)[:, 0:E])

            def load_large():
                pool.wait_ge(S["prep_wo"], 1)
                for part in range(PARTS):
                    load(beR[32 * part:32 * part + E, :], a["be"])
                load(bo1[:, :], a["bo1"].partition_broadcast(128))
                load(bk1[:, :], a["bk1"].partition_broadcast(128))
                load(k0[:, :, :], a["k0"].rearrange("(c p) n -> p c n", p=128))
                load(k1[:, :, :], a["k1"].rearrange("(c p) n -> p c n", p=128))
                load(k2[:, :, :], a["k2"].rearrange("(c p) n -> p c n", p=128))
                load(We[:, :, :], a["We"].rearrange("e d n -> d e n"))
                assert 16 * len(rest) == W_REST

            def softmax_group(n, g, u, t):
                if n is not None:
                    power(n + 1)
                if g is None:
                    mixture_constants()
                    load_small()
                if known(g, 1):
                    pool.wait_ge(S["prep_bo"], 1)
                elif g is not None:
                    xb_add(bo0, g - 1, "x1_ready", "xb_ready")
                if g is not None:
                    for c in range(16):
                        if n is None and c in (4, 8):
                            power(LN2 + c // 4 - 1)
                        pool.wait_ge(S["e_exp"], g * 16 + (c + 1))
                        mask_causal(Eq[c % NE]).then_inc(S["e_masked"], 1)
                if known(g, 1):
                    load_large()

            attention_schedule(pool, softmax_group)
            xb_add(bo0, GROUPS - 1, "x1_ready", "xb_ready")
            pool.wait_ge(S["x1_ready"], GROUPS)
            g_.memset(Vpad[0][:, :, :, :], 0.0)
            g_.memset(Vpad[1][:, :, :, :], 0.0).then_inc(S["vclear"], 1)
            with pool.Fori(LN2 + 2, LN3 + 1) as n:
                power(n)
            def linear_group(n, g, u, t):
                if n is not None:
                    power(n + (LN3 + 1))
                    for z, phi in (("q", phiQ[u][:, :]), ("k", phiK[:, :, :].rearrange("t b d -> t (b d)"))):
                        pool.wait_ge(S[f"{z}3_exp"], n + 1)
                        pool.wait_ge(S[f"{z}3_max"], n + 1)
                        if z == "q":
                            if not known(n, 2):
                                pool.wait_ge(S["p4_den"], n - 1)
                        elif not known(n, 1):
                            pool.wait_ge(S["k3_ready"], n)
                            pool.wait_ge(S["z3_ps"], n)
                        g_.tensor_tensor(phi, zmax[z], zexp[z], ALU.add).then_inc(S[f"{z}3_phi"], 1)
                if g is not None:
                    for c in range(1, 16, 2):
                        if c == 7 and not known(g, 1):
                            xb_add(bo1, g - 1, "x3_ready", "p4_xb")
                        if c == 7 and n is None:
                            power(LN4)
                        pool.wait_ge(S["p4_cp"], g * 8 + (c // 2 + 1))
                        mask_causal(Eq[c % NE]).then_inc(S["p4_aP"], 1)

            pool.wait_ge(S["prep_rest"], 1)
            attention_schedule(pool, linear_group)
            xb_add(bo1, GROUPS - 1, "x3_ready", "p4_xb")
            with pool.Fori(LN4 + 1, LN4 + GROUPS) as n:
                power(n)

        @block.vector
        def _(dve):
            v = nc.vector
            step = Steps(dve, S["dve_step"])

            def ln_stats(i):
                src = group(X, i)
                for b in range(GB):
                    last = v.bn_stats(stats[:, b, :], src[:, b, :])
                step(last)
                v.memset(veps[:, :], EPS)
                for b in range(GB):
                    last = v.bn_aggr(mv[:, b, :], stats[:, b, :])
                step(last)
                v.tensor_tensor(veps[:, :], veps[:, :], mv[:, :, 1], ALU.add).then_inc(S["ln_var"], 1)

            def ln_norm(i, count, read, reads, ready):
                dve.wait_ge(S["ln_rstd"], count)
                if reads is not None:
                    dve.wait_ge(S[read], reads)
                src = group(X, i)
                for b in range(GB):
                    last = v.tensor_scalar(xn[:, b, :], src[:, b, :], mv[:, b, 0:1], rstd[:, b:b + 1],
                                           ALU.subtract, ALU.mult)
                last.then_inc(S[ready], 1)

            v.memset(halfneg[:, :], -0.5).then_inc(S["eps_const"], 1)
            dve.wait_ge(S["x_first"], 16)
            ln_stats(0)
            ln_norm(0, 1, None, None, "xn_ready")
            v.memset(Kpad[0][:, :, :, :].rearrange("p q i n -> p (q i n)").bitcast(F32), 0.0).then_inc(S["kpad_clear"], 1)
            dve.wait_ge(S["w_attn"], W_ATTN)
            s = float(1.0 / np.sqrt(np.float32(HD)))
            v.tensor_scalar_mul(Wq0[:, :], Wq0[:, :], s)
            v.tensor_scalar_mul(cols[:, 5:6], cols[:, 0:1], s).then_inc(S["prep_q"], 1)
            v.tensor_copy(bvrep[:, :], cols[:, 2:3].broadcast_to([D, T])).then_inc(S["bv_rep"], 1)

            def prepare_output():
                v.memset(Kpad[1][:, :, :, :].rearrange("p q i n -> p (q i n)").bitcast(F32), 0.0).then_inc(S["kpad1_clear"], 1)
                v.memset(X[:, SEQS:SEQS + GB, :], 0.0)
                v.memset(beR[:, :], 0.0)
                dve.wait_ge(S["tanh_done"], 1)
                dve.wait_ge(S["w_wo"], W_WO)
                v.tensor_scalar_mul(Wo0R[:, :, :], Wo0R[:, :, :], tg[:, 0:1]).then_inc(S["prep_wo"], 1)
                dve.wait_ge(S["bo_ps"], 1)
                step(v.tensor_tensor(bo0[:, :], bo0[:, :], PO1[:, 0:D], ALU.add))
                v.tensor_scalar_mul(bo0[:, :], bo0[:, :], tg[:, 0:1]).then_inc(S["prep_bo"], 1)

            def prepare_rest():
                dve.wait_ge(S["w_rest"], W_REST)
                v.tensor_scalar_mul(Wo1[:, :], Wo1[:, :], tg[:, 1:2])
                v.tensor_scalar_mul(bo1[:, :], bo1[:, :], tg[:, 1:2]).then_inc(S["prep_rest"], 1)
                v.tensor_scalar_mul(sg[:, 2:3], sg[:, 0:1], 2.0)
                v.tensor_scalar_mul(fac[:, 2:3], sg[:, 1:2], 0.125)
                step(v.tensor_scalar_mul(fac[:, 1:2], sg[:, 1:2], 0.25))
                step(v.tensor_tensor(w0[:, :], k0[:, 0, :], k0[:, 1, :], ALU.subtract))
                v.tensor_scalar_mul(w0[:, :], w0[:, :], sg[:, 2:3])
                v.tensor_scalar(w1[:, :, :], k1[:, :, :], fac[:, 1:2], fac[:, 2:3], ALU.mult, ALU.subtract)
                v.tensor_scalar(w2[:, :, :], k2[:, :, :], 2.0, -1.0, ALU.mult, ALU.add)
                step(v.tensor_tensor(sc[:, 0:2], sc[:, 0:2], sg[:, 0:2], ALU.mult))
                step(v.tensor_tensor(fac[:, 0:1], sc[:, 0:1], sc[:, 1:2], ALU.mult))
                step(v.tensor_tensor(fac[:, 0:1], fac[:, 0:1], sc[:, 2:3], ALU.mult))
                step(v.tensor_scalar(fac[:, 0:1], fac[:, 0:1], tg[:, 3:4], 32.0, ALU.mult, ALU.mult))
                step(v.tensor_copy(BE[:, 0, :], beR[:, :]))
                step(v.tensor_tensor(beres[:, :], beR[:, :], BE[:, 0, :], ALU.subtract))
                step(v.tensor_copy(BE[:, 1, :], beres[:, :]))
                step(v.tensor_tensor(beres[:, :], beres[:, :], BE[:, 1, :], ALU.subtract))
                v.tensor_copy(BE[:, 2, :], beres[:, :]).then_inc(S["prep_rest"], 1)

            def normalise(g, earlier=0):
                at = g * 18 + (32 + earlier)
                dve.wait_ge(S["pa_ps"], at + 1)
                v.reciprocal(Rden[:, 0, :], PA0[:, :]).then_inc(S["pa_free"], 1)
                dve.wait_ge(S["pa_ps"], at + 2)
                v.reciprocal(Rden[0:64, 1, :], PA1[0:64, :]).then_inc(S["pa_free"], 1)
                dve.wait_ge(S["pa_free"], at + 2)
                if not known(g, 1):
                    dve.wait_ge(S["y_ps"], g)
                v.tensor_tensor(On[:, 0, :], Oraw[:, 0, :], Rden[:, 0, :], ALU.mult)
                v.tensor_tensor(On[0:64, 1, :], Oraw[0:64, 1, :], Rden[0:64, 1, :], ALU.mult).then_inc(S["o_norm"], 1)

            def softmax_group(n, g, u, t):
                if n is not None:
                    base = 0 if known(n, 1) else n * 18 - 2
                    if known(n, 2) and n == 1:
                        dve.wait_ge(S["x_rest"], 16)
                    ln_stats(n + 1)
                    dve.wait_ge(S["q_hi"], n + 1)
                    v.scalar_tensor_tensor(QS[u][:, 1, :], M1[:, :], cols[:, 5:6], QS[u][:, 0, :], ALU.add, ALU.subtract)\
                     .then_inc(S["q_lo"], 1)
                    dve.wait_ge(S["k_hi"], n + 1)
                    v.scalar_tensor_tensor(KS[u][:, 2, :], M0[:, :], cols[:, 1:2], KS[u][:, 0, :], ALU.add, ALU.subtract)\
                     .then_inc(S["k_lo"], 1)
                    if known(n, 1):
                        prepare_output()
                if g is not None and not known(g, 1):
                    normalise(g - 1)
                if n is None:
                    ln_stats(0)
                    ln_norm(0, LN2 + 1, None, None, "n2_ready")
                    ln_stats(1)
                    ln_norm(1, LN2 + 2, "t2_ps", 1, "n2_ready")
                    prepare_rest()
                    add_y(g - 1)
                else:
                    for c in range(16):
                        if c == 12 and g is not None and not known(g, 1):
                            add_y(g - 1)
                        if c == 4:
                            ln_norm(n + 1, n + 2, "xnT_ps", n + 1, "xn_ready")
                        dve.wait_ge(S["pa_ps"], base + (c + 1))
                        v.reduce_max(rowmax[:, c % 4, :, c // 4], PA[c % 2][:, :].rearrange("t (i s) -> t i s", i=PLACES),
                                     AX.X).then_inc(S["pa_free"], 1)
                    dve.wait_ge(S["pa_free"], base + 16)
                    if not known(n, 1):
                        dve.wait_ge(S["m_ps"], n)
                    mx = rowmax[:, :, :, :].rearrange("t b i q -> t (b i) q")
                    mp = mparts[:, :, :, :, :].rearrange("t b i r q -> t (b i) r q")
                    step(v.tensor_scalar_mul(mp[:, :, 0, :], mx, -1.0))
                    v.scalar_tensor_tensor(mp[:, :, 1, :], mx, -1.0, mp[:, :, 0, :], ALU.mult, ALU.subtract)\
                     .then_inc(S["m_split"], 1)

            def add_y(g):
                dve.wait_ge(S["xb_ready"], g + 1)
                dve.wait_ge(S["y_ps"], g + 1)
                v.tensor_tensor(group(X, g).rearrange("t b d -> t (b d)"), XB[:, :, :].rearrange("t b d -> t (b d)"),
                                M1[:, :], ALU.add).then_inc(S["x1_ready"], 1)

            attention_schedule(dve, softmax_group, step, 3)
            def over(x):
                return x[:, :].unsqueeze(2).broadcast_to([T, GB, E])

            ranks = rank[:, :].unsqueeze(1).broadcast_to([T, GB, E])
            flat = "t s e -> t (s e)"

            def mark_max(one, values):
                step(v.tensor_tensor(one[:, :, :], values[:, :, :], over(red), ALU.is_equal))
                step(v.tensor_tensor(one[:, :, :], one[:, :, :], ranks, ALU.mult))

            def mark_first(one):
                step(v.reduce_max(red[:, :], one[:, :, :], AX.X))
                step(v.tensor_tensor(one[:, :, :], ranks, over(red), ALU.is_equal))

            part = [G3[:, :, 32 * r:32 * r + E] for r in range(PARTS)]
            LAST_GATE_STAGE = 17

            def gate_stage(n, k):
                if k == 5:
                    dve.wait_ge(S["log_ps"], n + 1)
                    step(v.reduce_max(red[:, :], logits(n), AX.X))
                elif k == 6:
                    v.tensor_tensor(LOG[:, :, :], logits(n), over(red), ALU.subtract).then_inc(S["lmax"], 1)
                elif k == 8:
                    dve.wait_ge(S["lexp"], n + 1)
                    step(v.reduce_sum(red[:, :], PRB[:, :, :], AX.X))
                    step(v.reciprocal(red[:, :], red[:, :]))
                elif k == 9:
                    step(v.tensor_tensor(PRB[:, :, :], PRB[:, :, :], over(red), ALU.mult))
                    step(v.reduce_max(red[:, :], PRB[:, :, :], AX.X))
                elif k == 10:
                    mark_max(ONE1, PRB)
                elif k == 11:
                    mark_first(ONE1)
                elif k == 12:
                    step(v.scalar_tensor_tensor(TMP[:, :, :].rearrange(flat), ONE1[:, :, :].rearrange(flat), -2.0,
                                                PRB[:, :, :].rearrange(flat), ALU.mult, ALU.add))
                    step(v.reduce_max(red[:, :], TMP[:, :, :], AX.X))
                elif k == 13:
                    mark_max(ONE2, TMP)
                elif k == 14:
                    mark_first(ONE2)
                elif k == 15:
                    step(v.tensor_tensor(ONE1[:, :, :], ONE1[:, :, :], ONE2[:, :, :], ALU.add))
                    step(v.tensor_tensor(PRB[:, :, :], PRB[:, :, :], ONE1[:, :, :], ALU.mult))
                    step(v.tensor_scalar_mul(PRB[:, :, :], PRB[:, :, :], tg[:, 2:3]))
                elif k == 16:
                    if not known(n, 1):
                        dve.wait_ge(S["gt_ps"], n)
                    step(v.tensor_copy(part[0], PRB[:, :, :]))
                    step(v.tensor_tensor(TMP[:, :, :], PRB[:, :, :], part[0], ALU.subtract))
                elif k == LAST_GATE_STAGE:
                    step(v.tensor_copy(part[1], TMP[:, :, :]))
                    step(v.tensor_tensor(TMP[:, :, :], TMP[:, :, :], part[1], ALU.subtract))
                    v.tensor_copy(part[2], TMP[:, :, :]).then_inc(S["gates_done"], 1)

            def logits(n):
                return (PA1 if known(n, 1) else PO1)[:, 0:GB * E].rearrange("t (b e) -> t b e", b=GB)

            GATE_STEPS = 22

            def add_mix(g):
                dve.wait_ge(S["y3_tps"], g + 1)
                x = group(X, g).rearrange("t b d -> t (b d)")
                v.tensor_tensor(x, x, M1[:, :], ALU.add).then_inc(S["x2_ready"], 1)

            def mix_group(g, gates, inputs):
                for e in range(E):
                    dve.wait_ge(S["bc_ps"], g * E + (e + 1))
                    if not (known(g, 1) and e < 4):
                        dve.wait_ge(S["xs_used"], g * E + (e - 3))
                    v.tensor_tensor(xs[e % 4], group(XN2T, g, W), RING[e % 4][:, :], ALU.mult)\
                     .then_inc(S["xs_ready"], 1)
                    if e == 1 and inputs:
                        ln_stats(g + 2)
                    if e == 2:
                        if known(g, 1):
                            add_y(GROUPS - 1)
                        else:
                            add_mix(g - 1)
                    if e == 4 and inputs:
                        ln_norm(g + 2, g + (LN2 + 3), "t2_ps", g + 2, "n2_ready")
                    if not gates:
                        if e == 5:
                            ln_stats(0)
                        if e == 9:
                            ln_norm(0, LN3 + 1, None, None, "n3_ready")
                    if gates:
                        gate_stage(g + 1, e)

            dve.wait_ge(S["moe_consts"], 2)
            for k in range(LAST_GATE_STAGE + 1):
                gate_stage(0, k)
            normalise(GROUPS - 1, -16)
            mix_group(0, True, True)
            with dve.Fori(1, GROUPS - 2) as g:
                step.enter(g - 1, 2 + GATE_STEPS)
                mix_group(g, True, True)
            step.leave(GROUPS - 3)
            mix_group(GROUPS - 2, True, False)
            mix_group(GROUPS - 1, False, False)
            add_mix(GROUPS - 1)
            def x_lo(n):
                dve.wait_ge(S["x4_hi"], n + 1)
                v.tensor_tensor(xl[:, :], M0[:, :], xh[:, :], ALU.subtract).then_inc(S["x4_lo"], 1)

            def add_y4(g):
                dve.wait_ge(S["p4_xb"], g + 1)
                dve.wait_ge(S["p4_y"], g + 1)
                v.tensor_tensor(group(X, g).rearrange("t b d -> t (b d)"), XB[:, :, :].rearrange("t b d -> t (b d)"),
                                M1[:, :], ALU.add).then_inc(S["x3_ready"], 1)

            def denominators(g, u):
                dve.wait_ge(S["z3_ps"], g + 1)
                v.tensor_tensor(den[:, :], phiQ[u][:, :], PA[u][:, :], ALU.mult).then_inc(S["p4_den"], 1)
                dve.wait_ge(S["p4_den"], g + 1)
                step(v.tensor_scalar(den[:, :], den[:, :], 1e-6, SCALE1, ALU.add, ALU.mult))

            def invert(lo, hi):
                step(v.reciprocal(den[:, lo * T:hi * T], den[:, lo * T:hi * T]))

            def normalise4(g, u):
                dve.wait_ge(S["p4_pv"], g * 16 + 16)
                if not known(g, 1):
                    dve.wait_ge(S["p4_y"], g)
                v.tensor_tensor(On[:, 0, :], den[:, :], PO[u][:, :], ALU.mult).then_inc(S["p4_o"], 1)

            def linear_group(n, g, u, t):
                before = g is not None and not known(g, 1)
                if before:
                    denominators(g - 1, u)
                if n is not None:
                    ln_stats(n + 1)
                    dve.wait_ge(S["q3_ps"], n + 1)
                    if not known(n, 1):
                        dve.wait_ge(S["q3_exp"], n)
                        dve.wait_ge(S["q3_phi"], n)
                    v.tensor_scalar(zmin["q"], M1[:, :], cols[:, 3:4], 0.0, ALU.add, ALU.min).then_inc(S["q3_min"], 1)
                    v.tensor_scalar(zmax["q"], M1[:, :], cols[:, 3:4], 0.0, ALU.add, ALU.max).then_inc(S["q3_max"], 1)
                    dve.wait_ge(S["v3_hi"], n + 1)
                    v.scalar_tensor_tensor(KS[u][:, 2, :], M0[:, :], cols[:, 4:5], KS[u][:, 0, :], ALU.add, ALU.subtract)\
                     .then_inc(S["v3_lo"], 1)
                    dve.wait_ge(S["k3_ps"], n + 1)
                    v.tensor_tensor(ksum[:, :, :], M1[:, :].rearrange("t (b d) -> t b d", b=GB),
                                    bk1[:, :].unsqueeze(1).broadcast_to([T, GB, D]), ALU.add).then_inc(S["k3_sum"], 1)
                    dve.wait_ge(S["k3_sum"], n + 1)
                    if not known(n, 1):
                        dve.wait_ge(S["k3_exp"], n)
                        dve.wait_ge(S["k3_phi"], n)
                    z = ksum[:, :, :].rearrange("t b d -> t (b d)")
                    v.tensor_scalar_min(zmin["k"], z, 0.0).then_inc(S["k3_min"], 1)
                    v.tensor_scalar_max(zmax["k"], z, 0.0).then_inc(S["k3_max"], 1)
                for c in range(16):
                    if g is not None and c % 2 == 0:
                        dve.wait_ge(S["p4b_even"], g * 8 + (c // 2 + 1))
                        if not (known(g, 1) and c < NE):
                            dve.wait_ge(S["p4_pv"], g * 16 + (c + 1 - NE))
                        v.tensor_tensor(Eq[c % NE][:, :, :], PB0[:, :].rearrange("s (i t) -> s i t", i=PLACES),
                                        triT[:, :].unsqueeze(1).broadcast_to([T, PLACES, T]), ALU.mult)\
                         .then_inc(S["p4_aD"], 1)
                    if before and c in (2, 4, 6, 8):
                        invert(c // 2 - 1, c // 2)
                    if before and c == 10:
                        normalise4(g - 1, u)
                    if before and c == 13:
                        add_y4(g - 1)
                    if n is None:
                        if c == 3:
                            ln_stats(0)
                        if c == 12:
                            ln_norm(0, LN4 + 1, None, None, "n4_ready")
                            ln_stats(1)
                    if c == 6 and n is not None:
                        dve.wait_ge(S["q3_hi"], n + 1)
                        v.scalar_tensor_tensor(QS[u][:, 1, :], phiQ[u][:, :], SCALE1, QS[u][:, 0, :], ALU.mult, ALU.subtract)\
                         .then_inc(S["q3_lo"], 1)
                    if c == 8 and n is not None:
                        ln_norm(n + 1, n + (LN3 + 2), "t3_ps", n + 1, "n3_ready")

            attention_schedule(dve, linear_group, step, 7)
            ln_norm(1, LN4 + 2, "t4_ps", 1, "n4_ready")
            denominators(GROUPS - 1, (GROUPS - 1) % 2)
            x_lo(0)
            invert(0, GB)
            normalise4(GROUPS - 1, (GROUPS - 1) % 2)

            def relu_lo(dst, hi, hi_done, done, n, chunks=range(FC)):
                for f in chunks:
                    dve.wait_ge(S[hi_done], n * FC + (f + 1))
                    v.scalar_tensor_tensor(dst[:, f, :], RING[f][:, :], 0.0, hi[:, f, :], ALU.max, ALU.subtract)\
                     .then_inc(S[done], 1)

            relu_lo(u0l, u0h, "u0_hi", "u0_lo", 0)
            add_y4(GROUPS - 1)

            def mlp_out(n):
                dve.wait_ge(S["l3_ps"], n + 1)
                x = group(X, n).rearrange("t b d -> t (b d)")
                v.scalar_tensor_tensor(x, M1[:, :], fac[:, 0:1], x, ALU.mult, ALU.add).then_inc(S["out_ready"], 1)

            def mlp_group(n, more):
                if more:
                    ln_stats(n + 2)
                relu_lo(u1l, u1h, "u1_hi", "u1_lo", n, range(FC - 1))
                x_lo(n + 1)
                relu_lo(u1l, u1h, "u1_hi", "u1_lo", n, [FC - 1])
                relu_lo(u0l, u0h, "u0_hi", "u0_lo", n + 1)
                if more:
                    ln_norm(n + 2, n + (LN4 + 3), "t4_ps", n + 2, "n4_ready")
                mlp_out(n)

            with dve.Fori(0, GROUPS - 2) as n:
                step.enter(n, 2)
                mlp_group(n, True)
            step.leave(GROUPS - 2)
            mlp_group(GROUPS - 2, False)
            relu_lo(u1l, u1h, "u1_hi", "u1_lo", GROUPS - 1)
            mlp_out(GROUPS - 1)

        @block.tensor
        def _(pe):
            mm = nc.tensor.matmul

            def transposes(dst, src, done):
                for b in range(GB):
                    last = nc.tensor.transpose(dst[:, b * T:(b + 1) * T], src[:, b, :], idf[:, :])
                last.then_inc(S[done], 1)

            def cols_of(b):
                return slice(b * T, (b + 1) * T)

            pe.wait_ge(S["pool_consts"], 1)

            def project_by_token(u, wv, done):
                for b in range(GB):
                    last = mm(M1[:, cols_of(b)], ctxg[u][:, cols_of(b)], wv[:, :], start=True, stop=True)
                last.then_inc(S[done], 1)

            def key_scores(u, c, dst, done):
                b, q = c // 4, c % 4
                for i in range(PLACES):
                    last = mm(dst[:, i * T:(i + 1) * T], Kpad[u][:, q, i, cols_of(b)], Qst[u][:, q, cols_of(b)],
                              start=True, stop=True)
                last.then_inc(S[done], 1)


            def turn(u_of_n, t, j_static):
                return j_static + 1 if t is None else t + u_of_n

            def transposed(n, free, frees, src_ready, done):
                pe.wait_ge(S[src_ready], n + 1)
                if not known(n, 1):
                    pe.wait_ge(S[free], frees)
                transposes(M0, xn, done)

            def next_normalised(n):
                pe.wait_ge(S["xn_ready"], n + 2)
                pe.wait_ge(S["k_lo"], n + 1)
                transposes(M0, xn, "xnT_ps")

            def gate_transposes(n):
                pe.wait_ge(S["n2_ready"], n + 1)
                if known(n, 1):
                    pe.wait_ge(S["m_T"], GROUPS)
                else:
                    pe.wait_ge(S["hid_ready"], n)
                transposes(M0, xn, "t2_ps")

            def gate_hidden(n):
                pe.wait_ge(S["t2_ready"], n + 1)
                if known(n, 1):
                    pe.wait_ge(S["w_rest"], W_REST)
                else:
                    pe.wait_ge(S["gt_ready"], n)
                mm(M0[0:HID, :], wg1[:, :], group(XN2T, n, W), start=True, stop=True).then_inc(S["hid_ps"], 1)

            def gate_logits(n):
                pe.wait_ge(S["hid_ready"], n + 1)
                if known(n, 1):
                    pe.wait_ge(S["moe_consts"], 2)
                else:
                    pe.wait_ge(S["lmax"], n)
                for b in range(GB):
                    last = mm((PA1 if known(n, 1) else PO1)[:, b * E:(b + 1) * E], hT[:, cols_of(b)], wg2[:, :], start=True, stop=True)
                last.then_inc(S["log_ps"], 1)

            BEHIND = 3
            LAG = 5

            def softmax_group(n, g, u, t):
                last_g = n is None
                ug = 1 - u
                base = GROUPS * 18 - 2 if last_g else (0 if known(n, 1) else n * 18 - 2)
                jn = 1 if t is None else t + 2
                jg = (1 if known(g, 1) else GROUPS // 2) if t is None else (t + 1 if u == 0 else t + 2)

                def maxima_scores(c):
                    b, q = c % 4, c // 4
                    if b == 0:
                        pe.wait_ge(STACKED[u][q], jn * PER_QUAD)
                    if not (known(n, 1) and c < 2):
                        pe.wait_ge(S["pa_free"], base + (c - 1))
                    mm(PA[c % 2][:, :], idb[:, :], maskA[:, :].unsqueeze(1).broadcast_to([T, PLACES, T]), start=True, stop=False)
                    mm(PA[c % 2][:, :], Qst[u][:, q, cols_of(b)], Kpad[u][:, q, :, cols_of(b)], start=False, stop=True)\
                        .then_inc(S["pa_ps"], 1)

                def weigh_values(c):
                    b, q = c // 4, c % 4
                    pe.wait_ge(S["e_masked"], g * 16 + (c + 1))
                    if c == 0:
                        if known(g, 1):
                            pe.wait_ge(S["prep_bo"], 1)
                        else:
                            pe.wait_ge(S["o_raw"], g)
                    for i in range(PLACES):
                        h = 4 * q + i
                        at = 32 * ((h // 3) % 4)
                        last = mm(PO[h // 12][at:at + 32, cols_of(b)], Vpad[ug][:, b, h, :], Eq[c % NE][:, i, :],
                                  start=h % 3 == 0, stop=h % 3 == 2 or h == H - 1, tile_position=(0, at))
                    last.then_inc(S["pv_done"], 1)

                def attend(c):
                    if c < 16:
                        if c == 0:
                            pe.wait_ge(S[f"m_in{ug}"], jg * 64)
                            pe.wait_ge(S["v_ready"], g + 1)
                        if not (known(g, 1) and c < 2):
                            pe.wait_ge(S["e_exp"], g * 16 + (c - 1))
                        key_scores(ug, c, PB[c % 2], "pb_ps")
                    if c >= BEHIND:
                        weigh_values(c - BEHIND)

                if n is not None:
                    pe.wait_ge(S["xnT_ready"], n + 1)
                    if known(n, 1):
                        pe.wait_ge(S["prep_q"], 1)
                    else:
                        pe.wait_ge(S["v_ready"], n)
                    mm(M1[:, :], Wq0[:, :], xnT[:, :], start=True, stop=True).then_inc(S["q_ps"], 1)
                    pe.wait_ge(S[f"ctx0_in{u}"], jn * 16)
                    if not known(n, 1):
                        pe.wait_ge(S["m_T"], n)
                    mm(M0[:, :], Wk0[:, :], ctxg[u][:, :], start=True, stop=True).then_inc(S["k_ps"], 1)

                def values():
                    pe.wait_ge(S["q_lo"], n + 1)
                    project_by_token(u, Wv0, "v_ps")

                if n is not None:
                    values()
                if known(n, 1):
                    pe.wait_ge(S["w_wo"], W_WO)
                    pe.wait_ge(S["bv_rep"], 1)
                    mm(PO1[:, 0:D], bvrep[:, :], Wo0[:, :], start=True, stop=True).then_inc(S["bo_ps"], 1)
                if g is None:
                    for c in range(16):
                        maxima_scores(c)
                    next_normalised(n)
                else:
                    for c in range(16 + max(LAG, BEHIND)):
                        if c < 16 + BEHIND:
                            attend(c)
                        if 0 <= c - LAG < 16 and n is not None:
                            maxima_scores(c - LAG)
                        if c == 11 and not known(g, 1):
                            project_out(g - 1, GROUPS if last_g else n + 1)
                        if last_g and c == 6:
                            gate_transposes(0)
                        if last_g and c == 14:
                            gate_hidden(0)
                        if last_g and c == 17:
                            pe.wait_ge(S["pa_free"], base)
                            gate_logits(0)
                        if c == 15 + LAG - 3 and n is not None:
                            next_normalised(n)
                    at = base if last_g else base + 16
                    pe.wait_ge(S["o_raw"], g + 1)
                    if known(g, 1):
                        pe.wait_ge(S["pool_consts"], 2)
                    pe.wait_ge(S["pa_free"], at - 1)
                    mm(PA0[:, :], sel0[:, :, :, :].rearrange("p a i d -> p (a i d)"), Oraw[:, 0, :], start=True, stop=True)\
                        .then_inc(S["pa_ps"], 1)
                    pe.wait_ge(S["pa_free"], at)
                    if last_g:
                        pe.wait_ge(S["lmax"], 1)
                    mm(PA1[0:64, :], sel1[:, :, :, :].rearrange("p a i d -> p (a i d)"), Oraw[:, 1, :], start=True, stop=True)\
                        .then_inc(S["pa_ps"], 1)
                if n is not None:
                    pe.wait_ge(S["m_split"], n + 1)
                    pe.wait_ge(S["xnT_ready"], n + 2)
                    for b in range(GB):
                        last = mm(M0[0:32, cols_of(b)], mparts[:, b, :, :, :].rearrange("t i r q -> t (i r q)"), idh[:, :],
                                  start=True, stop=True)
                    last.then_inc(S["m_ps"], 1)

            def project_out(g, v_ready):
                pe.wait_ge(S["o_norm"], g + 1)
                pe.wait_ge(S["v_ready"], v_ready)
                if known(g, 1):
                    pe.wait_ge(S["prep_wo"], 1)
                for b in range(GB):
                    mm(M1[:, cols_of(b)], On[:, 0, cols_of(b)], Wo0R[:, 0, :], start=True, stop=False)
                    last = mm(M1[:, cols_of(b)], On[:, 1, cols_of(b)], Wo0R[:, 1, :], start=False, stop=True)
                last.then_inc(S["y_ps"], 1)

            pe.wait_ge(S["xn_ready"], 1)
            transposes(M0, xn, "xnT_ps")
            pe.wait_ge(S["w_attn"], W_ATTN)
            attention_schedule(pe, softmax_group)
            gate_transposes(1)

            def transpose_gates(n):
                pe.wait_ge(S["gates_done"], n + 1)
                pe.wait_ge(S["t2_ready"], min(n + 2, GROUPS) if isinstance(n, int) else n + 2)
                for b in range(GB):
                    last = mm(M0[:, cols_of(b)], G3[:, b, :], idb[:, :], start=True, stop=True)
                last.then_inc(S["gt_ps"], 1)

            def mix_group(g, more, inputs):
                gates = group(GT3, g, W)

                def spread_gate(e):
                    if not (known(g, 1) and e < 4):
                        pe.wait_ge(S["xs_ready"], g * E + (e - 3))
                    mm(RING[e % 4][:, :], SELE[:, e, :], gates, start=True, stop=True).then_inc(S["bc_ps"], 1)

                pe.wait_ge(S["gt_ready"], g + 1)
                for e in range(3):
                    spread_gate(e)
                if more:
                    gate_hidden(g + 1)
                if known(g, 1):
                    pe.wait_ge(S["prep_rest"], 2)
                else:
                    transpose_mix(g - 1)
                for part in range(PARTS):
                    mm(PO0[:, :], BE[:, part, :], gates, start=part == 0, stop=False)
                for e in range(E):
                    if e + 3 < E:
                        spread_gate(e + 3)
                    if more and e == 2:
                        gate_logits(g + 1)
                    if inputs and e == 6:
                        gate_transposes(g + 2)
                    if more and e == 18:
                        transpose_gates(g + 1)
                    if not more and e == 14:
                        pe.wait_ge(S["n3_ready"], 1)
                        transposes(M0, xn, "t3_ps")
                    pe.wait_ge(S["xs_ready"], g * E + (e + 1))
                    mm(PO0[:, :], We[:, e, :], xs[e % 4], start=False, stop=e == E - 1).then_inc(S["xs_used"], 1)

            def transpose_mix(g):
                pe.wait_ge(S["y3_T"], g + 1)
                if known(g, 1):
                    pe.wait_ge(S["x1_ready"], GROUPS)
                else:
                    pe.wait_ge(S["x2_ready"], g)
                for b in range(GB):
                    last = nc.tensor.transpose(M1[:, cols_of(b)], yT[:, cols_of(b)], idf[:, :])
                last.then_inc(S["y3_tps"], 1)

            transpose_gates(0)
            pe.wait_ge(S["x1_ready"], GROUPS - 1)
            project_out(GROUPS - 1, GROUPS)
            mix_group(0, True, True)
            with pe.Fori(1, GROUPS - 2) as g:
                mix_group(g, True, True)
            mix_group(GROUPS - 2, True, False)
            mix_group(GROUPS - 1, False, False)
            transpose_mix(GROUPS - 1)
            def linear_group(n, g, u, t):
                ug = 1 - u
                jn = 1 if t is None else t + 2
                jg = (1 if known(g, 1) else GROUPS // 2) if t is None else (t + 1 if u == 0 else t + 2)
                if n is not None:
                    pe.wait_ge(S["t3_ready"], n + 1)
                    if known(n, 1):
                        pe.wait_ge(S["x2_ready"], GROUPS)
                    else:
                        pe.wait_ge(S["k3_sum"], n)
                    mm(M1[:, :], Wq1[:, :], xnT[:, :], start=True, stop=True).then_inc(S["q3_ps"], 1)
                    pe.wait_ge(S[f"ctx1_in{u}"], jn * 16)
                    mm(M0[:, :], Wv1[:, :], ctxg[u][:, :], start=True, stop=True).then_inc(S["v3_ps"], 1)
                    pe.wait_ge(S["q3_max"], n + 1)
                    project_by_token(u, Wk1, "k3_ps")

                def key_sums():
                    pe.wait_ge(S["k3_phi"], n + 1)
                    if not known(n, 2):
                        pe.wait_ge(S["p4_den"], n - 1)
                    for b in range(GB):
                        last = mm(PA[u][:, cols_of(b)], phiK[:, b, :], triT[:, :], start=True, stop=True)
                    last.then_inc(S["z3_ps"], 1)

                def next_transposed():
                    pe.wait_ge(S["n3_ready"], n + 2)
                    pe.wait_ge(S["v3_lo"], n + 1)
                    transposes(M0, xn, "t3_ps")

                if g is None:
                    key_sums()
                    next_transposed()
                    return
                for c in range(16 + BEHIND):
                    if c < 16:
                        if c == 0:
                            for q in range(QUADS):
                                pe.wait_ge(STACKED[ug][q], (GROUPS // 2 + jg) * PER_QUAD)
                            pe.wait_ge(S["k3_ready"], g + 1)
                        if not (known(g, 1) and c < 2):
                            pe.wait_ge(S["p4_cp" if c % 2 else "p4_aD"], g * 8 + c // 2)
                        key_scores(ug, c, PB[c % 2], "p4b_odd" if c % 2 else "p4b_even")
                    if c >= BEHIND:
                        m = c - BEHIND
                        b, q = m // 4, m % 4
                        pe.wait_ge(S["p4_aP" if m % 2 else "p4_aD"], g * 8 + (m // 2 + 1))
                        if m == 0:
                            if known(g, 2):
                                pe.wait_ge(S["y3_T"], GROUPS)
                            else:
                                pe.wait_ge(S["p4_o"], g - 1)
                        for i in range(PLACES):
                            last = mm(PO[ug][32 * q:32 * q + 32, cols_of(b)], Vpad[ug][:, b, 4 * q + i, :], Eq[m % NE][:, i, :],
                                      start=i == 0, stop=i == PLACES - 1, tile_position=(0, 32 * q))
                        last.then_inc(S["p4_pv"], 1)
                    if c == 13 and not known(g, 1):
                        linear_out(g - 1, GROUPS if n is None else n + 1)
                    if c == 12 and n is not None:
                        key_sums()
                    if c == 15 and n is not None:
                        next_transposed()
                    if c == 15 and n is None:
                        pe.wait_ge(S["n4_ready"], 1)
                        pe.wait_ge(S["v3_lo"], GROUPS)
                        transposes(M0, xn, "t4_ps")

            def linear_out(g, keys_read):
                pe.wait_ge(S["p4_o"], g + 1)
                pe.wait_ge(S["k3_sum"], keys_read)
                if known(g, 1):
                    pe.wait_ge(S["prep_rest"], 1)
                for b in range(GB):
                    last = mm(M1[:, cols_of(b)], On[:, 0, cols_of(b)], Wo1[:, :], start=True, stop=True)
                last.then_inc(S["p4_y"], 1)

            attention_schedule(pe, linear_group)
            def mlp_first(n):
                pe.wait_ge(S["x4_lo"], n + 1)
                for f in range(FC):
                    if not known(n, 1):
                        pe.wait_ge(S["u1_lo"], n * FC + (f + 1 - FC))
                    cols_f = slice(f * 128, (f + 1) * 128)
                    mm(RING[f][:, :], w0[:, cols_f], xh[:, :], start=True, stop=False)
                    mm(RING[f][:, :], w0[:, cols_f], xl[:, :], start=False, stop=True).then_inc(S["l1_ps"], 1)

            def mlp_second(n, chunks=range(FC)):
                pe.wait_ge(S["u0_lo"], n * FC + FC)
                for f in chunks:
                    for k in range(FC):
                        w = w1[:, k, f * 128:(f + 1) * 128]
                        mm(RING[f][:, :], w, u0h[:, k, :], start=k == 0, stop=False)
                        last = mm(RING[f][:, :], w, u0l[:, k, :], start=False, stop=k == FC - 1)
                    last.then_inc(S["l2_ps"], 1)

            def mlp_third(n):
                pe.wait_ge(S["u1_lo"], n * FC + FC)
                if known(n, 1):
                    pe.wait_ge(S["x3_ready"], GROUPS)
                else:
                    pe.wait_ge(S["out_ready"], n)
                for b in range(GB):
                    for k in range(FC):
                        mm(M1[:, cols_of(b)], u1h[:, k, cols_of(b)], w2[:, k, :], start=k == 0, stop=False)
                        last = mm(M1[:, cols_of(b)], u1l[:, k, cols_of(b)], w2[:, k, :], start=False, stop=k == FC - 1)
                last.then_inc(S["l3_ps"], 1)

            pe.wait_ge(S["p4_den"], GROUPS)
            mlp_first(0)
            pe.wait_ge(S["x3_ready"], GROUPS - 1)
            linear_out(GROUPS - 1, GROUPS)

            def mlp_group(n):
                mlp_second(n, range(FC - 1))
                transposed(n + 1, "x4_lo", n + 1, "n4_ready", "t4_ps")
                mlp_second(n, [FC - 1])
                mlp_first(n + 1)
                mlp_third(n)

            mlp_group(0)
            with pe.Fori(1, GROUPS - 1) as n:
                mlp_group(n)
            mlp_second(GROUPS - 1)
            mlp_third(GROUPS - 1)


ARRAYS = {"x": "x", "g_xattn": "g_xattn", "g_ffn": "g_ffn",
          "bq0": "L0_xattn_bq", "bk0": "L0_xattn_bk", "bv0": "L0_xattn_bv", "bo0": "L0_xattn_bo",
          "wg1": "L0_ffn_wg1", "bg1": "L0_ffn_bg1", "wg2": "L0_ffn_wg2", "bg2": "L0_ffn_bg2", "We": "L0_ffn_We", "be": "L0_ffn_be",
          "Wq1": "L1_xattn_Wq", "Wk1": "L1_xattn_Wk", "Wv1": "L1_xattn_Wv", "Wo1": "L1_xattn_Wo",
          "bq1": "L1_xattn_bq", "bk1": "L1_xattn_bk", "bv1": "L1_xattn_bv", "bo1": "L1_xattn_bo"}


def kernel(**inputs):
    from concourse import bacc
    from concourse.bass_utils import run_bass_kernel_spmd
    i = {name: np.asarray(value) for name, value in inputs.items()}
    arrays = {short: i[name] for short, name in ARRAYS.items()}
    ctx_t = np.zeros((D, (GROUPS + EXTRA) * W), np.float32)
    ctx_t[:, :GROUPS * W] = i["ctx_1024"].transpose(2, 0, 1).reshape(D, GROUPS * W)
    arrays["ctxT"] = ctx_t
    for w in "qkvo":
        arrays[f"W{w}T0"] = i[f"L0_xattn_W{w}"].T
    for k in range(3):
        arrays[f"k{k}"] = i[f"L1_ffn_k{k}"]
        arrays[f"s{k}"] = i[f"L1_ffn_s{k}"].reshape(1)
    arrays = {name: np.ascontiguousarray(value) for name, value in arrays.items()}

    nc = bacc.Bacc("TRN2", target_bir_lowering=False, num_devices=1)
    aps = {name: nc.dram_tensor(f"in_{name}", list(value.shape), mybir.dt.from_np(value.dtype), kind="ExternalInput").ap()
           for name, value in arrays.items()}
    out = nc.dram_tensor("out_x", [SEQS, T, D], F32, kind="ExternalOutput").ap()
    build(nc, aps, out)
    result = run_bass_kernel_spmd(nc, [{f"in_{name}": value for name, value in arrays.items()}], core_ids=[0])
    return result.results[0]["out_x"]
```

```python
from contextlib import ExitStack

import numpy as np

import concourse.bass as bass
from concourse import mybir

F32 = mybir.dt.float32
F16 = mybir.dt.float16
BF16 = mybir.dt.bfloat16
U8 = mybir.dt.uint8
I32 = mybir.dt.int32
ALU = mybir.AluOpType
ACT = mybir.ActivationFunctionType
AX = mybir.AxisListType

SEQS, T, D = 32, 128, 128
GB = 4
GROUPS = SEQS // GB
W = GB * T
H, HD = 16, 8
QUADS, PLACES = 4, 4
E = 20
HID = 32
FF = 512
FC = FF // 128
PARTS = 3
SPAN, SPLIT = 5, 4
SPLITS = E // SPAN * SPLIT
EPS = 1e-5
NEG = -1e30
EXTRA = 1
NE = 4
VH = 18
SCALE1 = 32.0


class Steps:

    def __init__(self, eng, sem):
        self.eng, self.sem, self.n, self.reg, self.stride = eng, sem, 0, None, 0

    def __call__(self, ins):
        self.later(ins)
        self.settle()

    def later(self, ins):
        self.n += 1
        ins.then_inc(self.sem, 1)

    def settle(self):
        self.eng.wait_ge(self.sem, self.n if self.reg is None else self.reg * self.stride + self.n)

    def enter(self, reg, stride):
        self.reg, self.stride, self.start = reg, stride, self.n

    def leave(self, trips):
        assert self.n - self.start == self.stride, (self.n - self.start, self.stride)
        self.n, self.reg = self.start + trips * self.stride, None


def build(nc, a, out):
    ctx = ExitStack()
    with ctx:
        def sb(name, shape, dt=F32):
            return ctx.enter_context(nc.sbuf_tensor(name, shape, dt))

        def bank(name):
            return ctx.enter_context(nc.psum_tensor(name, [128, W], F32))

        def sem(name):
            return ctx.enter_context(nc.semaphore(name))

        X = sb("X", [T, SEQS + GB * EXTRA, D])
        XB = sb("XB", [T, GB, D])
        stats = sb("stats", [T, GB, 6])
        mv = sb("mv", [T, GB, 2])
        veps = sb("veps", [T, GB])
        rstd = sb("rstd", [T, GB])
        xn = sb("xn", [T, GB, D])
        xnT = sb("xnT", [D, W])
        XN2T = sb("XN2T", [D, GROUPS * W])
        ctxg = [sb(f"ctxg{u}", [D, W]) for u in range(2)]
        QS = [sb(f"QS{u}", [D, 4, W], F16) for u in range(2)]
        KS = [sb(f"KS{u}", [D, 4, W], F16) for u in range(2)]
        Qst = [sb(f"Qst{u}", [128, QUADS, W], F16) for u in range(2)]
        Kpad = [sb(f"Kpad{u}", [128, QUADS, PLACES, W], F16) for u in range(2)]
        Vpad = [sb(f"Vpad{u}", [T, GB, VH, 32]) for u in range(2)]
        Eq = [sb(f"Eq{k}", [T, PLACES, T]) for k in range(NE)]
        rowmax = sb("rowmax", [T, GB, PLACES, QUADS])
        halfneg = sb("halfneg", [T, GB])
        mparts = sb("mparts", [T, GB, PLACES, 2, QUADS], F16)
        mT = [sb(f"mT{u}", [32, W], F16) for u in range(2)]
        Oraw = sb("Oraw", [128, 2, W])
        Rden = sb("Rden", [128, 2, W])
        On = sb("On", [128, 2, W])
        hT = sb("hT", [HID + 1, W])
        LOG, PRB, TMP, ONE1, ONE2 = (sb(name, [T, GB, E]) for name in ("LOG", "PRB", "TMP", "ONE1", "ONE2"))
        red = sb("red", [T, GB])
        G3 = sb("G3", [T, GB, 128], BF16)
        GT3 = sb("GT3", [128, GROUPS * W], BF16)
        xs = [Eq[k][:, :, :].rearrange("d i t -> d (i t)") for k in range(4)]
        xs_hi, xs_lo = ([tile[:, part, :] for tile in QS + KS] for part in range(2))
        We_hi = [Qst[0][:, k, :] for k in range(E // SPAN)]
        We_lo = [tile[:, 2, :] for tile in QS + KS]
        yT = sb("yT", [D, W])
        scratch = [XN2T[:, k * W:(k + 1) * W] for k in range(6)]
        zmin, zexp, zmax = ({"q": scratch[2 * k], "k": scratch[2 * k + 1]} for k in range(3))
        den = sb("den", [128, W])
        phiQ = [sb(f"phiQ{u}", [128, W]) for u in range(2)]
        phiK = sb("phiK", [T, GB, D])
        ksum = sb("ksum", [T, GB, D])
        Wq0 = sb("Wq0", [D, D]); Wk0 = sb("Wk0", [D, D]); Wv0 = sb("Wv0", [D, D]); Wo0 = sb("Wo0", [D, D])
        Wo0R = sb("Wo0R", [128, 2, D])
        Wq1 = sb("Wq1", [D, D]); Wk1 = sb("Wk1", [D, D]); Wv1 = sb("Wv1", [D, D]); Wo1 = sb("Wo1", [D, D])
        cols = sb("cols", [128, 6])
        bvrep = sb("bvrep", [D, T])
        bo0 = sb("bo0", [T, D]); bo1 = sb("bo1", [T, D]); bk1 = sb("bk1", [T, D])
        wg1 = sb("wg1", [D, HID]); bg1 = sb("bg1", [HID, 1]); wg2 = sb("wg2", [HID + 1, E])
        We = sb("We", [D, E, D])
        beR = sb("beR", [128, D])
        beres = sb("beres", [128, D])
        BE = sb("BE", [128, PARTS, D], BF16)
        k0 = sb("k0", [D, 2, FF], U8); k1 = sb("k1", [128, FC, FF], U8); k2 = sb("k2", [128, FC, D], U8)
        w0 = sb("w0", [D, FF], F16); w1 = sb("w1", [128, FC, FF], F16); w2 = sb("w2", [128, FC, D], F16)
        gates = sb("gates", [128, 4]); tg = sb("tg", [128, 4])
        sc = sb("sc", [128, 3]); sg = sb("sg", [128, 3]); fac = sb("fac", [128, 3])
        idf = sb("idf", [128, 128]); idb = sb("idb", [128, 128], BF16); idh = sb("idh", [128, 128], F16)
        maskA = sb("maskA", [T, T], BF16)
        triT = sb("triT", [T, T])
        sel0 = sb("sel0", [128, 4, 4, 8]); sel1 = sb("sel1", [128, 2, 4, 8])
        SELE = sb("SELE", [128, E, 128], BF16); expert_rows = sb("expert_rows", [128, E])
        iotaI = sb("iotaI", [T, E], I32); rank = sb("rank", [T, E])
        xh, xl = Qst[0][:, 0, :], Qst[0][:, 1, :]
        u0h, u0l, u1h, u1l = (Kpad[0][:, k, :, :] for k in range(4))

        M0, M1, PA0, PA1, PB0, PB1, PO0, PO1 = (bank(n) for n in ("M0", "M1", "PA0", "PA1", "PB0", "PB1", "PO0", "PO1"))
        PA, PB, PO = [PA0, PA1], [PB0, PB1], [PO0, PO1]
        RING = [PB0, PB1, PA0, PA1]

        S = {}
        for name in ("x_first x_rest w_attn w_rest w_wo gates_in "
                     "pool_consts expert_rows wo_clear kpad_clear kpad1_clear vpad_clear kq_const eps_const prep_q prep_wo prep_bo tanh_done bv_rep bo_ps "
                     "ctx0_in0 ctx0_in1 ctx1_in0 ctx1_in1 ln_var ln_rstd dve_step pool_step "
                     "xn_ready xnT_ps xnT_ready q_ps q_hi q_lo k_ps k_hi k_lo v_ps v_ready "
                     "pa_ps pa_free m_split m_ps m_T m_in0 m_in1 "
                     "pb_ps e_exp e_masked pv_done o_raw o_norm y_ps x1_ready xb_ready "
                     "n2_ready t2_ps t2_ready hid_ps hid_ready log_ps lmax lexp gates_done moe_consts "
                     "gt_ps gt_ready bc_ps xs_ready xs_high xs_low xs_used we_scaled we_high we_split y3_T y3_tps x2_ready prep_rest "
                     "n3_ready t3_ps t3_ready q3_ps q3_min q3_exp q3_max q3_phi q3_hi q3_lo "
                     "v3_ps v3_hi v3_lo k3_ps k3_sum k3_min k3_exp k3_max k3_phi k3_ready z3_ps vclear "
                     "p4b_even p4b_odd p4_aD p4_cp p4_aP p4_pv p4_den p4_o p4_y x3_ready p4_xb "
                     "n4_ready t4_ps x4_hi x4_lo l1_ps u0_hi u0_lo l2_ps u1_hi u1_lo l3_ps out_ready out_done").split():
            S[name] = sem(name)
        STACKED = [[sem(f"stacked{u}_quad{q}") for q in range(QUADS)] for u in range(2)]
        PER_QUAD = 16 * (1 + PLACES)

        block = ctx.enter_context(nc.Block())
        W_ATTN, W_WO, W_REST = 16 * 6, 16 * 8, 16 * 19
        LN2 = GROUPS + EXTRA
        LN3 = LN2 + GROUPS
        LN4 = LN3 + GROUPS + EXTRA
        TRIPS = (GROUPS - 2) // 2

        def known(n, least):
            return isinstance(n, int) and n < least

        def attention_schedule(eng, body, step=None, steps=0):
            body(0, None, 0, None)
            body(1, 0, 1, None)
            with eng.Fori(0, TRIPS) as t:
                if step:
                    step.enter(t, 2 * steps)
                for half in range(2):
                    body(t * 2 + (half + 2), t * 2 + (half + 1), half, t)
            if step:
                step.leave(TRIPS)
            body(None, GROUPS - 1, 0, None)

        def splits(e):
            return e // SPAN * SPLIT + min(e % SPAN, SPLIT - 1) + 1

        def column(src):
            return a[src].rearrange("(p a) -> p a", a=1)

        def group(tile, i, width=GB):
            return tile[:, i * width:(i + 1) * width] if isinstance(i, int) else tile[:, bass.ds(i * width, width)]

        @block.sync
        def _(sp):
            xg = a["x"].rearrange("b t d -> t b d")
            sp.dma_start(X[:, 0:2 * GB, :], xg[:, 0:2 * GB, :]).then_inc(S["x_first"], 16)
            sp.dma_start(ctxg[0][:, :], a["ctxT"][:, 0:W]).then_inc(S["ctx0_in0"], 16)
            sp.dma_start(ctxg[1][:, :], a["ctxT"][:, W:2 * W]).then_inc(S["ctx0_in1"], 16)
            sp.dma_start(gates[:, 0:2], a["g_xattn"].partition_broadcast(128)).then_inc(S["gates_in"], 16)
            sp.dma_start(gates[:, 2:4], a["g_ffn"].partition_broadcast(128)).then_inc(S["gates_in"], 16)
            for j, src in enumerate(("s0", "s1", "s2")):
                sp.dma_start(sc[:, j:j + 1], a[src].partition_broadcast(128)).then_inc(S["gates_in"], 16)
            sp.dma_start(Wo0[:, :], a["WoT0"]).then_inc(S["w_wo"], 16)
            sp.dma_start(bo0[:, :], a["bo0"].partition_broadcast(128)).then_inc(S["w_wo"], 16)
            sp.wait_ge(S["wo_clear"], 1)
            for c in range(6):
                rows = 3 * HD if c < 5 else HD
                sp.dma_start(Wo0R[32 * (c % 4):32 * (c % 4) + rows, c // 4, :], a["WoT0"][24 * c:24 * c + rows, :])\
                  .then_inc(S["w_wo"], 16)
            sp.dma_start(X[:, 2 * GB:SEQS, :], xg[:, 2 * GB:SEQS, :]).then_inc(S["x_rest"], 16)

            def next_ctx(n, u, v_done, arrived):
                sp.wait_ge(S[v_done], n)
                sp.dma_start(ctxg[1 - u][:, :], group(a["ctxT"], n + 1, W)).then_inc(S[f"{arrived}{1 - u}"], 16)

            def stack_q(u, q):
                sp.dma_start(Qst[u][:, q, :], QS[u][32 * q:32 * q + 32, :, :]).then_inc(STACKED[u][q], 16)

            def stack_k(u, q):
                for i in range(PLACES):
                    p = 32 * q + 8 * i
                    sp.dma_start(Kpad[u][32 * i:32 * i + 32, q, i, :], KS[u][p:p + 8, :, :]).then_inc(STACKED[u][q], 16)

            def softmax_group(n, g, u, t):
                if n is None:
                    return
                if not known(n, 1):
                    next_ctx(n, u, "v_ps", "ctx0_in")
                sp.wait_ge(S["kpad_clear" if u == 0 else "kpad1_clear"], 1)
                sp.wait_ge(S["kq_const"], 1)
                if not known(n, 2):
                    sp.wait_ge(S["pv_done"], n * 16 - 16)
                sp.wait_ge(S["q_hi"], n + 1)
                sp.wait_ge(S["q_lo"], n + 1)
                sp.wait_ge(S["k_hi"], n + 1)
                sp.wait_ge(S["k_lo"], n + 1)
                for q in range(QUADS):
                    stack_q(u, q)
                    stack_k(u, q)
                sp.wait_ge(S["m_T"], n + 1)
                for i in range(PLACES):
                    sp.dma_start(Qst[u][32 * i + 3:32 * i + 8:4, :, :], mT[u][8 * i:8 * i + 8, :])\
                      .then_inc(S[f"m_in{u}"], 16)

            attention_schedule(sp, softmax_group)

            sp.wait_ge(S["ctx0_in0"], 16 * 5)
            sp.wait_ge(S["ctx0_in1"], 16 * 4)
            sp.wait_ge(S["v_ps"], GROUPS)
            sp.dma_start(ctxg[0][:, :], a["ctxT"][:, 0:W]).then_inc(S["ctx1_in0"], 16)
            sp.dma_start(ctxg[1][:, :], a["ctxT"][:, W:2 * W]).then_inc(S["ctx1_in1"], 16)

            def linear_group(n, g, u, t):
                if n is None:
                    return
                if not known(n, 1):
                    next_ctx(n, u, "k3_ps", "ctx1_in")
                if not known(n, 2):
                    sp.wait_ge(S["p4_pv"], n * 16 - 16)
                sp.wait_ge(S["v3_hi"], n + 1)
                sp.wait_ge(S["v3_lo"], n + 1)
                for q in range(QUADS):
                    stack_k(u, q)
                sp.wait_ge(S["q3_hi"], n + 1)
                sp.wait_ge(S["q3_lo"], n + 1)
                for q in range(QUADS):
                    stack_q(u, q)

            attention_schedule(sp, linear_group)
            sp.wait_ge(S["ctx1_in0"], 16 * 5)
            og = out.rearrange("b t d -> t b d")
            with sp.Fori(0, GROUPS) as n:
                sp.wait_ge(S["out_ready"], n + 1)
                sp.dma_start(og[:, bass.ds(n * GB, GB), :], X[:, bass.ds(n * GB, GB), :]).then_inc(S["out_done"], 16)
            sp.wait_ge(S["out_done"], 16 * GROUPS)

        @block.scalar
        def _(act):
            for dst, src in ((Wq0, "WqT0"), (Wk0, "WkT0"), (Wv0, "WvT0")):
                act.dma_start(dst[:, :], a[src]).then_inc(S["w_attn"], 16)
            for j, src in enumerate(("bq0", "bk0", "bv0")):
                act.dma_start(cols[:, j:j + 1], column(src)).then_inc(S["w_attn"], 16)

            def parts_read(u, count):
                for q in range(QUADS):
                    act.wait_ge(STACKED[u][q], count)

            def normalised_t(n, count):
                act.wait_ge(S["xnT_ps"], count)
                if not known(n, 1):
                    act.wait_ge(S["q_ps"], n)
                nc.scalar.copy(xnT[:, :], M0[:, :]).then_inc(S["xnT_ready"], 1)

            def gate_input(n):
                act.wait_ge(S["t2_ps"], n + 1)
                nc.scalar.copy(group(XN2T, n, W), M0[:, :]).then_inc(S["t2_ready"], 1)

            def gate_gelu(n):
                act.wait_ge(S["hid_ps"], n + 1)
                if known(n, 1):
                    act.wait_ge(S["w_rest"], W_REST)
                else:
                    act.wait_ge(S["log_ps"], n)
                nc.scalar.activation(hT[0:HID, :], M0[0:HID, :], ACT.Gelu, bias=bg1[:, :]).then_inc(S["hid_ready"], 1)

            def gate_exp(n):
                act.wait_ge(S["lmax"], n + 1)
                nc.scalar.activation(PRB[:, :, :].rearrange("t s e -> t (s e)"), LOG[:, :, :].rearrange("t s e -> t (s e)"),
                                     ACT.Exp).then_inc(S["lexp"], 1)

            def weights_scaled(k):
                span = We[:, SPAN * k:SPAN * k + SPAN, :]
                if k == 0:
                    act.wait_ge(S["w_rest"], W_REST)
                nc.scalar.activation(span, span, ACT.Copy, scale=SCALE1).then_inc(S["we_scaled"], 1)

            def weights_high(k):
                act.wait_ge(S["we_scaled"], k + 1)
                if k == 0:
                    act.wait_ge(S["pv_done"], (GROUPS - 1) * 16)
                nc.scalar.copy(We_hi[k].rearrange("d (e n) -> d e n", e=SPLIT), We[:, SPAN * k:SPAN * k + SPLIT, :])\
                  .then_inc(S["we_high"], 1)

            def gates_by_expert(n):
                act.wait_ge(S["gt_ps"], n + 1)
                nc.scalar.copy(group(GT3, n, W), M0[:, :]).then_inc(S["gt_ready"], 1)

            def softmax_group(n, g, u, t):
                def values_by_token():
                    act.wait_ge(S["v_ps"], n + 1)
                    if known(n, 2):
                        act.wait_ge(S["vpad_clear"], 1)
                    else:
                        act.wait_ge(S["pv_done"], n * 16 - 16)
                    vin = M1[:, :].rearrange("t (b c) -> t b c", b=GB)
                    vout = Vpad[u][:, :, :, :].rearrange("t b h c -> t b (h c)")
                    for i, (lo, at) in enumerate(((0, 0), (8, 0), (8, 8))):
                        nc.scalar.copy(vout[:, :, 40 * i:40 * i + 480].rearrange("t b (c e) -> t b c e", e=96)[:, :, :, 0:HD],
                                       vin[:, :, lo:lo + 120].rearrange("t b (c e) -> t b c e", e=24)[:, :, :, at:at + HD])
                    nc.scalar.copy(Vpad[u][:, :, H - 1, 0:HD], vin[:, :, D - HD:D]).then_inc(S["v_ready"], 1)

                if n is not None:
                    act.wait_ge(S["q_ps"], n + 1)
                    if known(n, 1):
                        act.wait_ge(S["prep_q"], 1)
                    if not known(n, 2):
                        parts_read(u, (t + 1) * PER_QUAD)
                    nc.scalar.activation(QS[u][:, 0:3:2, :], M1[:, :].unsqueeze(1).broadcast_to([128, 2, W]),
                                         ACT.Identity, bias=cols[:, 5:6]).then_inc(S["q_hi"], 1)
                    act.wait_ge(S["k_ps"], n + 1)
                    nc.scalar.activation(KS[u][:, 0:2, :], M0[:, :].unsqueeze(1).broadcast_to([128, 2, W]),
                                         ACT.Identity, bias=cols[:, 1:2]).then_inc(S["k_hi"], 1)
                if n is not None:
                    values_by_token()
                if g is None:
                    act.wait_ge(S["gates_in"], 80)
                    nc.scalar.activation(tg[:, :], gates[:, :], ACT.Tanh)
                    nc.scalar.activation(sg[:, :], sc[:, :], ACT.Sign).then_inc(S["tanh_done"], 1)
                if g is not None:
                    for c in range(16):
                        act.wait_ge(S["pb_ps"], g * 16 + (c + 1))
                        if not (known(g, 1) and c < NE):
                            act.wait_ge(S["pv_done"], g * 16 + (c + 1 - NE))
                        nc.scalar.activation(Eq[c % NE][:, :, :].rearrange("s i t -> s (i t)"), PB[c % 2][:, :],
                                             ACT.Exp).then_inc(S["e_exp"], 1)
                        if n is None and c == 7:
                            gate_input(0)
                        if n is None and c == 10:
                            gate_gelu(0)
                        if n is None and c == 13:
                            gate_exp(0)
                        if n is None and c in (3, 5, 7, 11):
                            weights_scaled((3, 5, 7, 11).index(c))
                        if n is None and c in (4, 6, 8, 12):
                            weights_high((4, 6, 8, 12).index(c))
                if n is not None:
                    normalised_t(n + 1, n + 2)
                if g is not None:
                    act.wait_ge(S["pv_done"], g * 16 + 16)
                    if known(g, 1):
                        act.wait_ge(S["vpad_clear"], 1)
                    else:
                        act.wait_ge(S["o_norm"], g)
                    nc.scalar.copy(Oraw[:, 0, :], PO0[:, :])
                    nc.scalar.copy(Oraw[0:64, 1, :], PO1[0:64, :]).then_inc(S["o_raw"], 1)
                if n is not None:
                    act.wait_ge(S["m_ps"], n + 1)
                    if not known(n, 2):
                        act.wait_ge(S[f"m_in{u}"], (t + 1) * 64)
                    nc.scalar.copy(mT[u][:, :], M0[0:32, :]).then_inc(S["m_T"], 1)
                if known(g, 1):
                    act.wait_ge(S["expert_rows"], 1)
                    nc.scalar.copy(SELE[:, :, :], expert_rows[:, :].unsqueeze(2).broadcast_to([128, E, 128]))\
                      .then_inc(S["moe_consts"], 1)

            normalised_t(0, 1)
            attention_schedule(act, softmax_group)
            def linear_t(n, count):
                act.wait_ge(S["t3_ps"], count)
                if not known(n, 1):
                    act.wait_ge(S["q3_ps"], n)
                nc.scalar.copy(xnT[:, :], M0[:, :]).then_inc(S["t3_ready"], 1)

            def inputs_high(g, e):
                if e % SPAN < SPLIT:
                    act.wait_ge(S["xs_ready"], g * E + (e + 1))
                    if not (known(g, 1) and e < SPAN):
                        act.wait_ge(S["xs_used"], g * E + (e + 1 - SPAN))
                    nc.scalar.copy(xs_hi[e % SPAN], xs[e % 4]).then_inc(S["xs_high"], 1)

            def mix_group(g, gates, inputs):
                for e in range(2, E):
                    inputs_high(g, e)
                    if gates and e == 3:
                        gate_exp(g + 1)
                    if inputs and e == 8:
                        gate_input(g + 2)
                    if inputs and e == 12:
                        gate_gelu(g + 2)
                    if gates and e == 17:
                        gates_by_expert(g + 1)
                    if not gates and e == 17:
                        linear_t(0, 1)
                if gates:
                    for e in range(2):
                        inputs_high(g + 1, e)
                act.wait_ge(S["xs_used"], g * E + E)
                if not known(g, 1):
                    act.wait_ge(S["y3_tps"], g)
                nc.scalar.activation(yT[:, :], PO0[:, :], ACT.Copy, scale=1 / (SCALE1 * SCALE1)).then_inc(S["y3_T"], 1)

            gate_input(1)
            gates_by_expert(0)
            gate_gelu(1)
            for e in range(2):
                inputs_high(0, e)
            mix_group(0, True, True)
            with act.Fori(1, GROUPS - 2) as g:
                mix_group(g, True, True)
            mix_group(GROUPS - 2, True, False)
            mix_group(GROUPS - 1, False, False)
            def linear_group(n, g, u, t):
                def q_hi():
                    act.wait_ge(S["q3_phi"], n + 1)
                    nc.scalar.activation(QS[u][:, 0:3:2, :], phiQ[u][:, :].unsqueeze(1).broadcast_to([128, 2, W]), ACT.Copy,
                                         scale=SCALE1).then_inc(S["q3_hi"], 1)

                def k_exp():
                    act.wait_ge(S["k3_min"], n + 1)
                    if not known(n, 1):
                        act.wait_ge(S["k3_phi"], n)
                    nc.scalar.activation(zmax["k"], ksum[:, :, :].rearrange("t b d -> t (b d)"), ACT.Relu)\
                      .then_inc(S["k3_max"], 1)
                    nc.scalar.activation(zexp["k"], zmin["k"], ACT.Exp).then_inc(S["k3_exp"], 1)

                def place_keys():
                    act.wait_ge(S["k3_phi"], n + 1)
                    if known(n, 2):
                        act.wait_ge(S["vclear"], 1)
                    else:
                        act.wait_ge(S["p4_pv"], n * 16 - 16)
                    vout = Vpad[u][:, :, :, :].rearrange("t b h c -> t b (h c)")
                    for i in range(PLACES):
                        at = 40 * i
                        last = nc.scalar.copy(
                            vout[:, :, 0:4 * D].rearrange("t b (q e) -> t b q e", e=D)[:, :, :, at:at + HD],
                            phiK[:, :, :].rearrange("t b (q e) -> t b q e", e=32)[:, :, :, 8 * i:8 * i + HD])
                    last.then_inc(S["k3_ready"], 1)

                if n is not None:
                    act.wait_ge(S["q3_min"], n + 1)
                    if not known(n, 1):
                        act.wait_ge(S["q3_phi"], n)
                    nc.scalar.activation(zmax["q"], M1[:, :], ACT.Relu, bias=cols[:, 3:4]).then_inc(S["q3_max"], 1)
                    act.wait_ge(S["v3_ps"], n + 1)
                    parts_read(u, (GROUPS // 2 + (0 if t is None else t + 1)) * PER_QUAD)
                    nc.scalar.activation(KS[u][:, 0:2, :], M0[:, :].unsqueeze(1).broadcast_to([128, 2, W]),
                                         ACT.Identity, bias=cols[:, 4:5]).then_inc(S["v3_hi"], 1)
                    nc.scalar.activation(zexp["q"], zmin["q"], ACT.Exp).then_inc(S["q3_exp"], 1)
                if g is not None:
                    for c in range(16):
                        if c == 4 and n is not None:
                            q_hi()
                        if c == 4 and n is not None:
                            k_exp()
                        if c == 10 and n is not None:
                            place_keys()
                        if c % 2 == 1:
                            act.wait_ge(S["p4b_odd"], g * 8 + (c // 2 + 1))
                            if not (known(g, 1) and c < NE):
                                act.wait_ge(S["p4_pv"], g * 16 + (c + 1 - NE))
                            nc.scalar.copy(Eq[c % NE][:, :, :].rearrange("s i t -> s (i t)"), PB1[:, :])\
                              .then_inc(S["p4_cp"], 1)
                else:
                    q_hi()
                    k_exp()
                    place_keys()
                if n is not None:
                    linear_t(n + 1, n + 2)

            attention_schedule(act, linear_group)
            def x_hi(n):
                act.wait_ge(S["t4_ps"], n + 1)
                nc.scalar.copy(xh[:, :], M0[:, :]).then_inc(S["x4_hi"], 1)

            def relu_hi(dst, ready, done, n, chunks=range(FC)):
                for f in chunks:
                    act.wait_ge(S[ready], n * FC + (f + 1))
                    nc.scalar.activation(dst[:, f, :], RING[f][:, :], ACT.Relu).then_inc(S[done], 1)

            x_hi(0)
            relu_hi(u0h, "l1_ps", "u0_hi", 0)
            with act.Fori(0, GROUPS - 1) as n:
                relu_hi(u1h, "l2_ps", "u1_hi", n, range(FC - 1))
                x_hi(n + 1)
                relu_hi(u1h, "l2_ps", "u1_hi", n, [FC - 1])
                relu_hi(u0h, "l1_ps", "u0_hi", n + 1)
            relu_hi(u1h, "l2_ps", "u1_hi", GROUPS - 1)

        @block.gpsimd
        def _(pool):
            g_ = nc.gpsimd
            step = Steps(pool, S["pool_step"])
            g_.memset(Wo0R[:, :, :], 0.0).then_inc(S["wo_clear"], 1)
            g_.memset(idf[:, :], 0.0)
            g_.memset(maskA[:, :], 0.0)
            step(g_.memset(triT[:, :], 1.0))
            step(g_.affine_select(out=idf[:, :], in_=idf[:, :], compare_op=ALU.not_equal, fill=1.0, base=0,
                                  pattern=[[-1, 128]], channel_multiplier=1))
            g_.affine_select(out=maskA[:, :], in_=maskA[:, :], compare_op=ALU.is_ge, fill=NEG, base=0,
                             pattern=[[-1, T]], channel_multiplier=1)
            g_.affine_select(out=triT[:, :], in_=triT[:, :], compare_op=ALU.is_ge, fill=0.0, base=0,
                             pattern=[[1, T]], channel_multiplier=-1)
            g_.tensor_copy(idb[:, :], idf[:, :])
            g_.tensor_copy(idh[:, :], idf[:, :]).then_inc(S["pool_consts"], 1)

            def mask_causal(e):
                last_query = slice(T - 1, T)
                g_.tensor_tensor(e[:, :, last_query], e[:, :, last_query],
                                 triT[:, last_query].unsqueeze(1).broadcast_to([T, PLACES, 1]), ALU.mult)
                return g_.affine_select(out=e[:, :, 0:T - 1], in_=e[:, :, 0:T - 1], compare_op=ALU.is_ge, fill=0.0, base=0,
                                        pattern=[[0, PLACES], [1, T - 1]], channel_multiplier=-1)

            def power(i):
                pool.wait_ge(S["ln_var"], i + 1)
                g_.tensor_tensor(rstd[:, :], veps[:, :], halfneg[:, :], ALU.pow).then_inc(S["ln_rstd"], 1)

            pool.wait_ge(S["eps_const"], 1)
            power(0)
            for u in range(2):
                g_.memset(QS[u][:, 3, :], 0.0)
                last = g_.memset(KS[u][:, 3, :], 1.0)
            last.then_inc(S["kq_const"], 1)
            g_.memset(Vpad[0][:, :, :, :], 0.0)
            step(g_.memset(Vpad[1][:, :, :, :], 0.0))
            for u in range(2):
                flat = Vpad[u][:, :, :, :].rearrange("t b h c -> t b (h c)").rearrange("t b (c e) -> t b c e", e=96)
                for i in range(3):
                    g_.memset(flat[:, :, 0:6 if i == 0 else 5, 33 * i + 24:33 * i + 25], 1.0)
            g_.memset(Oraw[:, 1, :], 0.0)
            g_.memset(On[:, 1, :], 0.0).then_inc(S["vpad_clear"], 1)

            g_.memset(sel0[:, :, :, :], 0.0)
            step(g_.memset(sel1[:, :, :, :], 0.0))

            def pick(dst, base, pattern):
                step(g_.affine_select(out=dst, in_=dst, compare_op=ALU.not_equal, fill=1.0, base=base,
                                      pattern=pattern, channel_multiplier=1))

            pick(sel0[:, :, 0:3, :], -24, [[-32, 4], [-1, 3], [0, 8]])
            pick(sel0[:, :, 3, :], -24, [[-32, 4], [0, 8]])
            pick(sel1[:, 0, 0:3, :], -24, [[-1, 3], [0, 8]])
            pick(sel1[:, 0, 3, :], -24, [[0, 8]])
            g_.affine_select(out=sel1[:, 1, :, :], in_=sel1[:, 1, :, :], compare_op=ALU.not_equal, fill=1.0, base=-56,
                             pattern=[[0, 4], [0, 8]], channel_multiplier=1).then_inc(S["pool_consts"], 1)

            def xb_add(bias, g, used, ready):
                if not known(g, 1):
                    pool.wait_ge(S[used], g)
                g_.tensor_tensor(XB[:, :, :], group(X, g), bias[:, :].unsqueeze(1).broadcast_to([T, GB, D]), ALU.add)\
                  .then_inc(S[ready], 1)

            def mixture_constants():
                step(g_.memset(G3[:, :, :].rearrange("t s c -> t (s c)"), 0.0))
                step(g_.memset(hT[HID:HID + 1, :], 1.0))
                step(g_.tensor_tensor(expert_rows[:, :], idf[:, 0:E], idf[:, 32:32 + E], ALU.add))
                g_.tensor_tensor(expert_rows[:, :], expert_rows[:, :], idf[:, 64:64 + E], ALU.add).then_inc(S["expert_rows"], 1)
                step(g_.iota(iotaI[:, :], [[-1, E]], base=E, channel_multiplier=0))
                g_.tensor_copy(rank[:, :], iotaI[:, :]).then_inc(S["moe_consts"], 1)

            def weights_low(k):
                if k == 0:
                    for q in range(QUADS):
                        pool.wait_ge(STACKED[0][q], GROUPS // 2 * PER_QUAD)
                        pool.wait_ge(STACKED[1][q], GROUPS // 2 * PER_QUAD)
                pool.wait_ge(S["we_high"], k + 1)
                g_.tensor_tensor(We_lo[k].rearrange("d (e n) -> d e n", e=SPLIT), We[:, SPAN * k:SPAN * k + SPLIT, :],
                                 We_hi[k].rearrange("d (e n) -> d e n", e=SPLIT), ALU.subtract).then_inc(S["we_split"], 1)

            rest = []

            def load(dst, src):
                rest.append(pool.dma_start(dst, src).then_inc(S["w_rest"], 16))

            def load_small():
                for dst, src in ((Wq1, "Wq1"), (Wk1, "Wk1"), (Wv1, "Wv1"), (Wo1, "Wo1"), (wg1, "wg1")):
                    load(dst[:, :], a[src])
                for dst, src in ((bg1, "bg1"), (cols[:, 3:4], "bq1"), (cols[:, 4:5], "bv1")):
                    load(dst[:, :], column(src))
                load(wg2[0:HID, :], a["wg2"][:, 0:E])
                load(wg2[HID:HID + 1, :], a["bg2"].rearrange("(a n) -> a n", a=1)[:, 0:E])

            def load_large():
                pool.wait_ge(S["prep_wo"], 1)
                for part in range(PARTS):
                    load(beR[32 * part:32 * part + E, :], a["be"])
                load(bo1[:, :], a["bo1"].partition_broadcast(128))
                load(bk1[:, :], a["bk1"].partition_broadcast(128))
                load(k0[:, :, :], a["k0"].rearrange("(c p) n -> p c n", p=128))
                load(k1[:, :, :], a["k1"].rearrange("(c p) n -> p c n", p=128))
                load(k2[:, :, :], a["k2"].rearrange("(c p) n -> p c n", p=128))
                load(We[:, :, :], a["We"].rearrange("e d n -> d e n"))
                assert 16 * len(rest) == W_REST

            def softmax_group(n, g, u, t):
                if n is not None:
                    power(n + 1)
                if g is None:
                    mixture_constants()
                    load_small()
                if known(g, 1):
                    pool.wait_ge(S["prep_bo"], 1)
                elif g is not None:
                    xb_add(bo0, g - 1, "x1_ready", "xb_ready")
                if g is not None:
                    for c in range(16):
                        if n is None and c in (4, 8):
                            power(LN2 + c // 4 - 1)
                        pool.wait_ge(S["e_exp"], g * 16 + (c + 1))
                        mask_causal(Eq[c % NE]).then_inc(S["e_masked"], 1)
                        if n is None and c in (6, 8, 10, 14):
                            weights_low((6, 8, 10, 14).index(c))
                if known(g, 1):
                    load_large()

            attention_schedule(pool, softmax_group)
            xb_add(bo0, GROUPS - 1, "x1_ready", "xb_ready")
            def mix_group(g, layer_norm=None, at=0):
                for e in range(E):
                    if layer_norm is not None and e == at:
                        power(layer_norm)
                    if e % SPAN < SPLIT:
                        pool.wait_ge(S["xs_high"], g * SPLITS + splits(e))
                        g_.tensor_tensor(xs_lo[e % SPAN], xs[e % 4], xs_hi[e % SPAN], ALU.subtract).then_inc(S["xs_low"], 1)

            mix_group(0, LN2 + 2, 2)
            with pool.Fori(1, GROUPS - 2) as g:
                mix_group(g, g + (LN2 + 2), 2)
            mix_group(GROUPS - 2)
            mix_group(GROUPS - 1, LN3, 6)

            def linear_group(n, g, u, t):
                def phi_q():
                    pool.wait_ge(S["q3_exp"], n + 1)
                    pool.wait_ge(S["q3_max"], n + 1)
                    if not known(n, 2):
                        pool.wait_ge(S["p4_den"], n - 1)
                    g_.tensor_tensor(phiQ[u][:, :], zmax["q"], zexp["q"], ALU.add).then_inc(S["q3_phi"], 1)

                def phi_k():
                    pool.wait_ge(S["k3_exp"], n + 1)
                    pool.wait_ge(S["k3_max"], n + 1)
                    if not known(n, 1):
                        pool.wait_ge(S["k3_ready"], n)
                        pool.wait_ge(S["z3_ps"], n)
                    g_.tensor_tensor(phiK[:, :, :].rearrange("t b d -> t (b d)"), zmax["k"], zexp["k"], ALU.add)\
                      .then_inc(S["k3_phi"], 1)

                if n is not None:
                    power(n + (LN3 + 1))
                    phi_q()
                if g is None:
                    phi_k()
                if g is not None:
                    for c in range(1, 16, 2):
                        if c == 5 and n is not None:
                            phi_k()
                        if c == 7 and not known(g, 1):
                            xb_add(bo1, g - 1, "x3_ready", "p4_xb")
                        if c == 7 and n is None:
                            power(LN4)
                        pool.wait_ge(S["p4_cp"], g * 8 + (c // 2 + 1))
                        mask_causal(Eq[c % NE]).then_inc(S["p4_aP"], 1)

            pool.wait_ge(S["prep_rest"], 1)
            attention_schedule(pool, linear_group)
            xb_add(bo1, GROUPS - 1, "x3_ready", "p4_xb")
            with pool.Fori(LN4 + 1, LN4 + GROUPS) as n:
                power(n)

        @block.vector
        def _(dve):
            v = nc.vector
            step = Steps(dve, S["dve_step"])

            def ln_stats(i):
                src = group(X, i)
                for b in range(GB):
                    last = v.bn_stats(stats[:, b, :], src[:, b, :])
                step(last)
                v.memset(veps[:, :], EPS)
                for b in range(GB):
                    last = v.bn_aggr(mv[:, b, :], stats[:, b, :])
                step(last)
                v.tensor_tensor(veps[:, :], veps[:, :], mv[:, :, 1], ALU.add).then_inc(S["ln_var"], 1)

            def ln_norm(i, count, read, reads, ready):
                dve.wait_ge(S["ln_rstd"], count)
                if reads is not None:
                    dve.wait_ge(S[read], reads)
                src = group(X, i)
                for b in range(GB):
                    last = v.tensor_scalar(xn[:, b, :], src[:, b, :], mv[:, b, 0:1], rstd[:, b:b + 1],
                                           ALU.subtract, ALU.mult)
                last.then_inc(S[ready], 1)

            v.memset(halfneg[:, :], -0.5).then_inc(S["eps_const"], 1)
            dve.wait_ge(S["x_first"], 16)
            ln_stats(0)
            ln_norm(0, 1, None, None, "xn_ready")
            dve.wait_ge(S["w_attn"], W_ATTN)
            s = float(1.0 / np.sqrt(np.float32(HD)))
            v.tensor_scalar_mul(Wq0[:, :], Wq0[:, :], s)
            v.tensor_scalar_mul(cols[:, 5:6], cols[:, 0:1], s).then_inc(S["prep_q"], 1)
            v.tensor_copy(bvrep[:, :], cols[:, 2:3].broadcast_to([D, T])).then_inc(S["bv_rep"], 1)
            v.memset(Kpad[0][:, :, :, :].rearrange("p q i n -> p (q i n)").bitcast(F32), 0.0).then_inc(S["kpad_clear"], 1)

            def prepare_output():
                v.memset(Kpad[1][:, :, :, :].rearrange("p q i n -> p (q i n)").bitcast(F32), 0.0).then_inc(S["kpad1_clear"], 1)
                v.memset(X[:, SEQS:SEQS + GB, :], 0.0)
                v.memset(beR[:, :], 0.0)
                dve.wait_ge(S["tanh_done"], 1)
                dve.wait_ge(S["w_wo"], W_WO)
                v.tensor_scalar_mul(Wo0R[:, :, :], Wo0R[:, :, :], tg[:, 0:1]).then_inc(S["prep_wo"], 1)
                dve.wait_ge(S["bo_ps"], 1)
                step(v.tensor_tensor(bo0[:, :], bo0[:, :], PO1[:, 0:D], ALU.add))
                v.tensor_scalar_mul(bo0[:, :], bo0[:, :], tg[:, 0:1]).then_inc(S["prep_bo"], 1)

            def prepare_rest():
                dve.wait_ge(S["w_rest"], W_REST)
                v.tensor_scalar_mul(Wo1[:, :], Wo1[:, :], tg[:, 1:2])
                v.tensor_scalar_mul(bo1[:, :], bo1[:, :], tg[:, 1:2]).then_inc(S["prep_rest"], 1)
                v.tensor_scalar_mul(sg[:, 2:3], sg[:, 0:1], 2.0)
                v.tensor_scalar_mul(fac[:, 2:3], sg[:, 1:2], 0.125)
                step(v.tensor_scalar_mul(fac[:, 1:2], sg[:, 1:2], 0.25))
                step(v.tensor_tensor(w0[:, :], k0[:, 0, :], k0[:, 1, :], ALU.subtract))
                v.tensor_scalar_mul(w0[:, :], w0[:, :], sg[:, 2:3])
                v.tensor_scalar(w1[:, :, :], k1[:, :, :], fac[:, 1:2], fac[:, 2:3], ALU.mult, ALU.subtract)
                v.tensor_scalar(w2[:, :, :], k2[:, :, :], 2.0, -1.0, ALU.mult, ALU.add)
                step(v.tensor_tensor(sc[:, 0:2], sc[:, 0:2], sg[:, 0:2], ALU.mult))
                step(v.tensor_tensor(fac[:, 0:1], sc[:, 0:1], sc[:, 1:2], ALU.mult))
                step(v.tensor_tensor(fac[:, 0:1], fac[:, 0:1], sc[:, 2:3], ALU.mult))
                step(v.tensor_scalar(fac[:, 0:1], fac[:, 0:1], tg[:, 3:4], 32.0, ALU.mult, ALU.mult))
                step(v.tensor_scalar_mul(beR[:, :], beR[:, :], SCALE1))
                step(v.tensor_copy(BE[:, 0, :], beR[:, :]))
                step(v.tensor_tensor(beres[:, :], beR[:, :], BE[:, 0, :], ALU.subtract))
                step(v.tensor_copy(BE[:, 1, :], beres[:, :]))
                step(v.tensor_tensor(beres[:, :], beres[:, :], BE[:, 1, :], ALU.subtract))
                v.tensor_copy(BE[:, 2, :], beres[:, :]).then_inc(S["prep_rest"], 1)

            def normalise(g, earlier=0):
                at = g * 18 + (32 + earlier)
                dve.wait_ge(S["pa_ps"], at + 1)
                v.reciprocal(Rden[:, 0, :], PA0[:, :]).then_inc(S["pa_free"], 1)
                dve.wait_ge(S["pa_ps"], at + 2)
                v.reciprocal(Rden[0:64, 1, :], PA1[0:64, :]).then_inc(S["pa_free"], 1)
                dve.wait_ge(S["pa_free"], at + 2)
                if not known(g, 1):
                    dve.wait_ge(S["y_ps"], g)
                v.tensor_tensor(On[:, 0, :], Oraw[:, 0, :], Rden[:, 0, :], ALU.mult)
                v.tensor_tensor(On[0:64, 1, :], Oraw[0:64, 1, :], Rden[0:64, 1, :], ALU.mult).then_inc(S["o_norm"], 1)

            def softmax_group(n, g, u, t):
                if n is not None:
                    base = 0 if known(n, 1) else n * 18 - 2
                    if known(n, 2) and n == 1:
                        dve.wait_ge(S["x_rest"], 16)
                    ln_stats(n + 1)
                    dve.wait_ge(S["q_hi"], n + 1)
                    v.scalar_tensor_tensor(QS[u][:, 1, :], M1[:, :], cols[:, 5:6], QS[u][:, 0, :], ALU.add, ALU.subtract)\
                     .then_inc(S["q_lo"], 1)
                    dve.wait_ge(S["k_hi"], n + 1)
                    v.scalar_tensor_tensor(KS[u][:, 2, :], M0[:, :], cols[:, 1:2], KS[u][:, 0, :], ALU.add, ALU.subtract)\
                     .then_inc(S["k_lo"], 1)
                    if known(n, 1):
                        prepare_output()
                if g is not None and not known(g, 1):
                    normalise(g - 1)
                if n is None:
                    ln_stats(0)
                    ln_norm(0, LN2 + 1, None, None, "n2_ready")
                    ln_stats(1)
                    ln_norm(1, LN2 + 2, "t2_ps", 1, "n2_ready")
                    step(v.tensor_scalar_mul(tg[:, 2:3], tg[:, 2:3], SCALE1))
                    dve.wait_ge(S["moe_consts"], 2)
                    for k in range(LAST_GATE_STAGE + 1):
                        gate_stage(0, k)
                    prepare_rest()
                    add_y(g - 1)
                else:
                    for c in range(16):
                        if c == 12 and g is not None and not known(g, 1):
                            add_y(g - 1)
                        if c == 4:
                            ln_norm(n + 1, n + 2, "xnT_ps", n + 1, "xn_ready")
                        dve.wait_ge(S["pa_ps"], base + (c + 1))
                        v.reduce_max(rowmax[:, c % 4, :, c // 4], PA[c % 2][:, :].rearrange("t (i s) -> t i s", i=PLACES),
                                     AX.X).then_inc(S["pa_free"], 1)
                    dve.wait_ge(S["pa_free"], base + 16)
                    if not known(n, 1):
                        dve.wait_ge(S["m_ps"], n)
                    mx = rowmax[:, :, :, :].rearrange("t b i q -> t (b i) q")
                    mp = mparts[:, :, :, :, :].rearrange("t b i r q -> t (b i) r q")
                    step(v.tensor_scalar_mul(mp[:, :, 0, :], mx, -1.0))
                    v.scalar_tensor_tensor(mp[:, :, 1, :], mx, -1.0, mp[:, :, 0, :], ALU.mult, ALU.subtract)\
                     .then_inc(S["m_split"], 1)

            def add_y(g):
                dve.wait_ge(S["xb_ready"], g + 1)
                dve.wait_ge(S["y_ps"], g + 1)
                v.tensor_tensor(group(X, g).rearrange("t b d -> t (b d)"), XB[:, :, :].rearrange("t b d -> t (b d)"),
                                M1[:, :], ALU.add).then_inc(S["x1_ready"], 1)

            def over(x):
                return x[:, :].unsqueeze(2).broadcast_to([T, GB, E])

            ranks = rank[:, :].unsqueeze(1).broadcast_to([T, GB, E])
            flat = "t s e -> t (s e)"

            def mark_max(one, values):
                step(v.tensor_tensor(one[:, :, :], values[:, :, :], over(red), ALU.is_equal))
                step.later(v.tensor_tensor(one[:, :, :], one[:, :, :], ranks, ALU.mult))

            def mark_first(one):
                step(v.reduce_max(red[:, :], one[:, :, :], AX.X))
                step.later(v.tensor_tensor(one[:, :, :], ranks, over(red), ALU.is_equal))

            part = [G3[:, :, 32 * r:32 * r + E] for r in range(PARTS)]
            LAST_GATE_STAGE = 17

            def gate_stage(n, k):
                if k in (6, *range(9, LAST_GATE_STAGE + 1)):
                    step.settle()
                if k == 5:
                    dve.wait_ge(S["log_ps"], n + 1)
                    step.later(v.reduce_max(red[:, :], logits(n), AX.X))
                elif k == 6:
                    v.tensor_tensor(LOG[:, :, :], logits(n), over(red), ALU.subtract).then_inc(S["lmax"], 1)
                elif k == 8:
                    dve.wait_ge(S["lexp"], n + 1)
                    step(v.reduce_sum(red[:, :], PRB[:, :, :], AX.X))
                    step.later(v.reciprocal(red[:, :], red[:, :]))
                elif k == 9:
                    step(v.tensor_tensor(PRB[:, :, :], PRB[:, :, :], over(red), ALU.mult))
                    step.later(v.reduce_max(red[:, :], PRB[:, :, :], AX.X))
                elif k == 10:
                    mark_max(ONE1, PRB)
                elif k == 11:
                    mark_first(ONE1)
                elif k == 12:
                    step(v.scalar_tensor_tensor(TMP[:, :, :].rearrange(flat), ONE1[:, :, :].rearrange(flat), -2.0,
                                                PRB[:, :, :].rearrange(flat), ALU.mult, ALU.add))
                    step.later(v.reduce_max(red[:, :], TMP[:, :, :], AX.X))
                elif k == 13:
                    mark_max(ONE2, TMP)
                elif k == 14:
                    mark_first(ONE2)
                elif k == 15:
                    step(v.tensor_tensor(ONE1[:, :, :], ONE1[:, :, :], ONE2[:, :, :], ALU.add))
                    step.later(v.scalar_tensor_tensor(PRB[:, :, :].rearrange(flat), PRB[:, :, :].rearrange(flat), tg[:, 2:3],
                                                      ONE1[:, :, :].rearrange(flat), ALU.mult, ALU.mult))
                elif k == 16:
                    if not known(n, 1):
                        dve.wait_ge(S["gt_ps"], n)
                    step(v.tensor_copy(part[0], PRB[:, :, :]))
                    step.later(v.tensor_tensor(TMP[:, :, :], PRB[:, :, :], part[0], ALU.subtract))
                elif k == LAST_GATE_STAGE:
                    step(v.tensor_copy(part[1], TMP[:, :, :]))
                    step(v.tensor_tensor(TMP[:, :, :], TMP[:, :, :], part[1], ALU.subtract))
                    v.tensor_copy(part[2], TMP[:, :, :]).then_inc(S["gates_done"], 1)

            def logits(n):
                return (PA1 if known(n, 1) else PO1)[:, 0:GB * E].rearrange("t (b e) -> t b e", b=GB)

            GATE_STEPS = 21

            attention_schedule(dve, softmax_group, step, 3)
            def add_mix(g):
                dve.wait_ge(S["y3_tps"], g + 1)
                x = group(X, g).rearrange("t b d -> t (b d)")
                v.tensor_tensor(x, x, M1[:, :], ALU.add).then_inc(S["x2_ready"], 1)

            def mix_group(g, gates, inputs):
                for e in range(E):
                    dve.wait_ge(S["bc_ps"], g * E + (e + 1))
                    v.tensor_tensor(xs[e % 4], group(XN2T, g, W), RING[e % 4][:, :], ALU.mult)\
                     .then_inc(S["xs_ready"], 1)
                    if e == 1 and inputs:
                        ln_stats(g + 2)
                    if e == 4 and known(g, 1):
                        add_y(GROUPS - 1)
                    if e == 3 and not known(g, 1):
                        add_mix(g - 1)
                    if e == 4 and inputs:
                        ln_norm(g + 2, g + (LN2 + 3), "t2_ps", g + 2, "n2_ready")
                    if not gates:
                        if e == 5:
                            ln_stats(0)
                        if e == 9:
                            ln_norm(0, LN3 + 1, None, None, "n3_ready")
                    if not inputs and not gates and e >= E - 2 * GB:
                        u, b = divmod(e - (E - 2 * GB), GB)
                        last = v.memset(Vpad[u][:, b, :, :], 0.0)
                        if e == E - 1:
                            last.then_inc(S["vclear"], 1)
                    if gates and e < 2:
                        gate_stage(g + 1, e + 5)
                    if gates and 5 <= e <= LAST_GATE_STAGE - 3:
                        gate_stage(g + 1, e + 3)

            normalise(GROUPS - 1, -16)
            mix_group(0, True, True)
            with dve.Fori(1, GROUPS - 2) as g:
                step.enter(g - 1, 2 + GATE_STEPS)
                mix_group(g, True, True)
            step.leave(GROUPS - 3)
            mix_group(GROUPS - 2, True, False)
            mix_group(GROUPS - 1, False, False)
            add_mix(GROUPS - 1)
            def x_lo(n):
                dve.wait_ge(S["x4_hi"], n + 1)
                v.tensor_tensor(xl[:, :], M0[:, :], xh[:, :], ALU.subtract).then_inc(S["x4_lo"], 1)

            def add_y4(g):
                dve.wait_ge(S["p4_xb"], g + 1)
                dve.wait_ge(S["p4_y"], g + 1)
                v.tensor_tensor(group(X, g).rearrange("t b d -> t (b d)"), XB[:, :, :].rearrange("t b d -> t (b d)"),
                                M1[:, :], ALU.add).then_inc(S["x3_ready"], 1)

            def denominators(g, u):
                dve.wait_ge(S["z3_ps"], g + 1)
                v.tensor_tensor(den[:, :], phiQ[u][:, :], PA[u][:, :], ALU.mult).then_inc(S["p4_den"], 1)
                dve.wait_ge(S["p4_den"], g + 1)
                step(v.tensor_scalar(den[:, :], den[:, :], 1e-6, SCALE1, ALU.add, ALU.mult))

            def invert(lo, hi):
                step(v.reciprocal(den[:, lo * T:hi * T], den[:, lo * T:hi * T]))

            def normalise4(g, u):
                dve.wait_ge(S["p4_pv"], g * 16 + 16)
                if not known(g, 1):
                    dve.wait_ge(S["p4_y"], g)
                v.tensor_tensor(On[:, 0, :], den[:, :], PO[u][:, :], ALU.mult).then_inc(S["p4_o"], 1)

            def linear_group(n, g, u, t):
                before = g is not None and not known(g, 1)
                if before:
                    denominators(g - 1, u)
                if n is not None:
                    ln_stats(n + 1)
                    dve.wait_ge(S["q3_ps"], n + 1)
                    if not known(n, 1):
                        dve.wait_ge(S["q3_exp"], n)
                    v.tensor_scalar(zmin["q"], M1[:, :], cols[:, 3:4], 0.0, ALU.add, ALU.min).then_inc(S["q3_min"], 1)
                    dve.wait_ge(S["v3_hi"], n + 1)
                    v.scalar_tensor_tensor(KS[u][:, 2, :], M0[:, :], cols[:, 4:5], KS[u][:, 0, :], ALU.add, ALU.subtract)\
                     .then_inc(S["v3_lo"], 1)
                    dve.wait_ge(S["k3_ps"], n + 1)
                    if not known(n, 1):
                        dve.wait_ge(S["k3_max"], n)
                    v.tensor_tensor(ksum[:, :, :], M1[:, :].rearrange("t (b d) -> t b d", b=GB),
                                    bk1[:, :].unsqueeze(1).broadcast_to([T, GB, D]), ALU.add).then_inc(S["k3_sum"], 1)
                for c in range(16):
                    if g is not None and c % 2 == 0:
                        dve.wait_ge(S["p4b_even"], g * 8 + (c // 2 + 1))
                        if not (known(g, 1) and c < NE):
                            dve.wait_ge(S["p4_pv"], g * 16 + (c + 1 - NE))
                        v.tensor_tensor(Eq[c % NE][:, :, :], PB0[:, :].rearrange("s (i t) -> s i t", i=PLACES),
                                        triT[:, :].unsqueeze(1).broadcast_to([T, PLACES, T]), ALU.mult)\
                         .then_inc(S["p4_aD"], 1)
                    if c == 2 and n is not None:
                        dve.wait_ge(S["k3_sum"], n + 1)
                        if not known(n, 1):
                            dve.wait_ge(S["k3_exp"], n)
                        v.tensor_scalar_min(zmin["k"], ksum[:, :, :].rearrange("t b d -> t (b d)"), 0.0)\
                         .then_inc(S["k3_min"], 1)
                    if before and c in (2, 4, 8, 10):
                        part = (2, 4, 8, 10).index(c)
                        invert(part, part + 1)
                    if before and c == 11:
                        normalise4(g - 1, u)
                    if before and c == 13:
                        add_y4(g - 1)
                    if n is None:
                        if c == 3:
                            ln_stats(0)
                        if c == 12:
                            ln_norm(0, LN4 + 1, None, None, "n4_ready")
                            ln_stats(1)
                    if c == 6 and n is not None:
                        dve.wait_ge(S["q3_hi"], n + 1)
                        v.scalar_tensor_tensor(QS[u][:, 1, :], phiQ[u][:, :], SCALE1, QS[u][:, 0, :], ALU.mult, ALU.subtract)\
                         .then_inc(S["q3_lo"], 1)
                    if c == 14 and n is not None:
                        ln_norm(n + 1, n + (LN3 + 2), "t3_ps", n + 1, "n3_ready")

            attention_schedule(dve, linear_group, step, 7)
            ln_norm(1, LN4 + 2, "t4_ps", 1, "n4_ready")
            denominators(GROUPS - 1, (GROUPS - 1) % 2)
            x_lo(0)
            invert(0, GB)
            normalise4(GROUPS - 1, (GROUPS - 1) % 2)

            def relu_lo(dst, hi, hi_done, done, n, chunks=range(FC)):
                for f in chunks:
                    dve.wait_ge(S[hi_done], n * FC + (f + 1))
                    v.scalar_tensor_tensor(dst[:, f, :], RING[f][:, :], 0.0, hi[:, f, :], ALU.max, ALU.subtract)\
                     .then_inc(S[done], 1)

            relu_lo(u0l, u0h, "u0_hi", "u0_lo", 0)
            add_y4(GROUPS - 1)

            def mlp_out(n):
                dve.wait_ge(S["l3_ps"], n + 1)
                x = group(X, n).rearrange("t b d -> t (b d)")
                v.scalar_tensor_tensor(x, M1[:, :], fac[:, 0:1], x, ALU.mult, ALU.add).then_inc(S["out_ready"], 1)

            def mlp_group(n, more):
                if more:
                    ln_stats(n + 2)
                relu_lo(u1l, u1h, "u1_hi", "u1_lo", n, range(FC - 1))
                x_lo(n + 1)
                relu_lo(u1l, u1h, "u1_hi", "u1_lo", n, [FC - 1])
                relu_lo(u0l, u0h, "u0_hi", "u0_lo", n + 1)
                if more:
                    ln_norm(n + 2, n + (LN4 + 3), "t4_ps", n + 2, "n4_ready")
                mlp_out(n)

            with dve.Fori(0, GROUPS - 2) as n:
                step.enter(n, 2)
                mlp_group(n, True)
            step.leave(GROUPS - 2)
            mlp_group(GROUPS - 2, False)
            relu_lo(u1l, u1h, "u1_hi", "u1_lo", GROUPS - 1)
            mlp_out(GROUPS - 1)

        @block.tensor
        def _(pe):
            mm = nc.tensor.matmul

            def transposes(dst, src, done):
                for b in range(GB):
                    last = nc.tensor.transpose(dst[:, b * T:(b + 1) * T], src[:, b, :], idf[:, :])
                last.then_inc(S[done], 1)

            def cols_of(b):
                return slice(b * T, (b + 1) * T)

            pe.wait_ge(S["pool_consts"], 1)

            def project_by_token(u, wv, done):
                for b in range(GB):
                    last = mm(M1[:, cols_of(b)], ctxg[u][:, cols_of(b)], wv[:, :], start=True, stop=True)
                last.then_inc(S[done], 1)

            def key_scores(u, c, dst, done):
                b, q = c // 4, c % 4
                for i in range(PLACES):
                    last = mm(dst[:, i * T:(i + 1) * T], Kpad[u][:, q, i, cols_of(b)], Qst[u][:, q, cols_of(b)],
                              start=True, stop=True)
                last.then_inc(S[done], 1)


            def turn(u_of_n, t, j_static):
                return j_static + 1 if t is None else t + u_of_n

            def transposed(n, free, frees, src_ready, done):
                pe.wait_ge(S[src_ready], n + 1)
                if not known(n, 1):
                    pe.wait_ge(S[free], frees)
                transposes(M0, xn, done)

            def next_normalised(n):
                pe.wait_ge(S["xn_ready"], n + 2)
                pe.wait_ge(S["k_lo"], n + 1)
                transposes(M0, xn, "xnT_ps")

            def gate_transposes(n):
                pe.wait_ge(S["n2_ready"], n + 1)
                if known(n, 1):
                    pe.wait_ge(S["m_T"], GROUPS)
                elif known(n, 2):
                    pe.wait_ge(S["hid_ready"], n)
                else:
                    pe.wait_ge(S["gt_ready"], n - 1)
                transposes(M0, xn, "t2_ps")

            def gate_hidden(n):
                pe.wait_ge(S["t2_ready"], n + 1)
                if known(n, 1):
                    pe.wait_ge(S["w_rest"], W_REST)
                elif known(n, 2):
                    pe.wait_ge(S["gt_ready"], n)
                mm(M0[0:HID, :], wg1[:, :], group(XN2T, n, W), start=True, stop=True).then_inc(S["hid_ps"], 1)

            def gate_logits(n):
                pe.wait_ge(S["hid_ready"], n + 1)
                if known(n, 1):
                    pe.wait_ge(S["moe_consts"], 2)
                else:
                    pe.wait_ge(S["lmax"], n)
                for b in range(GB):
                    last = mm((PA1 if known(n, 1) else PO1)[:, b * E:(b + 1) * E], hT[:, cols_of(b)], wg2[:, :], start=True, stop=True)
                last.then_inc(S["log_ps"], 1)

            BEHIND = 3
            LAG = 5

            def softmax_group(n, g, u, t):
                last_g = n is None
                ug = 1 - u
                base = GROUPS * 18 - 2 if last_g else (0 if known(n, 1) else n * 18 - 2)
                jn = 1 if t is None else t + 2
                jg = (1 if known(g, 1) else GROUPS // 2) if t is None else (t + 1 if u == 0 else t + 2)

                def maxima_scores(c):
                    b, q = c % 4, c // 4
                    if b == 0:
                        pe.wait_ge(STACKED[u][q], jn * PER_QUAD)
                    if not (known(n, 1) and c < 2):
                        pe.wait_ge(S["pa_free"], base + (c - 1))
                    mm(PA[c % 2][:, :], idb[:, :], maskA[:, :].unsqueeze(1).broadcast_to([T, PLACES, T]), start=True, stop=False)
                    mm(PA[c % 2][:, :], Qst[u][:, q, cols_of(b)], Kpad[u][:, q, :, cols_of(b)], start=False, stop=True)\
                        .then_inc(S["pa_ps"], 1)

                def weigh_values(c):
                    b, q = c // 4, c % 4
                    pe.wait_ge(S["e_masked"], g * 16 + (c + 1))
                    if c == 0:
                        if known(g, 1):
                            pe.wait_ge(S["prep_bo"], 1)
                        else:
                            pe.wait_ge(S["o_raw"], g)
                    for i in range(PLACES):
                        h = 4 * q + i
                        at = 32 * ((h // 3) % 4)
                        last = mm(PO[h // 12][at:at + 32, cols_of(b)], Vpad[ug][:, b, h, :], Eq[c % NE][:, i, :],
                                  start=h % 3 == 0, stop=h % 3 == 2 or h == H - 1, tile_position=(0, at))
                    last.then_inc(S["pv_done"], 1)

                def attend(c):
                    if c < 16:
                        if c == 0:
                            pe.wait_ge(S[f"m_in{ug}"], jg * 64)
                            pe.wait_ge(S["v_ready"], g + 1)
                        if not (known(g, 1) and c < 2):
                            pe.wait_ge(S["e_exp"], g * 16 + (c - 1))
                        key_scores(ug, c, PB[c % 2], "pb_ps")
                    if c >= BEHIND:
                        weigh_values(c - BEHIND)

                if n is not None:
                    pe.wait_ge(S["xnT_ready"], n + 1)
                    if known(n, 1):
                        pe.wait_ge(S["prep_q"], 1)
                    else:
                        pe.wait_ge(S["v_ready"], n)
                    mm(M1[:, :], Wq0[:, :], xnT[:, :], start=True, stop=True).then_inc(S["q_ps"], 1)
                    pe.wait_ge(S[f"ctx0_in{u}"], jn * 16)
                    if not known(n, 1):
                        pe.wait_ge(S["m_T"], n)
                    mm(M0[:, :], Wk0[:, :], ctxg[u][:, :], start=True, stop=True).then_inc(S["k_ps"], 1)

                def values():
                    pe.wait_ge(S["q_lo"], n + 1)
                    project_by_token(u, Wv0, "v_ps")

                if n is not None:
                    values()
                if known(n, 1):
                    pe.wait_ge(S["w_wo"], W_WO)
                    pe.wait_ge(S["bv_rep"], 1)
                    mm(PO1[:, 0:D], bvrep[:, :], Wo0[:, :], start=True, stop=True).then_inc(S["bo_ps"], 1)
                if g is None:
                    for c in range(16):
                        maxima_scores(c)
                    next_normalised(n)
                else:
                    for c in range(16 + max(LAG, BEHIND)):
                        if c < 16 + BEHIND:
                            attend(c)
                        if 0 <= c - LAG < 16 and n is not None:
                            maxima_scores(c - LAG)
                        if c == 11 and not known(g, 1):
                            project_out(g - 1, GROUPS if last_g else n + 1)
                        if last_g and c == 5:
                            gate_transposes(0)
                        if last_g and c == 10:
                            gate_hidden(0)
                        if last_g and c == 12:
                            pe.wait_ge(S["pa_free"], base)
                            gate_logits(0)
                        if c == 15 + LAG - 3 and n is not None:
                            next_normalised(n)
                    at = base if last_g else base + 16
                    pe.wait_ge(S["o_raw"], g + 1)
                    if known(g, 1):
                        pe.wait_ge(S["pool_consts"], 2)
                    pe.wait_ge(S["pa_free"], at - 1)
                    mm(PA0[:, :], sel0[:, :, :, :].rearrange("p a i d -> p (a i d)"), Oraw[:, 0, :], start=True, stop=True)\
                        .then_inc(S["pa_ps"], 1)
                    pe.wait_ge(S["pa_free"], at)
                    if last_g:
                        pe.wait_ge(S["lmax"], 1)
                    mm(PA1[0:64, :], sel1[:, :, :, :].rearrange("p a i d -> p (a i d)"), Oraw[:, 1, :], start=True, stop=True)\
                        .then_inc(S["pa_ps"], 1)
                if n is not None:
                    pe.wait_ge(S["m_split"], n + 1)
                    pe.wait_ge(S["xnT_ready"], n + 2)
                    for b in range(GB):
                        last = mm(M0[0:32, cols_of(b)], mparts[:, b, :, :, :].rearrange("t i r q -> t (i r q)"), idh[:, :],
                                  start=True, stop=True)
                    last.then_inc(S["m_ps"], 1)

            def project_out(g, v_ready):
                pe.wait_ge(S["o_norm"], g + 1)
                pe.wait_ge(S["v_ready"], v_ready)
                if known(g, 1):
                    pe.wait_ge(S["prep_wo"], 1)
                for b in range(GB):
                    mm(M1[:, cols_of(b)], On[:, 0, cols_of(b)], Wo0R[:, 0, :], start=True, stop=False)
                    last = mm(M1[:, cols_of(b)], On[:, 1, cols_of(b)], Wo0R[:, 1, :], start=False, stop=True)
                last.then_inc(S["y_ps"], 1)

            pe.wait_ge(S["xn_ready"], 1)
            transposes(M0, xn, "xnT_ps")
            pe.wait_ge(S["w_attn"], W_ATTN)
            attention_schedule(pe, softmax_group)
            gate_transposes(1)

            def transpose_gates(n):
                pe.wait_ge(S["gates_done"], n + 1)
                if known(n, 1):
                    pe.wait_ge(S["t2_ready"], n + 2)
                elif isinstance(n, int) and n == GROUPS - 1:
                    pe.wait_ge(S["gt_ready"], n)
                else:
                    pe.wait_ge(S["hid_ready"], n + 2)
                for b in range(GB):
                    last = mm(M0[:, cols_of(b)], G3[:, b, :], idb[:, :], start=True, stop=True)
                last.then_inc(S["gt_ps"], 1)

            def spread_gate(g, e):
                if e == 0:
                    pe.wait_ge(S["gt_ready"], g + 1)
                if not (known(g, 1) and e < 4):
                    pe.wait_ge(S["xs_ready"], g * E + (e - 3))
                mm(RING[e % 4][:, :], SELE[:, e, :], group(GT3, g, W), start=True, stop=True).then_inc(S["bc_ps"], 1)

            def mix_group(g, more, inputs):
                if known(g, 1):
                    pe.wait_ge(S["prep_rest"], 2)
                else:
                    transpose_mix(g - 1)
                for part in range(PARTS):
                    mm(PO0[:, :], BE[:, part, :], group(GT3, g, W), start=part == 0, stop=False)
                for e in range(E):
                    if known(g, 1) and e == 1:
                        pe.wait_ge(S["x1_ready"], GROUPS - 1)
                        project_out(GROUPS - 1, GROUPS)
                    if inputs and e == 6:
                        gate_transposes(g + 2)
                    if inputs and e == 9:
                        gate_hidden(g + 2)
                    if inputs and e == 13:
                        gate_logits(g + 2)
                    if more and e == 15:
                        transpose_gates(g + 1)
                    if not more and e == 14:
                        pe.wait_ge(S["n3_ready"], 1)
                        transposes(M0, xn, "t3_ps")
                    k, j = divmod(e, SPAN)
                    if j < SPLIT:
                        if known(g, 1) and j == 0:
                            pe.wait_ge(S["we_split"], k + 1)
                        own = slice(j * D, j * D + D)
                        pe.wait_ge(S["xs_high"], g * SPLITS + splits(e))
                        mm(PO0[:, :], We_hi[k][:, own], xs_hi[j], start=False, stop=False)
                        mm(PO0[:, :], We_lo[k][:, own], xs_hi[j], start=False, stop=False)
                        pe.wait_ge(S["xs_low"], g * SPLITS + splits(e))
                        mm(PO0[:, :], We_hi[k][:, own], xs_lo[j], start=False, stop=False).then_inc(S["xs_used"], 1)
                    else:
                        pe.wait_ge(S["xs_ready"], g * E + (e + 1))
                        mm(PO0[:, :], We[:, e, :], xs[e % 4], start=False, stop=e == E - 1).then_inc(S["xs_used"], 1)
                    if e + 4 < E:
                        spread_gate(g, e + 4)
                    elif more:
                        spread_gate(g + 1, e + 4 - E)

            def transpose_mix(g):
                pe.wait_ge(S["y3_T"], g + 1)
                if known(g, 1):
                    pe.wait_ge(S["x1_ready"], GROUPS)
                else:
                    pe.wait_ge(S["x2_ready"], g)
                for b in range(GB):
                    last = nc.tensor.transpose(M1[:, cols_of(b)], yT[:, cols_of(b)], idf[:, :])
                last.then_inc(S["y3_tps"], 1)

            transpose_gates(0)
            for e in range(2):
                spread_gate(0, e)
            gate_hidden(1)
            gate_logits(1)
            pe.wait_ge(S["pa_free"], GROUPS * 18)
            for e in range(2, 4):
                spread_gate(0, e)
            mix_group(0, True, True)
            with pe.Fori(1, GROUPS - 2) as g:
                mix_group(g, True, True)
            mix_group(GROUPS - 2, True, False)
            mix_group(GROUPS - 1, False, False)
            transpose_mix(GROUPS - 1)
            def linear_group(n, g, u, t):
                ug = 1 - u
                jn = 1 if t is None else t + 2
                jg = (1 if known(g, 1) else GROUPS // 2) if t is None else (t + 1 if u == 0 else t + 2)
                if n is not None:
                    pe.wait_ge(S["t3_ready"], n + 1)
                    if known(n, 1):
                        pe.wait_ge(S["x2_ready"], GROUPS)
                    else:
                        pe.wait_ge(S["k3_sum"], n)
                    mm(M1[:, :], Wq1[:, :], xnT[:, :], start=True, stop=True).then_inc(S["q3_ps"], 1)
                    pe.wait_ge(S[f"ctx1_in{u}"], jn * 16)
                    mm(M0[:, :], Wv1[:, :], ctxg[u][:, :], start=True, stop=True).then_inc(S["v3_ps"], 1)
                    pe.wait_ge(S["q3_max"], n + 1)
                    project_by_token(u, Wk1, "k3_ps")

                def key_sums():
                    pe.wait_ge(S["k3_phi"], n + 1)
                    if not known(n, 2):
                        pe.wait_ge(S["p4_den"], n - 1)
                    for b in range(GB):
                        last = mm(PA[u][:, cols_of(b)], phiK[:, b, :], triT[:, :], start=True, stop=True)
                    last.then_inc(S["z3_ps"], 1)

                def next_transposed():
                    pe.wait_ge(S["n3_ready"], n + 2)
                    pe.wait_ge(S["v3_lo"], n + 1)
                    transposes(M0, xn, "t3_ps")

                if g is None:
                    key_sums()
                    next_transposed()
                    return
                for c in range(16 + BEHIND):
                    if c < 16:
                        if c == 0:
                            for q in range(QUADS):
                                pe.wait_ge(STACKED[ug][q], (GROUPS // 2 + jg) * PER_QUAD)
                            pe.wait_ge(S["k3_ready"], g + 1)
                        if not (known(g, 1) and c < 2):
                            pe.wait_ge(S["p4_cp" if c % 2 else "p4_aD"], g * 8 + c // 2)
                        key_scores(ug, c, PB[c % 2], "p4b_odd" if c % 2 else "p4b_even")
                    if c >= BEHIND:
                        m = c - BEHIND
                        b, q = m // 4, m % 4
                        pe.wait_ge(S["p4_aP" if m % 2 else "p4_aD"], g * 8 + (m // 2 + 1))
                        if m == 0:
                            if known(g, 2):
                                pe.wait_ge(S["y3_T"], GROUPS)
                            else:
                                pe.wait_ge(S["p4_o"], g - 1)
                        for i in range(PLACES):
                            last = mm(PO[ug][32 * q:32 * q + 32, cols_of(b)], Vpad[ug][:, b, 4 * q + i, :], Eq[m % NE][:, i, :],
                                      start=i == 0, stop=i == PLACES - 1, tile_position=(0, 32 * q))
                        last.then_inc(S["p4_pv"], 1)
                    if c == 13 and not known(g, 1):
                        linear_out(g - 1, GROUPS if n is None else n + 1)
                    if c == 12 and n is not None:
                        key_sums()
                    if c == 18 and n is not None:
                        next_transposed()
                    if c == 15 and n is None:
                        pe.wait_ge(S["n4_ready"], 1)
                        pe.wait_ge(S["v3_lo"], GROUPS)
                        transposes(M0, xn, "t4_ps")

            def linear_out(g, keys_read):
                pe.wait_ge(S["p4_o"], g + 1)
                pe.wait_ge(S["k3_sum"], keys_read)
                if known(g, 1):
                    pe.wait_ge(S["prep_rest"], 1)
                for b in range(GB):
                    last = mm(M1[:, cols_of(b)], On[:, 0, cols_of(b)], Wo1[:, :], start=True, stop=True)
                last.then_inc(S["p4_y"], 1)

            attention_schedule(pe, linear_group)
            def mlp_first(n):
                pe.wait_ge(S["x4_lo"], n + 1)
                for f in range(FC):
                    if not known(n, 1):
                        pe.wait_ge(S["u1_lo"], n * FC + (f + 1 - FC))
                    cols_f = slice(f * 128, (f + 1) * 128)
                    mm(RING[f][:, :], w0[:, cols_f], xh[:, :], start=True, stop=False)
                    mm(RING[f][:, :], w0[:, cols_f], xl[:, :], start=False, stop=True).then_inc(S["l1_ps"], 1)

            def mlp_second(n, chunks=range(FC)):
                pe.wait_ge(S["u0_lo"], n * FC + FC)
                for f in chunks:
                    for k in range(FC):
                        w = w1[:, k, f * 128:(f + 1) * 128]
                        mm(RING[f][:, :], w, u0h[:, k, :], start=k == 0, stop=False)
                        last = mm(RING[f][:, :], w, u0l[:, k, :], start=False, stop=k == FC - 1)
                    last.then_inc(S["l2_ps"], 1)

            def mlp_third(n):
                pe.wait_ge(S["u1_lo"], n * FC + FC)
                if known(n, 1):
                    pe.wait_ge(S["x3_ready"], GROUPS)
                else:
                    pe.wait_ge(S["out_ready"], n)
                for b in range(GB):
                    for k in range(FC):
                        mm(M1[:, cols_of(b)], u1h[:, k, cols_of(b)], w2[:, k, :], start=k == 0, stop=False)
                        last = mm(M1[:, cols_of(b)], u1l[:, k, cols_of(b)], w2[:, k, :], start=False, stop=k == FC - 1)
                last.then_inc(S["l3_ps"], 1)

            pe.wait_ge(S["p4_den"], GROUPS)
            mlp_first(0)
            pe.wait_ge(S["x3_ready"], GROUPS - 1)
            linear_out(GROUPS - 1, GROUPS)

            def mlp_group(n):
                mlp_second(n, range(FC - 1))
                transposed(n + 1, "x4_lo", n + 1, "n4_ready", "t4_ps")
                mlp_second(n, [FC - 1])
                mlp_first(n + 1)
                mlp_third(n)

            mlp_group(0)
            with pe.Fori(1, GROUPS - 1) as n:
                mlp_group(n)
            mlp_second(GROUPS - 1)
            mlp_third(GROUPS - 1)


ARRAYS = {"x": "x", "g_xattn": "g_xattn", "g_ffn": "g_ffn",
          "bq0": "L0_xattn_bq", "bk0": "L0_xattn_bk", "bv0": "L0_xattn_bv", "bo0": "L0_xattn_bo",
          "wg1": "L0_ffn_wg1", "bg1": "L0_ffn_bg1", "wg2": "L0_ffn_wg2", "bg2": "L0_ffn_bg2", "We": "L0_ffn_We", "be": "L0_ffn_be",
          "Wq1": "L1_xattn_Wq", "Wk1": "L1_xattn_Wk", "Wv1": "L1_xattn_Wv", "Wo1": "L1_xattn_Wo",
          "bq1": "L1_xattn_bq", "bk1": "L1_xattn_bk", "bv1": "L1_xattn_bv", "bo1": "L1_xattn_bo"}


def kernel(**inputs):
    from concourse import bacc
    from concourse.bass_utils import run_bass_kernel_spmd
    i = {name: np.asarray(value) for name, value in inputs.items()}
    arrays = {short: i[name] for short, name in ARRAYS.items()}
    ctx_t = np.zeros((D, (GROUPS + EXTRA) * W), np.float32)
    ctx_t[:, :GROUPS * W] = i["ctx_1024"].transpose(2, 0, 1).reshape(D, GROUPS * W)
    arrays["ctxT"] = ctx_t
    for w in "qkvo":
        arrays[f"W{w}T0"] = i[f"L0_xattn_W{w}"].T
    for k in range(3):
        arrays[f"k{k}"] = i[f"L1_ffn_k{k}"]
        arrays[f"s{k}"] = i[f"L1_ffn_s{k}"].reshape(1)
    arrays = {name: np.ascontiguousarray(value) for name, value in arrays.items()}

    nc = bacc.Bacc("TRN2", target_bir_lowering=False, num_devices=1)
    aps = {name: nc.dram_tensor(f"in_{name}", list(value.shape), mybir.dt.from_np(value.dtype), kind="ExternalInput").ap()
           for name, value in arrays.items()}
    out = nc.dram_tensor("out_x", [SEQS, T, D], F32, kind="ExternalOutput").ap()
    build(nc, aps, out)
    result = run_bass_kernel_spmd(nc, [{f"in_{name}": value for name, value in arrays.items()}], core_ids=[0])
    return result.results[0]["out_x"]
```
